# Optimizing a Trainium2 kernel written in Bass

```python
import numpy as np
import jax
import jax.numpy as jnp

def _softmax(x, axis=-1):
    return jax.nn.softmax(x, axis=axis)

def _gelu(x):
    return jax.nn.gelu(x, approximate=True)

def _silu(x):
    return jax.nn.silu(x)

def _sigmoid(x):
    return jax.nn.sigmoid(x)

def _layernorm(x, axis=-1, eps=1e-05):
    m = jnp.mean(x, axis=axis, keepdims=True)
    v = jnp.var(x, axis=axis, keepdims=True)
    return (x - m) / jnp.sqrt(v + eps)

def _scatter_add(tgt, idx, src, axis=0):
    return tgt.at[idx].add(src)

def _segment_sum(src, seg, n):
    return jax.ops.segment_sum(src, seg, n)
kernel_name = 'mk_xattn_seq_d2_seqx_r8_bc8aa5'

def setup_inputs(seed: int=0):
    np.random.seed(seed)
    _w = jnp.asarray

    def _rec_inputs():
        import jax
        import jax.numpy as jnp
        _rk = jax.random.key(seed)
        x = -0.0002928 + 1 * jax.random.normal(jax.random.fold_in(_rk, 1), (8, 256, 128), jnp.float32)
        _lenS = 256 - jax.random.randint(jax.random.fold_in(_rk, 7), (8,), 0, max(1, 256 // 4) + 1, jnp.int32)
        _lenS2 = 256 - jax.random.randint(jax.random.fold_in(_rk, 8), (8,), 0, max(1, 256 // 4) + 1, jnp.int32)
        _ctx_1024P = jax.random.normal(jax.random.fold_in(_rk, 11), (8, 16, 128), jnp.float32)
        _ctx_1024c = jax.random.dirichlet(jax.random.fold_in(_rk, 511), 0.3 * jnp.ones((16,), jnp.float32), (8, 256))
        _ctx_1024t = jnp.einsum('bsk,bkd->bsd', _ctx_1024c, _ctx_1024P)
        _ctx_1024t = _ctx_1024t * jax.lax.rsqrt(jnp.mean(jnp.square(_ctx_1024t)) + 1e-12) * 0.953939
        ctx_1024 = -1.39393e-06 + 0.999914 * (_ctx_1024t + 0.3 * jax.random.normal(jax.random.fold_in(_rk, 611), (8, 256, 128), jnp.float32))
        _validS = jnp.arange(256)[None, :] < _lenS[:, None]
        _validS2 = jnp.arange(256)[None, :] < _lenS2[:, None]
        _causal = jnp.tril(jnp.ones((256, 256), dtype=bool))
        mask_Bx1x1xS2_if1 = jnp.where(jnp.ones((8, 1, 1, 256), dtype=bool), 1, 0).astype(jnp.int32)
        mask_Bx1xSxS2_if1 = jnp.where(jnp.ones((8, 1, 256, 256), dtype=bool), 1, 0).astype(jnp.int32)
        return (x, ctx_1024, mask_Bx1x1xS2_if1, mask_Bx1xSxS2_if1)
    x, ctx_1024, mask_Bx1x1xS2_if1, mask_Bx1xSxS2_if1 = _rec_inputs()

    def _L0_xattn_setup():
        import jax, jax.numpy as jnp
        import numpy as np
        D_MODEL = 128
        N_HEADS = 16
        D_K = D_MODEL // N_HEADS
        D_FF = 512
        B, S = (2, 256)
        LN_EPS = 1e-05
        NEG_INF = -1e+30

        def layer_norm(x, g, b):
            mu = jnp.mean(x, axis=-1, keepdims=True)
            var = jnp.mean(jnp.square(x - mu), axis=-1, keepdims=True)
            return (x - mu) * jax.lax.rsqrt(var + LN_EPS) * g + b
        key = jax.random.key(seed)
        ks = jax.random.split(key, 16)
        sd = 0.02
        inp = {'query': jax.random.normal(ks[0], (B, S, D_MODEL), jnp.float32), 'key': jax.random.normal(ks[1], (B, S, D_MODEL), jnp.float32), 'values': jax.random.normal(ks[2], (B, S, D_MODEL), jnp.float32), 'Wq': jax.random.normal(ks[3], (D_MODEL, D_MODEL), jnp.float32) * sd, 'bq': jnp.zeros((D_MODEL,), jnp.float32), 'Wk': jax.random.normal(ks[4], (D_MODEL, D_MODEL), jnp.float32) * sd, 'bk': jnp.zeros((D_MODEL,), jnp.float32), 'Wv': jax.random.normal(ks[5], (D_MODEL, D_MODEL), jnp.float32) * sd, 'bv': jnp.zeros((D_MODEL,), jnp.float32), 'Wo': jax.random.normal(ks[6], (D_MODEL, D_MODEL), jnp.float32) * sd, 'bo': jnp.zeros((D_MODEL,), jnp.float32), 'ln1_g': jnp.ones((D_MODEL,), jnp.float32), 'ln1_b': jnp.zeros((D_MODEL,), jnp.float32), 'W1': jax.random.normal(ks[7], (D_MODEL, D_FF), jnp.float32) * sd, 'b1': jnp.zeros((D_FF,), jnp.float32), 'W2': jax.random.normal(ks[8], (D_FF, D_MODEL), jnp.float32) * sd, 'b2': jnp.zeros((D_MODEL,), jnp.float32), 'ln2_g': jnp.ones((D_MODEL,), jnp.float32), 'ln2_b': jnp.zeros((D_MODEL,), jnp.float32), 'mask': 0}
        return inp
    _L0_xattn_all = _L0_xattn_setup()
    _L0_xattn_in = {k: v for k, v in _L0_xattn_all.items() if k in ('Wq', 'bq', 'Wk', 'bk', 'Wv', 'bv', 'Wo', 'bo', 'ln1_g', 'ln1_b', 'W1', 'b1', 'W2', 'b2', 'ln2_g', 'ln2_b')}
    del _L0_xattn_all

    def _L1_xattn_setup():
        import jax, jax.numpy as jnp
        import numpy as np
        D_MODEL = 128
        NUM_HEADS = 16
        D_FF = 512
        D_K = D_MODEL // NUM_HEADS
        LN_EPS = 1e-05

        def _linear(x, w, b):
            return jnp.einsum('bsd,od->bso', x, w) + b

        def _layernorm(x, g, b):
            mu = jnp.mean(x, axis=-1, keepdims=True)
            var = jnp.mean(jnp.square(x - mu), axis=-1, keepdims=True)
            return (x - mu) * jax.lax.rsqrt(var + LN_EPS) * g + b

        def _mha(q_in, kv_in, mask, wq, bq, wk, bk, wv, bv, wo, bo):
            B, Sq, _ = q_in.shape
            Sk = kv_in.shape[1]
            q = _linear(q_in, wq, bq).reshape(B, Sq, NUM_HEADS, D_K).transpose(0, 2, 1, 3)
            k = _linear(kv_in, wk, bk).reshape(B, Sk, NUM_HEADS, D_K).transpose(0, 2, 1, 3)
            v = _linear(kv_in, wv, bv).reshape(B, Sk, NUM_HEADS, D_K).transpose(0, 2, 1, 3)
            scores = jnp.einsum('bhqd,bhkd->bhqk', q, k) / jnp.sqrt(jnp.asarray(D_K, q.dtype))
            scores = jnp.where(mask == 0, jnp.asarray(-1000000000.0, scores.dtype), scores)
            attn = jax.nn.softmax(scores, axis=-1)
            out = jnp.einsum('bhqk,bhkd->bhqd', attn, v)
            out = out.transpose(0, 2, 1, 3).reshape(B, Sq, D_MODEL)
            return _linear(out, wo, bo)
        key = jax.random.key(seed)
        ks = jax.random.split(key, 24)
        B, S = (4, 256)
        s = 0.02
        d = {'tgt': jax.random.normal(ks[0], (B, S, D_MODEL), jnp.float32), 'enc_output': jax.random.normal(ks[1], (B, S, D_MODEL), jnp.float32), 'src_mask': jnp.ones((B, 1, 1, S), jnp.int32), 'tgt_mask': jnp.ones((B, 1, S, S), jnp.int32)}
        names = ['sa_wq', 'sa_wk', 'sa_wv', 'sa_wo', 'ca_wq', 'ca_wk', 'ca_wv', 'ca_wo']
        for i, n in enumerate(names):
            d[n] = jax.random.normal(ks[2 + i], (D_MODEL, D_MODEL), jnp.float32) * s
            d[n.replace('w', 'b')] = jnp.zeros((D_MODEL,), jnp.float32)
        d['ffn_w1'] = jax.random.normal(ks[10], (D_FF, D_MODEL), jnp.float32) * s
        d['ffn_b1'] = jnp.zeros((D_FF,), jnp.float32)
        d['ffn_w2'] = jax.random.normal(ks[11], (D_MODEL, D_FF), jnp.float32) * s
        d['ffn_b2'] = jnp.zeros((D_MODEL,), jnp.float32)
        for i in (1, 2, 3):
            d[f'ln{i}_g'] = jnp.ones((D_MODEL,), jnp.float32)
            d[f'ln{i}_b'] = jnp.zeros((D_MODEL,), jnp.float32)
        return d
    _L1_xattn_all = _L1_xattn_setup()
    _L1_xattn_in = {k: v for k, v in _L1_xattn_all.items() if k in ('sa_wq', 'sa_bq', 'sa_wk', 'sa_bk', 'sa_wv', 'sa_bv', 'sa_wo', 'sa_bo', 'ca_wq', 'ca_bq', 'ca_wk', 'ca_bk', 'ca_wv', 'ca_bv', 'ca_wo', 'ca_bo', 'ffn_w1', 'ffn_b1', 'ffn_w2', 'ffn_b2', 'ln1_g', 'ln1_b', 'ln2_g', 'ln2_b', 'ln3_g', 'ln3_b')}
    del _L1_xattn_all
    return {'x': x, 'ctx_1024': ctx_1024, 'mask_Bx1x1xS2_if1': mask_Bx1x1xS2_if1, 'mask_Bx1xSxS2_if1': mask_Bx1xSxS2_if1, 'L0_xattn_Wq': _L0_xattn_in['Wq'], 'L0_xattn_bq': _L0_xattn_in['bq'], 'L0_xattn_Wk': _L0_xattn_in['Wk'], 'L0_xattn_bk': _L0_xattn_in['bk'], 'L0_xattn_Wv': _L0_xattn_in['Wv'], 'L0_xattn_bv': _L0_xattn_in['bv'], 'L0_xattn_Wo': _L0_xattn_in['Wo'], 'L0_xattn_bo': _L0_xattn_in['bo'], 'L0_xattn_ln1_g': _L0_xattn_in['ln1_g'], 'L0_xattn_ln1_b': _L0_xattn_in['ln1_b'], 'L0_xattn_W1': _L0_xattn_in['W1'], 'L0_xattn_b1': _L0_xattn_in['b1'], 'L0_xattn_W2': _L0_xattn_in['W2'], 'L0_xattn_b2': _L0_xattn_in['b2'], 'L0_xattn_ln2_g': _L0_xattn_in['ln2_g'], 'L0_xattn_ln2_b': _L0_xattn_in['ln2_b'], 'L1_xattn_sa_wq': _L1_xattn_in['sa_wq'], 'L1_xattn_sa_bq': _L1_xattn_in['sa_bq'], 'L1_xattn_sa_wk': _L1_xattn_in['sa_wk'], 'L1_xattn_sa_bk': _L1_xattn_in['sa_bk'], 'L1_xattn_sa_wv': _L1_xattn_in['sa_wv'], 'L1_xattn_sa_bv': _L1_xattn_in['sa_bv'], 'L1_xattn_sa_wo': _L1_xattn_in['sa_wo'], 'L1_xattn_sa_bo': _L1_xattn_in['sa_bo'], 'L1_xattn_ca_wq': _L1_xattn_in['ca_wq'], 'L1_xattn_ca_bq': _L1_xattn_in['ca_bq'], 'L1_xattn_ca_wk': _L1_xattn_in['ca_wk'], 'L1_xattn_ca_bk': _L1_xattn_in['ca_bk'], 'L1_xattn_ca_wv': _L1_xattn_in['ca_wv'], 'L1_xattn_ca_bv': _L1_xattn_in['ca_bv'], 'L1_xattn_ca_wo': _L1_xattn_in['ca_wo'], 'L1_xattn_ca_bo': _L1_xattn_in['ca_bo'], 'L1_xattn_ffn_w1': _L1_xattn_in['ffn_w1'], 'L1_xattn_ffn_b1': _L1_xattn_in['ffn_b1'], 'L1_xattn_ffn_w2': _L1_xattn_in['ffn_w2'], 'L1_xattn_ffn_b2': _L1_xattn_in['ffn_b2'], 'L1_xattn_ln1_g': _L1_xattn_in['ln1_g'], 'L1_xattn_ln1_b': _L1_xattn_in['ln1_b'], 'L1_xattn_ln2_g': _L1_xattn_in['ln2_g'], 'L1_xattn_ln2_b': _L1_xattn_in['ln2_b'], 'L1_xattn_ln3_g': _L1_xattn_in['ln3_g'], 'L1_xattn_ln3_b': _L1_xattn_in['ln3_b']}

def reference(x, ctx_1024, mask_Bx1x1xS2_if1, mask_Bx1xSxS2_if1, L0_xattn_Wq, L0_xattn_bq, L0_xattn_Wk, L0_xattn_bk, L0_xattn_Wv, L0_xattn_bv, L0_xattn_Wo, L0_xattn_bo, L0_xattn_ln1_g, L0_xattn_ln1_b, L0_xattn_W1, L0_xattn_b1, L0_xattn_W2, L0_xattn_b2, L0_xattn_ln2_g, L0_xattn_ln2_b, L1_xattn_sa_wq, L1_xattn_sa_bq, L1_xattn_sa_wk, L1_xattn_sa_bk, L1_xattn_sa_wv, L1_xattn_sa_bv, L1_xattn_sa_wo, L1_xattn_sa_bo, L1_xattn_ca_wq, L1_xattn_ca_bq, L1_xattn_ca_wk, L1_xattn_ca_bk, L1_xattn_ca_wv, L1_xattn_ca_bv, L1_xattn_ca_wo, L1_xattn_ca_bo, L1_xattn_ffn_w1, L1_xattn_ffn_b1, L1_xattn_ffn_w2, L1_xattn_ffn_b2, L1_xattn_ln1_g, L1_xattn_ln1_b, L1_xattn_ln2_g, L1_xattn_ln2_b, L1_xattn_ln3_g, L1_xattn_ln3_b):
    import jax
    import jax.numpy as jnp

    def _L0_xattn_ref(query, key, values, Wq, bq, Wk, bk, Wv, bv, Wo, bo, ln1_g, ln1_b, W1, b1, W2, b2, ln2_g, ln2_b, mask):
        import jax, jax.numpy as jnp
        import numpy as np
        D_MODEL = 128
        N_HEADS = 16
        D_K = D_MODEL // N_HEADS
        D_FF = 512
        B, S = (2, 256)
        LN_EPS = 1e-05
        NEG_INF = -1e+30

        def layer_norm(x, g, b):
            mu = jnp.mean(x, axis=-1, keepdims=True)
            var = jnp.mean(jnp.square(x - mu), axis=-1, keepdims=True)
            return (x - mu) * jax.lax.rsqrt(var + LN_EPS) * g + b
        b, s, d = query.shape
        q = (query @ Wq + bq).reshape(b, s, N_HEADS, D_K).transpose(0, 2, 1, 3)
        k = (key @ Wk + bk).reshape(b, s, N_HEADS, D_K).transpose(0, 2, 1, 3)
        v = (values @ Wv + bv).reshape(b, s, N_HEADS, D_K).transpose(0, 2, 1, 3)
        scores = jnp.einsum('bhqd,bhkd->bhqk', q, k) / jnp.sqrt(jnp.float32(D_K))
        i = jnp.arange(s)[:, None]
        j = jnp.arange(s)[None, :]
        allowed = j < i + mask
        scores = jnp.where(allowed, scores, NEG_INF)
        attn = jax.nn.softmax(scores, axis=-1)
        if mask == 0:
            attn = attn.at[:, :, 0, :].set(0.0)
        ctx = jnp.einsum('bhqk,bhkd->bhqd', attn, v)
        ctx = ctx.transpose(0, 2, 1, 3).reshape(b, s, d)
        attn_out = ctx @ Wo + bo
        x = layer_norm(query + attn_out, ln1_g, ln1_b)
        ffn = jax.nn.relu(x @ W1 + b1) @ W2 + b2
        out = layer_norm(x + ffn, ln2_g, ln2_b)
        return out

    def _L1_xattn_ref(tgt, enc_output, src_mask, tgt_mask, sa_wq, sa_bq, sa_wk, sa_bk, sa_wv, sa_bv, sa_wo, sa_bo, ca_wq, ca_bq, ca_wk, ca_bk, ca_wv, ca_bv, ca_wo, ca_bo, ffn_w1, ffn_b1, ffn_w2, ffn_b2, ln1_g, ln1_b, ln2_g, ln2_b, ln3_g, ln3_b):
        import jax, jax.numpy as jnp
        import numpy as np
        D_MODEL = 128
        NUM_HEADS = 16
        D_FF = 512
        D_K = D_MODEL // NUM_HEADS
        LN_EPS = 1e-05

        def _linear(x, w, b):
            return jnp.einsum('bsd,od->bso', x, w) + b

        def _layernorm(x, g, b):
            mu = jnp.mean(x, axis=-1, keepdims=True)
            var = jnp.mean(jnp.square(x - mu), axis=-1, keepdims=True)
            return (x - mu) * jax.lax.rsqrt(var + LN_EPS) * g + b

        def _mha(q_in, kv_in, mask, wq, bq, wk, bk, wv, bv, wo, bo):
            B, Sq, _ = q_in.shape
            Sk = kv_in.shape[1]
            q = _linear(q_in, wq, bq).reshape(B, Sq, NUM_HEADS, D_K).transpose(0, 2, 1, 3)
            k = _linear(kv_in, wk, bk).reshape(B, Sk, NUM_HEADS, D_K).transpose(0, 2, 1, 3)
            v = _linear(kv_in, wv, bv).reshape(B, Sk, NUM_HEADS, D_K).transpose(0, 2, 1, 3)
            scores = jnp.einsum('bhqd,bhkd->bhqk', q, k) / jnp.sqrt(jnp.asarray(D_K, q.dtype))
            scores = jnp.where(mask == 0, jnp.asarray(-1000000000.0, scores.dtype), scores)
            attn = jax.nn.softmax(scores, axis=-1)
            out = jnp.einsum('bhqk,bhkd->bhqd', attn, v)
            out = out.transpose(0, 2, 1, 3).reshape(B, Sq, D_MODEL)
            return _linear(out, wo, bo)
        t2 = _mha(tgt, tgt, tgt_mask, sa_wq, sa_bq, sa_wk, sa_bk, sa_wv, sa_bv, sa_wo, sa_bo)
        x = _layernorm(tgt + t2, ln1_g, ln1_b)
        t2 = _mha(x, enc_output, src_mask, ca_wq, ca_bq, ca_wk, ca_bk, ca_wv, ca_bv, ca_wo, ca_bo)
        x = _layernorm(x + t2, ln2_g, ln2_b)
        t2 = _linear(jax.nn.relu(_linear(x, ffn_w1, ffn_b1)), ffn_w2, ffn_b2)
        return _layernorm(x + t2, ln3_g, ln3_b)
    x = _L0_xattn_ref(x, ctx_1024, ctx_1024, L0_xattn_Wq, L0_xattn_bq, L0_xattn_Wk, L0_xattn_bk, L0_xattn_Wv, L0_xattn_bv, L0_xattn_Wo, L0_xattn_bo, L0_xattn_ln1_g, L0_xattn_ln1_b, L0_xattn_W1, L0_xattn_b1, L0_xattn_W2, L0_xattn_b2, L0_xattn_ln2_g, L0_xattn_ln2_b, 0)
    x = _L1_xattn_ref(x, ctx_1024, mask_Bx1x1xS2_if1, mask_Bx1xSxS2_if1, L1_xattn_sa_wq, L1_xattn_sa_bq, L1_xattn_sa_wk, L1_xattn_sa_bk, L1_xattn_sa_wv, L1_xattn_sa_bv, L1_xattn_sa_wo, L1_xattn_sa_bo, L1_xattn_ca_wq, L1_xattn_ca_bq, L1_xattn_ca_wk, L1_xattn_ca_bk, L1_xattn_ca_wv, L1_xattn_ca_bv, L1_xattn_ca_wo, L1_xattn_ca_bo, L1_xattn_ffn_w1, L1_xattn_ffn_b1, L1_xattn_ffn_w2, L1_xattn_ffn_b2, L1_xattn_ln1_g, L1_xattn_ln1_b, L1_xattn_ln2_g, L1_xattn_ln2_b, L1_xattn_ln3_g, L1_xattn_ln3_b)
    return x

_drawn_inputs = setup_inputs


def setup_inputs(seed=0):
    import zlib

    import numpy as np

    out = dict(_drawn_inputs(seed))
    spreads = {'L0_xattn_bq': (0.0, 2.0),
     'L0_xattn_bk': (0.0, 2.0),
     'L0_xattn_bv': (0.0, 0.354),
     'L0_xattn_bo': (0.0, 0.1),
     'L0_xattn_ln1_g': (1.0, 0.2),
     'L0_xattn_ln1_b': (0.0, 0.1),
     'L0_xattn_b1': (0.0, 0.302),
     'L0_xattn_b2': (0.0, 0.1),
     'L0_xattn_ln2_g': (1.0, 0.2),
     'L0_xattn_ln2_b': (0.0, 0.1),
     'L1_xattn_sa_bq': (0.0, 0.8),
     'L1_xattn_sa_bk': (0.0, 2.0),
     'L1_xattn_sa_bv': (0.0, 0.348),
     'L1_xattn_sa_bo': (0.0, 0.1),
     'L1_xattn_ca_bq': (0.0, 2.0),
     'L1_xattn_ca_bk': (0.0, 2.0),
     'L1_xattn_ca_bv': (0.0, 0.382),
     'L1_xattn_ca_bo': (0.0, 0.1),
     'L1_xattn_ffn_b1': (0.0, 0.1),
     'L1_xattn_ffn_b2': (0.0, 0.1),
     'L1_xattn_ln1_g': (1.0, 0.2),
     'L1_xattn_ln1_b': (0.0, 0.1),
     'L1_xattn_ln2_g': (1.0, 0.2),
     'L1_xattn_ln2_b': (0.0, 0.1),
     'L1_xattn_ln3_g': (1.0, 0.2),
     'L1_xattn_ln3_b': (0.0, 0.1)}
    factors = {'L0_xattn_Wq': 8.0,
     'L0_xattn_Wk': 8.0,
     'L1_xattn_sa_wq': 8.0,
     'L1_xattn_sa_wk': 8.0,
     'L1_xattn_sa_wv': 6.022,
     'L1_xattn_ca_wq': 8.0,
     'L1_xattn_ca_wk': 8.0}
    for name, (base, spread) in spreads.items():
        noise = np.random.default_rng([zlib.crc32(name.encode()), seed]).standard_normal(out[name].shape)
        drawn = base * np.exp(spread * noise) if base else spread * noise
        out[name] = jnp.asarray(drawn.astype(out[name].dtype))
    for name, factor in factors.items():
        out[name] = (out[name] * factor).astype(out[name].dtype)
    return out
```

```python
import numpy as np
import concourse.bass as bass
from concourse import mybir
from contextlib import ExitStack

f32 = mybir.dt.float32
bf16 = mybir.dt.bfloat16
i32 = mybir.dt.int32
ALU = mybir.AluOpType
ACT = mybir.ActivationFunctionType
AX = mybir.AxisListType

BATCHES, TOKENS, D = 8, 256, 128
HEADS, DK, FF = 16, 8, 512
P = 128
TILES = TOKENS // P
CHUNKS = FF // P
PAIRS = HEADS // 2
LAYERS = 3
CAUSAL, SELF, CROSS = range(LAYERS)
EPS = 1e-5
BIG = float(2 ** 100)
SCALE = float(1 / np.sqrt(np.float32(DK)))

PRODUCTS = [(0, 0), (0, 1), (1, 0), (1, 1), (0, 2), (2, 0)]
TERMS = len(PRODUCTS)
MAX_ROW = 1 + TERMS * DK
ROWS_S = MAX_ROW
ROWS_T = MAX_ROW + 3
VW = DK + 1
VCOLS = HEADS * VW + 16

LOOP_FROM, LOOP_TO = 3, 7
STEPS = 16
UNITS = [12, 16, 16]

BQ, BK, BO = 0, 3, 6
B2, B1 = 9, 11
NCOL = B1 + 2 * CHUNKS
BV, LNG, LNB = 0, 3, 8
NROW = 13
LN_OUT = {CAUSAL: 0, SELF: 2, CROSS: 3}
LN_TAIL = {CAUSAL: 1, CROSS: 4}
FFN = {CAUSAL: 0, CROSS: 1}


class Batch:

    def __init__(self, reg, off):
        self.reg, self.off = reg, off

    def __add__(self, n):
        return Batch(self.reg, self.off + n)

    def __sub__(self, n):
        return Batch(self.reg, self.off - n)


def exists(b):
    return isinstance(b, Batch) or 0 <= b < BATCHES


def value(b, per=1, plus=0):
    if isinstance(b, Batch):
        return b.reg * per + (b.off * per + plus)
    return b * per + plus


class Signals:

    def __init__(self, sem, names, by=1):
        self.sem, self.names, self.by = sem, list(names), by

    def upto(self, b, name):
        n = len(self.names)
        return self.sem, value(b, n * self.by, (self.names.index(name) + 1) * self.by)


def slot_tasks(i, s):
    return ((s, i - s),
            (s + 1, i - s - 1) if s < 2 else (0, i + 1),
            (s - 1, i - s + 1) if s else (2, i - 3),
            (s - 2, i - s + 2) if s == 2 else (s + 1, i - s - 2))


def units(l, g, step):
    n = UNITS[l] // 2
    at = step - 8 * g
    return [u + g * n for u in range(n) if at == u * 8 // n] if 0 <= at < 8 else []


def unit_of(l, u):
    n = UNITS[l] // 2
    g, v = divmod(u, n)
    if l != CAUSAL:
        return v % 2, 8 * g + 2 * (v // 2), 2
    short = v % 3 == 0
    return (0, 8 * g + 4 * (v // 3), 4) if short else (1, 8 * g + 4 * (v // 3) + 2 * (v % 3 - 1), 2)


def attention_program(nc, x, ctx, key_mask, self_mask, w4, w1, w2, bias_col, bias_row, out, mask_rows):
    es = ExitStack()
    with es:
        def sb(name, shape, dt=f32):
            return es.enter_context(nc.sbuf_tensor(name, shape, dt))

        def sem(name):
            return es.enter_context(nc.semaphore(name))

        def signals(name, names, by=1):
            return Signals(sem(name), names, by)

        def per_layer(name, names, by=1):
            return [signals(f"{name}{l}", names(l) if callable(names) else names, by) for l in range(LAYERS)]

        w4_sb = sb("w4_sb", [P, 4 * LAYERS, D])
        w1_sb = sb("w1_sb", [P, 2, FF])
        w2_sb = sb("w2_sb", [P, 2, CHUNKS, D])
        col = sb("col", [P, NCOL])
        row = sb("row", [P, NROW, D])
        ident_f = sb("ident_f", [P, P])
        ident_b = sb("ident_b", [P, P], bf16)
        causal_q = sb("causal_q", [P, P], bf16)
        causal_k = sb("causal_k", [P, P], bf16)
        keep_row = sb("keep_row", [P, 1])
        half_neg = sb("half_neg", [P, TILES])
        wait_carrier = sb("wait_carrier", [P, 1])
        eps = sb("eps", [P, TILES])
        km_int = sb("km_int", [BATCHES, TOKENS], i32)
        km_bias = sb("km_bias", [BATCHES, TOKENS], bf16)

        stacks = [sb(f"stacks{l}", [ROWS_T, HEADS, 2, TOKENS], bf16) for l in range(LAYERS)]
        q_stack = [st[:, :, 0, :] for st in stacks]
        k_stack = [st[:, :, 1, :] for st in stacks]
        v_sb = [sb(f"v_sb{l}", [P, TILES, VCOLS]) for l in range(LAYERS)]
        neg_max = [sb(f"neg_max{l}", [P, TILES, HEADS]) for l in range(LAYERS)]
        max_rest = [sb(f"max_rest{l}", [P, TILES, HEADS]) for l in range(LAYERS)]
        max_part = [sb(f"max_part{l}", [P, 2, TILES, 3, 8], bf16) for l in range(LAYERS)]
        max_rows = [sb(f"max_rows{l}", [24, 2, TOKENS], bf16) for l in range(LAYERS)]
        ot_sb = [sb(f"ot_sb{l}", [P, 2, 512]) for l in range(LAYERS)]
        rsum = [sb(f"rsum{l}", [P, TILES, PAIRS, 2]) for l in range(LAYERS)]
        heads = [sb(f"heads{l}", [P, TILES, D]) for l in range(LAYERS)]
        heads_t = [sb(f"heads_t{l}", [P, TOKENS]) for l in range(LAYERS)]
        y_t = [sb(f"y_t{l}", [P, TOKENS]) for l in range(LAYERS)]
        y = [sb(f"y{l}", [P, TILES, D]) for l in range(LAYERS)]
        stats = [sb(f"stats{l}", [P, TILES, 6]) for l in range(LAYERS)]
        mean_var = [sb(f"mean_var{l}", [P, TILES, 2]) for l in range(LAYERS)]
        var_eps = [sb(f"var_eps{l}", [P, TILES]) for l in range(LAYERS)]
        rstd = [sb(f"rstd{l}", [P, TILES]) for l in range(LAYERS)]
        centred = [sb(f"centred{l}", [P, TILES, D]) for l in range(LAYERS)]
        x1 = [sb(f"x1_{l}", [P, TILES, D]) for l in range(LAYERS)]
        x2 = [sb(f"x2_{l}", [P, TILES, D]) for l in range(LAYERS)]
        resid = [sb(f"resid{l}", [P, TILES, D]) for l in range(LAYERS)]
        x1_t = [sb(f"x1_t{l}", [P, TOKENS]) for l in range(LAYERS)]
        hid_t = [sb(f"hid_t{l}", [P, CHUNKS, TOKENS]) for l in range(LAYERS)]
        z_t = [sb(f"z_t{l}", [P, TOKENS]) for l in range(LAYERS)]
        z = [sb(f"z{l}", [P, TILES, D]) for l in range(LAYERS)]
        tstats = [sb(f"tstats{l}", [P, TILES, 6]) for l in range(LAYERS)]
        tmean_var = [sb(f"tmean_var{l}", [P, TILES, 2]) for l in range(LAYERS)]
        tvar_eps = [sb(f"tvar_eps{l}", [P, TILES]) for l in range(LAYERS)]
        trstd = [sb(f"trstd{l}", [P, TILES]) for l in range(LAYERS)]
        tcentred = [sb(f"tcentred{l}", [P, TILES, D]) for l in range(LAYERS)]
        x_in = sb("x_in", [P, TILES, D])
        ctx_in = {CAUSAL: sb("ctx_in0", [P, TILES, D]), CROSS: sb("ctx_in2", [P, TILES, D])}
        in_t = [sb(f"in_t{l}", [P, 2, TOKENS]) for l in range(LAYERS)]
        qk = [sb(f"qk{l}", [P, 2 * TOKENS]) for l in range(LAYERS)]
        qk_rest = [sb(f"qk_rest{l}", [P, 2 * TOKENS]) for l in range(LAYERS)]
        qk_part = [sb(f"qk_part{l}", [P, 2, 3, TOKENS], bf16) for l in range(LAYERS)]
        sm_int = sb("sm_int", [P, TILES, TOKENS], i32)
        sm_q = sb("sm_q", [P, TILES, TOKENS], bf16)
        sm_k = sb("sm_k", [P, TILES, TOKENS], bf16)
        p_sb = sb("p_sb", [P, TILES, HEADS, TOKENS])

        bank = [es.enter_context(nc.psum_tensor(f"bank{n}", [P, 512], f32)) for n in range(8)]
        S_BANK, T_BANK = bank[0:2], bank[2:4]
        O_BANK, M_BANK, OUT_BANK, TAIL_BANK = bank[4:8]

        loaded = [sem(f"loaded{n}") for n in range(6)]
        consts = signals("consts", ["selects", "mask"])
        stacks_set = [sem(f"stacks_set{l}") for l in range(LAYERS)]
        made = sem("made")
        mask_saved = sem("mask_saved")
        x_loaded = sem("x_loaded")
        ctx_loaded = {CAUSAL: sem("ctx_loaded0"), CROSS: sem("ctx_loaded2")}
        resid_loaded = sem("resid_loaded")
        sm_loaded = sem("sm_loaded")
        out_stored = sem("out_stored")
        stacked = [sem(f"stacked{l}") for l in range(LAYERS)]
        STACKED = [TERMS * 16, TERMS * 16, (TERMS + 1) * 16]
        s_written = per_layer("s_written", lambda l: range(UNITS[l]))
        s_read = per_layer("s_read", lambda l: range(UNITS[l]))
        t_written = per_layer("t_written", lambda l: range(UNITS[l]))
        p_ready = per_layer("p_ready", lambda l: range(UNITS[l]))
        max_split = per_layer("max_split", [(g, n) for g in range(2) for n in ("part1", "rest", "part2", "part3")])
        max_turned = per_layer("max_turned", range(2))
        max_copied = per_layer("max_copied", range(2))
        max_in = [[signals(f"max_in{l}_{g}", ["dma"], 16) for g in range(2)] for l in range(LAYERS)]
        pv_done = per_layer("pv_done", range(2))
        o_copied = per_layer("o_copied", range(2))
        out_pe = per_layer("out_pe", ["o0", "o1", "heads", "wo", "back"])
        out_act = per_layer("out_act", ["heads", "wo"])
        out_dve = per_layer("out_dve", lambda l: ["recip0"] + ["keep0"] * (l == CAUSAL) + [
            "norm0", "recip1", "norm1", "add", "stats", "aggr", "centre0", "centre1", "norm_a", "norm_b"])
        out_pool = per_layer("out_pool", ["eps", "pow"])
        tail_pe = per_layer("tail_pe", ["x", "up0", "up1", "down", "back"])
        tail_act = per_layer("tail_act", ["x", "up0", "up1", "down"])
        tail_dve = per_layer("tail_dve", ["add", "stats", "aggr", "centre0", "centre1", "norm_a", "norm_b"])
        tail_pool = per_layer("tail_pool", ["eps", "pow"])
        prep_pe = per_layer("prep_pe", lambda l: ["mask"] * (l == SELF) + ["in", "qk", "v"])
        prep_act = per_layer("prep_act", lambda l: ["mask"] * (l == SELF) + ["in", "qk"])
        prep_dve = per_layer("prep_dve", ["part1", "v", "part2"])
        prep_pool = per_layer("prep_pool", ["rest", "part3"])
        mask_q = signals("mask_q", ["bias"])
        resid_kept = {SELF: signals("resid_kept1", ["copy"]), CROSS: signals("resid_kept2", ["copy"])}

        def iterations(eng, slot):
            for i in range(-1, LOOP_FROM):
                for s in range(3):
                    slot(i, s)
            with eng.Fori(LOOP_FROM, LOOP_TO) as reg:
                for s in range(3):
                    slot(Batch(reg, 0), s)
            for i in range(LOOP_TO, BATCHES + LAYERS):
                for s in range(3):
                    slot(i, s)

        def constant_rows(eng, l):
            for n, (rows, is_) in enumerate(((v_sb[l][:], 1.0), (k_stack[l][32:ROWS_T], 1.0),
                                             (q_stack[l][0:1], 1.0), (k_stack[l][0:1], 0.0))):
                if n and eng is nc.gpsimd:
                    eng.wait_ge(stacks_set[l], n)
                eng.memset(rows, is_).then_inc(stacks_set[l], 1)

        SET = 4

        def starts(b):
            return not isinstance(b, Batch) and b == 0

        def halves(a):
            return a[:, :].rearrange("p (c t) -> p c t", c=2)

        def earlier_slot(i, s):
            while True:
                i, s = (i, s - 1) if s else (i - 1, 2)
                if isinstance(i, Batch):
                    return i, s
                if i < 0:
                    return None
                if exists(i - s):
                    return i, s

        block = es.enter_context(nc.Block())

        @block.sync
        def _(sp):
            sp.dma_start(w4_sb[:], w4.rearrange("n i o -> i n o")).then_inc(loaded[0], 16)
            sp.dma_start(w1_sb[:], w1.rearrange("n i f -> i n f")).then_inc(loaded[1], 16)
            sp.dma_start(w2_sb[:], w2.rearrange("n (c f) o -> f n c o", f=P)).then_inc(loaded[2], 16)

            def tokens(a, b):
                at = bass.ds(value(b), 1) if isinstance(b, Batch) else slice(b, b + 1)
                return a[at, :, :].rearrange("a (t p) d -> (a p) t d", p=P)

            def load_prepare0(b):
                if isinstance(b, Batch) or b > 0:
                    sp.wait_ge(*prep_pe[CAUSAL].upto(b - 1, "in"))
                sp.dma_start(x_in[:], tokens(x, b)).then_inc(x_loaded, 16)
                sp.dma_start(ctx_in[CAUSAL][:], tokens(ctx, b)).then_inc(ctx_loaded[CAUSAL], 16)

            def stack(l, b):
                if starts(b):
                    sp.wait_ge(stacks_set[l], SET)
                for part, of in (("part1", prep_dve), ("part2", prep_dve), ("part3", prep_pool)):
                    sp.wait_ge(*of[l].upto(b, part))
                    n = int(part[-1]) - 1
                    if n == 0 and l == CROSS:
                        at = bass.ds(value(b), 1) if isinstance(b, Batch) else slice(b, b + 1)
                        sp.dma_start(k_stack[l][0:1, :, :],
                                     mask_rows[at, :].rearrange("(a h) k -> a h k", a=1)
                                     .broadcast_to([1, HEADS, TOKENS])).then_inc(stacked[l], 16)
                    for t, (qn, kn) in enumerate(PRODUCTS):
                        if max(qn, kn) == n:
                            flat = qk_part[l][:, :, :, :].rearrange("p c n t -> p (c n) t")
                            sp.dma_start(stacks[l][1 + DK * t:1 + DK * (t + 1), :, :, :],
                                         flat[:, qn:3 + kn + 1:3 + kn - qn, :]).then_inc(stacked[l], 16)

            def max_dma(l, b, g):
                sp.wait_ge(*max_copied[l].upto(b, g))
                sp.dma_start(q_stack[l][MAX_ROW:MAX_ROW + 3, 8 * g:8 * g + 8, :],
                             max_rows[l][:, g, :]).then_inc(max_in[l][g].sem, 16)

            def slot(i, s):
                (l, b), (ln, bn), (lo, bo), (lt, bt) = slot_tasks(i, s)
                first = not isinstance(i, Batch) and i == -1
                if s == 0 and exists(i + 1) and not first:
                    load_prepare0(i + 1)
                if s == 0 and exists(i):
                    sp.dma_start(resid[CAUSAL][:], tokens(x, i)).then_inc(resid_loaded, 16)
                if s == 1 and exists(i):
                    at = bass.ds(value(i), 1) if isinstance(i, Batch) else slice(i, i + 1)
                    sp.dma_start(sm_int[:], self_mask[at, :, :].rearrange("a (t p) k -> (a p) t k", p=P))\
                        .then_inc(sm_loaded, 16)
                if s == 2 and exists(i - 1):
                    if isinstance(i, Batch) or i > 1:
                        sp.wait_ge(*prep_pe[CROSS].upto(i - 2, "in"))
                    sp.dma_start(ctx_in[CROSS][:], tokens(ctx, i - 1)).then_inc(ctx_loaded[CROSS], 16)
                if exists(b):
                    max_dma(l, b, 1)
                if s == 1 and exists(i + 1):
                    stack(CAUSAL, i + 1)
                if s == 0 and exists(bt):
                    stack(CROSS, bt)
                if exists(bn):
                    max_dma(ln, bn, 0)
                if s == 1 and exists(bt):
                    sp.wait_ge(*tail_dve[CROSS].upto(bt, "norm_b"))
                    sp.dma_start(tokens(out, bt), x2[CROSS][:]).then_inc(out_stored, 16)
                if s == 2 and exists(bt):
                    stack(SELF, bt)

            sp.dma_start(km_int[:], key_mask).then_inc(loaded[5], 16)
            load_prepare0(0)
            sp.dma_start(col[:], bias_col).then_inc(loaded[3], 16)
            sp.dma_start(row[:], bias_row.rearrange("(a n) d -> a n d", a=1).broadcast_to([P, NROW, D]))\
                .then_inc(loaded[4], 16)
            sp.wait_ge(*consts.upto(0, "mask"))
            sp.dma_start(mask_rows[:, :], km_bias[:]).then_inc(mask_saved, 16)
            sp.wait_ge(mask_saved, 16)
            iterations(sp, slot)
            sp.wait_ge(out_stored, 16 * BATCHES)

        @block.tensor
        def _(pe):
            last_read = {"o": None, "m": None, "out": None, "tail": None, "s": None}

            def bank_free(name):
                if last_read[name] is not None:
                    pe.wait_ge(*last_read[name][0].upto(*last_read[name][1:]))

            def scores(l, b, u):
                if u == 0:
                    if starts(b):
                        pe.wait_ge(stacks_set[l], SET)
                    pe.wait_ge(stacked[l], value(b, STACKED[l], STACKED[l]))
                    if l == SELF:
                        pe.wait_ge(*mask_q.upto(b, "bias"))
                if u >= 2:
                    pe.wait_ge(*s_read[l].upto(b, u - 2))
                elif last_read["s"] is not None:
                    lp, bp = last_read["s"]
                    pe.wait_ge(*s_read[lp].upto(bp, UNITS[lp] - 2 + u))
                qt, h0, n = unit_of(l, u)
                keys = TOKENS if n == 2 else P
                dst = S_BANK[u % 2]
                if l == SELF:
                    nc.tensor.matmul(dst[:, :], ident_b[:], sm_q[:, qt:qt + 1, :].broadcast_to([P, 2, TOKENS]),
                                     start=True, stop=False)
                if l == CAUSAL:
                    nc.tensor.matmul(dst[:, :].rearrange("p (h k) -> p h k", h=n)[:, :, keys - P:keys],
                                     ident_b[:], causal_q[:, :].rearrange("p (a k) -> p a k", a=1)
                                     .broadcast_to([P, n, P]), start=True, stop=False, skip_group_check=True)
                for e in range(n):
                    mm = nc.tensor.matmul(dst[:, e * keys:(e + 1) * keys],
                                          q_stack[l][0:ROWS_S, h0 + e, qt * P:(qt + 1) * P],
                                          k_stack[l][0:ROWS_S, h0 + e, 0:keys],
                                          start=(l == CROSS), stop=(l == CROSS or e == n - 1),
                                          skip_group_check=(l == CAUSAL))
                mm.then_inc(s_written[l].sem, 1)
                if u == UNITS[l] - 1:
                    last_read["s"] = (l, b)

            def scores_t(l, b, u, i, s):
                n = UNITS[l]
                if u % (n // 2) == 0:
                    pe.wait_ge(*max_in[l][u // (n // 2)].upto(b, "dma"))
                if u == 0 and l == SELF:
                    pe.wait_ge(*prep_act[SELF].upto(b, "mask"))
                if u >= 2:
                    pe.wait_ge(*p_ready[l].upto(b, u - 2))
                elif (before := earlier_slot(i, s)) is not None:
                    lp, bp = before[1], before[0] - before[1]
                    pe.wait_ge(*p_ready[lp].upto(bp, UNITS[lp] - 2 + u))
                kt, h0, n = unit_of(l, u)
                if l == CAUSAL:
                    kt = 1 - kt
                q0 = P if n == 4 else 0
                qs = TOKENS - q0
                dst = T_BANK[u % 2]
                if l == SELF:
                    nc.tensor.matmul(dst[:, :], ident_b[:], sm_k[:, kt:kt + 1, :].broadcast_to([P, 2, TOKENS]),
                                     start=True, stop=False)
                if l == CAUSAL:
                    nc.tensor.matmul(dst[:, :].rearrange("p (h q) -> p h q", h=n)[:, :, 0:P],
                                     ident_b[:], causal_k[:, :].rearrange("p (a k) -> p a k", a=1)
                                     .broadcast_to([P, n, P]), start=True, stop=False, skip_group_check=True)
                for e in range(n):
                    mm = nc.tensor.matmul(dst[:, e * qs:(e + 1) * qs],
                                          k_stack[l][0:ROWS_T, h0 + e, kt * P:(kt + 1) * P],
                                          q_stack[l][0:ROWS_T, h0 + e, q0:TOKENS],
                                          start=(l == CROSS), stop=(l == CROSS or e == n - 1),
                                          skip_group_check=(l == CAUSAL))
                mm.then_inc(t_written[l].sem, 1)

            def turn_max(l, b, g):
                bank_free("m")
                pe.wait_ge(*max_split[l].upto(b, (g, "part3")))
                for qt in range(TILES):
                    mm = nc.tensor.transpose(M_BANK[0:24, :].bitcast(bf16)[:, qt * P:(qt + 1) * P],
                                             max_part[l][:, g, qt, :, :].rearrange("p c h -> p (c h)"), ident_b[:])
                mm.then_inc(max_turned[l].sem, 1)
                last_read["m"] = (max_copied[l], b, g)

            def pv(l, b, g):
                bank_free("o")
                if g == 0:
                    pe.wait_ge(*prep_dve[l].upto(b, "v"))
                pe.wait_ge(*p_ready[l].upto(b, (g + 1) * UNITS[l] // 2 - 1))
                for kt in range(TILES):
                    for j in range(4):
                        pair = 4 * g + j
                        q0 = P if (kt == 1 and l == CAUSAL) else 0
                        mm = nc.tensor.matmul(
                            O_BANK[32 * j:32 * j + 32, :].rearrange("p (e q) -> p e q", e=2)[:, :, q0:TOKENS],
                            v_sb[l][:, kt, 2 * VW * pair:2 * VW * pair + 32],
                            p_sb[:, kt, 2 * pair:2 * pair + 2, q0:TOKENS],
                            start=(kt == 0), stop=(kt == 1), skip_group_check=True)
                mm.then_inc(pv_done[l].sem, 1)
                last_read["o"] = (o_copied[l], b, g)

            def out_turn_o(l, b, qt):
                bank_free("out")
                pe.wait_ge(*o_copied[l].upto(b, 1))
                for g in range(2):
                    for e in range(2):
                        mm = nc.tensor.transpose(OUT_BANK[:, 256 * e + P * g:256 * e + P * (g + 1)],
                                                 ot_sb[l][:, g, e * TOKENS + qt * P:e * TOKENS + (qt + 1) * P],
                                                 ident_f[:])
                mm.then_inc(out_pe[l].sem, 1)
                last_read["out"] = (out_dve[l], b, f"norm{qt}")

            def two_turns(dst, src):
                for t in range(TILES):
                    mm = nc.tensor.transpose(dst[:, t * P:(t + 1) * P], src(t), ident_f[:])
                return mm

            def out_heads(l, b):
                bank_free("out")
                two_turns(OUT_BANK, lambda t: heads[l][:, t, :]).then_inc(out_pe[l].sem, 1)
                last_read["out"] = (out_act[l], b, "heads")

            def out_wo(l, b):
                bank_free("out")
                nc.tensor.matmul(OUT_BANK[:, 0:TOKENS], w4_sb[:, 4 * l + 3, :], heads_t[l][:],
                                 start=True, stop=True).then_inc(out_pe[l].sem, 1)
                last_read["out"] = (out_act[l], b, "wo")

            def out_back(l, b):
                bank_free("out")
                two_turns(OUT_BANK, lambda t: y_t[l][:, t * P:(t + 1) * P]).then_inc(out_pe[l].sem, 1)
                last_read["out"] = (out_dve[l], b, "add")

            def tail_x(l, b):
                bank_free("tail")
                pe.wait_ge(*out_dve[l].upto(b, "norm_b"))
                two_turns(TAIL_BANK, lambda t: x1[l][:, t, :]).then_inc(tail_pe[l].sem, 1)
                last_read["tail"] = (tail_act[l], b, "x")

            def tail_up(l, b, n):
                bank_free("tail")
                for c in range(2):
                    mm = nc.tensor.matmul(TAIL_BANK[:, c * TOKENS:(c + 1) * TOKENS],
                                          w1_sb[:, FFN[l], (2 * n + c) * P:(2 * n + c + 1) * P], x1_t[l][:],
                                          start=True, stop=True)
                mm.then_inc(tail_pe[l].sem, 1)
                last_read["tail"] = (tail_act[l], b, f"up{n}")

            def tail_down(l, b):
                bank_free("tail")
                for c in range(CHUNKS):
                    mm = nc.tensor.matmul(TAIL_BANK[:, 0:TOKENS], w2_sb[:, FFN[l], c, :], hid_t[l][:, c, :],
                                          start=(c == 0), stop=(c == CHUNKS - 1))
                mm.then_inc(tail_pe[l].sem, 1)
                last_read["tail"] = (tail_act[l], b, "down")

            def tail_back(l, b):
                bank_free("tail")
                two_turns(TAIL_BANK, lambda t: z_t[l][:, t * P:(t + 1) * P]).then_inc(tail_pe[l].sem, 1)
                last_read["tail"] = (tail_dve[l], b, "add")

            def prep_in(l, b):
                bank_free("tail")
                if l == CAUSAL:
                    pe.wait_ge(x_loaded, value(b, 16, 16))
                    src = x_in
                elif l == SELF:
                    pe.wait_ge(*tail_dve[CAUSAL].upto(b, "norm_b"))
                    src = x2[CAUSAL]
                else:
                    pe.wait_ge(*out_dve[SELF].upto(b, "norm_b"))
                    src = x1[SELF]
                mm = two_turns(TAIL_BANK, lambda t: src[:, t, :])
                if l != SELF:
                    pe.wait_ge(ctx_loaded[l], value(b, 16, 16))
                    mm = two_turns(TAIL_BANK[:, TOKENS:2 * TOKENS], lambda t: ctx_in[l][:, t, :])
                mm.then_inc(prep_pe[l].sem, 1)
                last_read["tail"] = (prep_act[l], b, "in")

            def prep_qk(l, b):
                bank_free("tail")
                for c in range(2):
                    mm = nc.tensor.matmul(TAIL_BANK[:, c * TOKENS:(c + 1) * TOKENS], w4_sb[:, 4 * l + c, :],
                                          in_t[l][:, 0 if l == SELF else c, :], start=True, stop=True)
                mm.then_inc(prep_pe[l].sem, 1)
                last_read["tail"] = (prep_act[l], b, "qk")

            def prep_v(l, b):
                bank_free("tail")
                kv = 0 if l == SELF else 1
                for kt in range(TILES):
                    mm = nc.tensor.matmul(TAIL_BANK[:, kt * D:(kt + 1) * D], in_t[l][:, kv, kt * P:(kt + 1) * P],
                                          w4_sb[:, 4 * l + 2, :], start=True, stop=True)
                mm.then_inc(prep_pe[l].sem, 1)
                last_read["tail"] = (prep_dve[l], b, "v")

            def prep_mask(b):
                bank_free("tail")
                pe.wait_ge(*mask_q.upto(b, "bias"))
                for kt in range(TILES):
                    for qt in range(TILES):
                        mm = nc.tensor.transpose(
                            TAIL_BANK[:, :].bitcast(bf16)[:, kt * TOKENS + qt * P:kt * TOKENS + (qt + 1) * P],
                            sm_q[:, qt, kt * P:(kt + 1) * P], ident_b[:])
                mm.then_inc(prep_pe[SELF].sem, 1)
                last_read["tail"] = (prep_act[SELF], b, "mask")

            def slot(i, s):
                (l, b), (ln, bn), (lo, bo), (lt, bt) = slot_tasks(i, s)
                for t in range(STEPS):
                    if t == 2 and exists(b):
                        turn_max(l, b, 1)
                    if exists(b):
                        for u in [*units(l, 0, t), *units(l, 1, t)]:
                            scores_t(l, b, u, i, s)
                    if exists(bn):
                        for u in [*units(ln, 0, t), *units(ln, 1, t)]:
                            scores(ln, bn, u)
                    if t == 1 and exists(bo):
                        pv(lo, bo, 1)
                    if t == 10 and exists(b):
                        pv(l, b, 0)
                    if t == 10 and exists(bn):
                        turn_max(ln, bn, 0)
                    if exists(bo):
                        if t == 4:
                            out_turn_o(lo, bo, 0)
                        if t == 6:
                            out_turn_o(lo, bo, 1)
                        if t == 8:
                            out_heads(lo, bo)
                        if t == 10:
                            out_wo(lo, bo)
                        if t == 11:
                            out_back(lo, bo)
                    if exists(bt) and lt == CROSS:
                        if t == 1:
                            tail_x(lt, bt)
                        if t == 4:
                            tail_up(lt, bt, 0)
                        if t == 6:
                            tail_up(lt, bt, 1)
                        if t == 8:
                            tail_down(lt, bt)
                        if t == 10:
                            tail_back(lt, bt)
                    if exists(bt) and lt == CAUSAL:
                        if t == 0:
                            tail_x(lt, bt)
                        if t == 1:
                            tail_up(lt, bt, 0)
                        if t == 2:
                            tail_up(lt, bt, 1)
                        if t == 3:
                            tail_down(lt, bt)
                        if t == 4:
                            tail_back(lt, bt)
                        if t == 6:
                            prep_mask(bt)
                        if t == 8:
                            prep_in(SELF, bt)
                        if t == 9:
                            prep_qk(SELF, bt)
                        if t == 11:
                            prep_v(SELF, bt)
                    if exists(bt) and lt == SELF:
                        if t == 1:
                            prep_in(CROSS, bt)
                        if t == 3:
                            prep_qk(CROSS, bt)
                        if t == 5:
                            prep_v(CROSS, bt)
                    if s == 0 and exists(i + 1):
                        if t == 8:
                            prep_in(CAUSAL, i + 1)
                        if t == 11:
                            prep_qk(CAUSAL, i + 1)
                    if s == 1 and exists(i + 1) and t == 2:
                        prep_v(CAUSAL, i + 1)

            for n in range(5):
                if n != 4:
                    pe.wait_ge(loaded[n], 16)
            pe.wait_ge(*consts.upto(0, "selects"))

            def looping(eng, slot):
                for i in range(-1, LOOP_FROM):
                    for s in range(3):
                        slot(i, s)
                with eng.Fori(LOOP_FROM, LOOP_TO) as reg:
                    for k, v in last_read.items():
                        last_read[k] = (v[0], Batch(reg, v[1] - LOOP_FROM), *v[2:])
                    before = dict(last_read)
                    for s in range(3):
                        slot(Batch(reg, 0), s)
                    for k, v in last_read.items():
                        assert (v[0], v[1].off, *v[2:]) == (before[k][0], before[k][1].off + 1, *before[k][2:])
                for k, v in last_read.items():
                    last_read[k] = (v[0], v[1].off + LOOP_TO - 1, *v[2:])
                for i in range(LOOP_TO, BATCHES + LAYERS):
                    for s in range(3):
                        slot(i, s)
            looping(pe, slot)

        @block.scalar
        def _(act):
            def exps(l, b, u, i, s):
                n = UNITS[l] // 2
                if u % n == 0 and (before := earlier_slot(i, s)) is not None:
                    act.wait_ge(*pv_done[before[1]].upto(before[0] - before[1], u // n))
                act.wait_ge(*t_written[l].upto(b, u))
                kt, h0, nh = unit_of(l, u)
                if l == CAUSAL:
                    kt = 1 - kt
                q0 = P if nh == 4 else 0
                nc.scalar.activation(p_sb[:, kt, h0:h0 + nh, q0:TOKENS],
                                     T_BANK[u % 2][:, :].rearrange("p (h q) -> p h q", h=nh),
                                     ACT.Exp, scale=SCALE).then_inc(p_ready[l].sem, 1)

            def copy_max(l, b, g):
                act.wait_ge(*max_turned[l].upto(b, g))
                nc.scalar.activation(max_rows[l][:, g, :], M_BANK[0:24, :].bitcast(bf16)[:, 0:TOKENS], ACT.Copy)\
                    .then_inc(max_copied[l].sem, 1)

            def copy_o(l, b, g):
                act.wait_ge(*pv_done[l].upto(b, g))
                nc.scalar.activation(ot_sb[l][:, g, :], O_BANK[:, :], ACT.Copy).then_inc(o_copied[l].sem, 1)

            def out_heads(l, b):
                act.wait_ge(*out_pe[l].upto(b, "heads"))
                nc.scalar.activation(heads_t[l][:], OUT_BANK[:, 0:TOKENS], ACT.Copy).then_inc(out_act[l].sem, 1)

            def out_wo(l, b):
                act.wait_ge(*out_pe[l].upto(b, "wo"))
                nc.scalar.activation(y_t[l][:], OUT_BANK[:, 0:TOKENS], ACT.Identity,
                                     bias=col[:, BO + l:BO + l + 1]).then_inc(out_act[l].sem, 1)

            def tail_x(l, b):
                act.wait_ge(*tail_pe[l].upto(b, "x"))
                nc.scalar.activation(x1_t[l][:], TAIL_BANK[:, 0:TOKENS], ACT.Copy).then_inc(tail_act[l].sem, 1)

            def tail_up(l, b, n):
                act.wait_ge(*tail_pe[l].upto(b, f"up{n}"))
                for c in range(2):
                    at = B1 + FFN[l] * CHUNKS + 2 * n + c
                    ins = nc.scalar.activation(hid_t[l][:, 2 * n + c, :], TAIL_BANK[:, c * TOKENS:(c + 1) * TOKENS],
                                               ACT.Relu, bias=col[:, at:at + 1])
                ins.then_inc(tail_act[l].sem, 1)

            def tail_down(l, b):
                act.wait_ge(*tail_pe[l].upto(b, "down"))
                nc.scalar.activation(z_t[l][:], TAIL_BANK[:, 0:TOKENS], ACT.Identity,
                                     bias=col[:, B2 + FFN[l]:B2 + FFN[l] + 1]).then_inc(tail_act[l].sem, 1)

            def prep_in(l, b):
                act.wait_ge(*prep_pe[l].upto(b, "in"))
                n = 1 if l == SELF else 2
                nc.scalar.activation(in_t[l][:, 0:n, :].rearrange("p a t -> p (a t)"), TAIL_BANK[:, 0:n * TOKENS],
                                     ACT.Copy).then_inc(prep_act[l].sem, 1)

            def prep_qk(l, b):
                act.wait_ge(*prep_pe[l].upto(b, "qk"))
                for c, at in ((0, BQ + l), (1, BK + l)):
                    ins = nc.scalar.activation(qk[l][:, c * TOKENS:(c + 1) * TOKENS],
                                               TAIL_BANK[:, c * TOKENS:(c + 1) * TOKENS], ACT.Identity,
                                               bias=col[:, at:at + 1])
                ins.then_inc(prep_act[l].sem, 1)

            def prep_mask(b):
                act.wait_ge(*prep_pe[SELF].upto(b, "mask"))
                nc.scalar.activation(sm_k[:, :, :].rearrange("p t q -> p (t q)"),
                                     TAIL_BANK[:, :].bitcast(bf16)[:, 0:2 * TOKENS], ACT.Copy)\
                    .then_inc(prep_act[SELF].sem, 1)

            def slot(i, s):
                (l, b), (ln, bn), (lo, bo), (lt, bt) = slot_tasks(i, s)
                for t in range(STEPS + 1):
                    if t == 3 and exists(b):
                        copy_max(l, b, 1)
                    if exists(b):
                        for u in [*units(l, 0, t), *units(l, 1, t)]:
                            exps(l, b, u, i, s)
                    if t == 2 and exists(bo):
                        copy_o(lo, bo, 1)
                    if t == 11 and exists(b):
                        copy_o(l, b, 0)
                    if t == 11 and exists(bn):
                        copy_max(ln, bn, 0)
                    if exists(bo):
                        if t == 8:
                            out_heads(lo, bo)
                        if t == 10:
                            out_wo(lo, bo)
                    if exists(bt) and lt == CROSS:
                        if t == 1:
                            tail_x(lt, bt)
                        if t == 5:
                            tail_up(lt, bt, 0)
                        if t == 7:
                            tail_up(lt, bt, 1)
                        if t == 8:
                            tail_down(lt, bt)
                    if exists(bt) and lt == CAUSAL:
                        if t == 0:
                            tail_x(lt, bt)
                        if t == 1:
                            tail_up(lt, bt, 0)
                        if t == 2:
                            tail_up(lt, bt, 1)
                        if t == 3:
                            tail_down(lt, bt)
                        if t == 6:
                            prep_mask(bt)
                        if t == 8:
                            prep_in(SELF, bt)
                        if t == 9:
                            prep_qk(SELF, bt)
                    if exists(bt) and lt == SELF:
                        if t == 2:
                            prep_in(CROSS, bt)
                        if t == 4:
                            prep_qk(CROSS, bt)
                    if s == 0 and exists(i + 1):
                        if t == 9:
                            prep_in(CAUSAL, i + 1)
                        if t == 12:
                            prep_qk(CAUSAL, i + 1)

            act.wait_ge(loaded[3], 16)
            iterations(act, slot)

        @block.vector
        def _(dve):
            def reduce_unit(l, b, u):
                dve.wait_ge(*s_written[l].upto(b, u))
                qt, h0, n = unit_of(l, u)
                nc.vector.tensor_reduce(neg_max[l][:, qt, h0:h0 + n],
                                        S_BANK[u % 2][:, :].rearrange("p (h k) -> p h k", h=n),
                                        axis=AX.X, op=ALU.max, negate=True).then_inc(s_read[l].sem, 1)

            def split_max(l, b, g):
                src = neg_max[l][:, :, 8 * g:8 * g + 8]
                rest = max_rest[l][:, :, 8 * g:8 * g + 8]
                part = max_part[l][:, g, :, :, :]
                dve.wait_ge(*s_read[l].upto(b, (g + 1) * UNITS[l] // 2 - 1))
                nc.vector.tensor_copy(part[:, :, 0, :], src).then_inc(max_split[l].sem, 1)
                dve.wait_ge(*max_split[l].upto(b, (g, "part1")))
                nc.vector.tensor_tensor(rest, src, part[:, :, 0, :], ALU.subtract).then_inc(max_split[l].sem, 1)
                dve.wait_ge(*max_split[l].upto(b, (g, "rest")))
                nc.vector.tensor_copy(part[:, :, 1, :], rest).then_inc(max_split[l].sem, 1)
                dve.wait_ge(*max_split[l].upto(b, (g, "part2")))
                nc.vector.tensor_tensor(part[:, :, 2, :], rest, part[:, :, 1, :], ALU.subtract)\
                    .then_inc(max_split[l].sem, 1)

            def out_norm(l, b, qt):
                done = out_dve[l]
                dve.wait_ge(*out_pe[l].upto(b, f"o{qt}"))
                sums = bass.AP(OUT_BANK, DK, [[512, P], [32, PAIRS], [256 + VW, 2]])
                vals = bass.AP(OUT_BANK, 0, [[512, P], [32, PAIRS], [256 + VW, 2], [1, DK]])
                nc.vector.reciprocal(rsum[l][:, qt, :, :], sums).then_inc(done.sem, 1)
                dve.wait_ge(*done.upto(b, f"recip{qt}"))
                if qt == 0:
                    if l == CAUSAL:
                        nc.vector.tensor_scalar(rsum[l][:, 0, :, :], rsum[l][:, 0, :, :], keep_row[:, 0:1], None,
                                                ALU.mult).then_inc(done.sem, 1)
                        dve.wait_ge(*done.upto(b, "keep0"))
                r = rsum[l][:, qt, :, :].rearrange("p (a b) (e c) -> p (a b) e c", a=1, c=1)\
                    .broadcast_to([P, PAIRS, 2, DK])
                nc.vector.tensor_tensor(heads[l][:, qt, :].rearrange("p (a e d) -> p a e d", e=2, d=DK), vals, r,
                                        ALU.mult).then_inc(done.sem, 1)

            def layer_norm(l, b, done, pool, psum, res, y, st, mv, rs, cen, ln, dst):
                nc.vector.tensor_tensor(y[l][:].rearrange("p t d -> p (t d)"), psum[:, 0:TOKENS],
                                        res[:].rearrange("p t d -> p (t d)"), ALU.add).then_inc(done.sem, 1)
                dve.wait_ge(*done.upto(b, "add"))
                nc.vector.bn_stats(st[l][:, 0, :], y[l][:, 0, :])
                nc.vector.bn_stats(st[l][:, 1, :], y[l][:, 1, :]).then_inc(done.sem, 1)
                dve.wait_ge(*done.upto(b, "stats"))
                nc.vector.memset(wait_carrier[:], 0.0)
                nc.vector.bn_aggr(mv[l][:, 0, :], st[l][:, 0, :])
                nc.vector.bn_aggr(mv[l][:, 1, :], st[l][:, 1, :]).then_inc(done.sem, 1)
                dve.wait_ge(*done.upto(b, "aggr"))
                for t in range(TILES):
                    nc.vector.scalar_tensor_tensor(out=cen[l][:, t, :], in0=y[l][:, t, :], scalar=mv[l][:, t, 0:1],
                                                   in1=row[:, LNG + ln, :], op0=ALU.subtract, op1=ALU.mult)\
                        .then_inc(done.sem, 1)

            def layer_norm_end(l, b, done, pool, rs, cen, ln, dst):
                dve.wait_ge(*pool[l].upto(b, "pow"))
                dve.wait_ge(*done.upto(b, "centre1"))
                for t in range(TILES):
                    nc.vector.scalar_tensor_tensor(out=dst[l][:, t, :], in0=cen[l][:, t, :], scalar=rs[l][:, t:t + 1],
                                                   in1=row[:, LNB + ln, :], op0=ALU.mult, op1=ALU.add)\
                        .then_inc(done.sem, 1)

            def out_ln(l, b):
                dve.wait_ge(*out_pe[l].upto(b, "back"))
                if l == CAUSAL:
                    dve.wait_ge(resid_loaded, value(b, 16, 16))
                else:
                    dve.wait_ge(*resid_kept[l].upto(b, "copy"))
                layer_norm(l, b, out_dve[l], out_pool, OUT_BANK, resid[l], y, stats, mean_var, rstd, centred,
                           LN_OUT[l], x1)

            def out_ln_end(l, b):
                if l == SELF and (isinstance(b, Batch) or b > 0):
                    dve.wait_ge(*resid_kept[CROSS].upto(b - 1, "copy"))
                layer_norm_end(l, b, out_dve[l], out_pool, rstd, centred, LN_OUT[l], x1)

            def tail_ln(l, b):
                dve.wait_ge(*tail_pe[l].upto(b, "back"))
                layer_norm(l, b, tail_dve[l], tail_pool, TAIL_BANK, x1[l], z, tstats, tmean_var, trstd, tcentred,
                           LN_TAIL[l], x2)

            def tail_ln_end(l, b):
                if l == CROSS and (isinstance(b, Batch) or b > 0):
                    dve.wait_ge(out_stored, value(b, 16))
                if l == CAUSAL and (isinstance(b, Batch) or b > 0):
                    dve.wait_ge(*resid_kept[SELF].upto(b - 1, "copy"))
                layer_norm_end(l, b, tail_dve[l], tail_pool, trstd, tcentred, LN_TAIL[l], x2)

            def prep_v(l, b):
                if starts(b):
                    dve.wait_ge(stacks_set[l], SET)
                dve.wait_ge(*prep_pe[l].upto(b, "v"))
                nc.vector.tensor_tensor(
                    v_sb[l][:, :, 0:HEADS * VW].rearrange("p t (h w) -> p t h w", w=VW)[:, :, :, 0:DK],
                    TAIL_BANK[:, 0:TILES * D].rearrange("p (t h d) -> p t h d", t=TILES, d=DK),
                    row[:, BV + l:BV + l + 1, :].rearrange("p a (h d) -> p a h d", d=DK)
                    .broadcast_to([P, TILES, HEADS, DK]), ALU.add).then_inc(prep_dve[l].sem, 1)

            def prep_part1(l, b):
                if isinstance(b, Batch) or b > 0:
                    dve.wait_ge(*t_written[l].upto(b - 1, UNITS[l] - 1))
                    dve.wait_ge(stacked[l], value(b, STACKED[l]))
                dve.wait_ge(*prep_act[l].upto(b, "qk"))
                nc.vector.tensor_copy(qk_part[l][:, :, 0, :], halves(qk[l])).then_inc(prep_dve[l].sem, 1)

            def prep_part2(l, b):
                dve.wait_ge(*prep_pool[l].upto(b, "rest"))
                nc.vector.tensor_copy(qk_part[l][:, :, 1, :], halves(qk_rest[l])).then_inc(prep_dve[l].sem, 1)

            def keep_residual(l, b, src, src_done):
                if isinstance(b, Batch) or b > 0:
                    dve.wait_ge(*out_dve[l].upto(b - 1, "add"))
                dve.wait_ge(*src_done.upto(b, "norm_b"))
                nc.vector.tensor_copy(resid[l][:], src[:]).then_inc(resid_kept[l].sem, 1)

            def mask_bias(b):
                if isinstance(b, Batch) or b > 0:
                    dve.wait_ge(*s_written[SELF].upto(b - 1, UNITS[SELF] - 1))
                    dve.wait_ge(*prep_pe[SELF].upto(b - 1, "mask"))
                dve.wait_ge(sm_loaded, value(b, 16, 16))
                nc.vector.tensor_scalar(sm_q[:].rearrange("p t k -> p (t k)"),
                                        sm_int[:].rearrange("p t k -> p (t k)"), 0.0, -BIG,
                                        ALU.is_equal, ALU.mult).then_inc(mask_q.sem, 1)

            def slot(i, s):
                (l, b), (ln, bn), (lo, bo), (lt, bt) = slot_tasks(i, s)
                for t in range(STEPS + 1):
                    if t == 2 and s == 0 and exists(i - 1):
                        keep_residual(SELF, i - 1, x2[CAUSAL], tail_dve[CAUSAL])
                    if t == 2 and s == 1 and exists(i - 2):
                        keep_residual(CROSS, i - 2, x1[SELF], out_dve[SELF])
                    if t == 3 and s == 2 and exists(i):
                        mask_bias(i)
                    if t == 1 and exists(b):
                        split_max(l, b, 1)
                    if t == 0 and s == 1 and exists(i + 1):
                        prep_part1(CAUSAL, i + 1)
                    if exists(bn):
                        for u in [*units(ln, 0, t), *units(ln, 1, t)]:
                            reduce_unit(ln, bn, u)
                    if t == 8 and exists(bn):
                        split_max(ln, bn, 0)
                    if exists(bo):
                        if t == 4:
                            out_norm(lo, bo, 0)
                        if t == 6:
                            out_norm(lo, bo, 1)
                        if t == 12:
                            out_ln(lo, bo)
                        if t == 14:
                            out_ln_end(lo, bo)
                    if exists(bt) and lt == CROSS:
                        if t == 10:
                            tail_ln(lt, bt)
                        if t == 12:
                            tail_ln_end(lt, bt)
                    if exists(bt) and lt == CAUSAL:
                        if t == 5:
                            tail_ln(lt, bt)
                        if t == 7:
                            tail_ln_end(lt, bt)
                        if t == 10:
                            prep_part1(SELF, bt)
                        if t == 11:
                            prep_v(SELF, bt)
                        if t == 12:
                            prep_part2(SELF, bt)
                    if exists(bt) and lt == SELF:
                        if t == 5:
                            prep_part1(CROSS, bt)
                            prep_v(CROSS, bt)
                        if t == 8:
                            prep_part2(CROSS, bt)
                    if s == 1 and exists(i + 1) and t == 3:
                        prep_v(CAUSAL, i + 1)
                        prep_part2(CAUSAL, i + 1)

            constant_rows(nc.vector, CAUSAL)
            dve.wait_ge(loaded[4], 16)
            dve.wait_ge(*consts.upto(0, "selects"))
            iterations(dve, slot)

        @block.gpsimd
        def _(pool):
            nc.gpsimd.memset(ident_f[:], 0.0).then_inc(made, 1)
            nc.gpsimd.memset(ident_b[:], 0.0).then_inc(made, 1)
            nc.gpsimd.memset(causal_q[:], 0.0).then_inc(made, 1)
            nc.gpsimd.memset(causal_k[:], 0.0).then_inc(made, 1)
            nc.gpsimd.memset(keep_row[:], 1.0).then_inc(made, 1)
            nc.gpsimd.memset(half_neg[:], -0.5).then_inc(made, 1)
            nc.gpsimd.memset(eps[:], EPS).then_inc(made, 1)
            pool.wait_ge(made, 7)
            for m in (ident_f, ident_b):
                nc.gpsimd.affine_select(out=m[:], in_=m[:], compare_op=ALU.not_equal, fill=1.0, base=0,
                                        pattern=[[-1, P]], channel_multiplier=1).then_inc(made, 1)
            nc.gpsimd.affine_select(out=causal_q[:], in_=causal_q[:], compare_op=ALU.is_gt, fill=-BIG, base=0,
                                    pattern=[[-1, P]], channel_multiplier=1).then_inc(made, 1)
            nc.gpsimd.affine_select(out=causal_k[:], in_=causal_k[:], compare_op=ALU.is_gt, fill=-BIG, base=0,
                                    pattern=[[1, P]], channel_multiplier=-1).then_inc(made, 1)
            pool.wait_ge(made, 11)
            nc.gpsimd.affine_select(out=keep_row[:], in_=keep_row[:], compare_op=ALU.is_gt, fill=0.0, base=0,
                                    pattern=[[0, 1]], channel_multiplier=1).then_inc(consts.sem, 1)
            pool.wait_ge(loaded[5], 16)
            nc.gpsimd.tensor_scalar(km_bias[:], km_int[:], 0.0, -BIG, ALU.is_equal, ALU.mult)\
                .then_inc(consts.sem, 1)
            pool.wait_ge(*consts.upto(0, "mask"))
            constant_rows(nc.gpsimd, SELF)
            pool.wait_ge(stacks_set[SELF], SET)
            constant_rows(nc.gpsimd, CROSS)

            def rstd_of(l, b, dve, done, mv, ve, rs):
                pool.wait_ge(*dve[l].upto(b, "aggr"))
                nc.gpsimd.tensor_tensor(ve[l][:], mv[l][:, :, 1], eps[:], ALU.add).then_inc(done[l].sem, 1)
                pool.wait_ge(*done[l].upto(b, "eps"))
                nc.gpsimd.tensor_tensor(rs[l][:], ve[l][:], half_neg[:], ALU.pow).then_inc(done[l].sem, 1)

            def prep_rest(l, b):
                pool.wait_ge(*prep_dve[l].upto(b, "part1"))
                nc.gpsimd.tensor_tensor(halves(qk_rest[l]), halves(qk[l]), qk_part[l][:, :, 0, :], ALU.subtract)\
                    .then_inc(prep_pool[l].sem, 1)

            def prep_part3(l, b):
                pool.wait_ge(*prep_dve[l].upto(b, "part2"))
                nc.gpsimd.tensor_tensor(qk_part[l][:, :, 2, :], halves(qk_rest[l]), qk_part[l][:, :, 1, :], ALU.subtract)\
                    .then_inc(prep_pool[l].sem, 1)

            def slot(i, s):
                (l, b), (ln, bn), (lo, bo), (lt, bt) = slot_tasks(i, s)
                if s == 1 and exists(i + 1):
                    prep_rest(CAUSAL, i + 1)
                    prep_part3(CAUSAL, i + 1)
                if exists(bt) and lt == SELF:
                    prep_rest(CROSS, bt)
                    prep_part3(CROSS, bt)
                if exists(bt) and lt in FFN:
                    rstd_of(lt, bt, tail_dve, tail_pool, tmean_var, tvar_eps, trstd)
                if exists(bt) and lt == CAUSAL:
                    prep_rest(SELF, bt)
                if exists(bo) and not (exists(bt) and lt == CAUSAL):
                    rstd_of(lo, bo, out_dve, out_pool, mean_var, var_eps, rstd)
                if exists(bt) and lt == CAUSAL:
                    prep_part3(SELF, bt)
                    if exists(bo):
                        rstd_of(lo, bo, out_dve, out_pool, mean_var, var_eps, rstd)

            iterations(pool, slot)


def kernel(**inputs):
    import concourse.bacc as bacc
    from concourse.bass_utils import run_bass_kernel_spmd

    a = {k: np.asarray(v) for k, v in inputs.items()}
    L0, L1 = "L0_xattn_", "L1_xattn_"
    by_dim = np.arange(D).reshape(HEADS, DK).T.reshape(-1)
    w4 = [a[L0 + "Wq"][:, by_dim], a[L0 + "Wk"][:, by_dim], a[L0 + "Wv"], a[L0 + "Wo"]]
    for n in ("sa", "ca"):
        w4 += [a[f"{L1}{n}_wq"].T[:, by_dim], a[f"{L1}{n}_wk"].T[:, by_dim], a[f"{L1}{n}_wv"].T, a[f"{L1}{n}_wo"].T]
    cols = [a[L0 + "bq"][by_dim], a[L1 + "sa_bq"][by_dim], a[L1 + "ca_bq"][by_dim],
            a[L0 + "bk"][by_dim], a[L1 + "sa_bk"][by_dim], a[L1 + "ca_bk"][by_dim],
            a[L0 + "bo"], a[L1 + "sa_bo"], a[L1 + "ca_bo"], a[L0 + "b2"], a[L1 + "ffn_b2"],
            *a[L0 + "b1"].reshape(CHUNKS, P), *a[L1 + "ffn_b1"].reshape(CHUNKS, P)]
    rows = [a[L0 + "bv"], a[L1 + "sa_bv"], a[L1 + "ca_bv"],
            a[L0 + "ln1_g"], a[L0 + "ln2_g"], a[L1 + "ln1_g"], a[L1 + "ln2_g"], a[L1 + "ln3_g"],
            a[L0 + "ln1_b"], a[L0 + "ln2_b"], a[L1 + "ln1_b"], a[L1 + "ln2_b"], a[L1 + "ln3_b"]]
    arrays = {
        "x": a["x"], "ctx": a["ctx_1024"],
        "key_mask": a["mask_Bx1x1xS2_if1"].reshape(BATCHES, TOKENS),
        "self_mask": a["mask_Bx1xSxS2_if1"].reshape(BATCHES, TOKENS, TOKENS),
        "w4": np.stack(w4), "w1": np.stack([a[L0 + "W1"], a[L1 + "ffn_w1"].T]),
        "w2": np.stack([a[L0 + "W2"], a[L1 + "ffn_w2"].T]),
        "bias_col": np.stack(cols, axis=1), "bias_row": np.stack(rows),
    }
    arrays = {k: np.ascontiguousarray(v) for k, v in arrays.items()}
    nc = bacc.Bacc("TRN2", target_bir_lowering=False, num_devices=1)
    args = [nc.dram_tensor(k, v.shape, mybir.dt.from_np(v.dtype), kind="ExternalInput").ap()
            for k, v in arrays.items()]
    out = nc.dram_tensor("out", (BATCHES, TOKENS, D), f32, kind="ExternalOutput").ap()
    mask_rows = nc.dram_tensor("mask_rows", (BATCHES, TOKENS), bf16, kind="Internal").ap()
    attention_program(nc, *args, out, mask_rows)
    r = run_bass_kernel_spmd(nc, [arrays], core_ids=[0])
    return r.results[0]["out"]
```

```python
import numpy as np
import concourse.bass as bass
from concourse import mybir
from contextlib import ExitStack

f32 = mybir.dt.float32
bf16 = mybir.dt.bfloat16
i32 = mybir.dt.int32
ALU = mybir.AluOpType
ACT = mybir.ActivationFunctionType
AX = mybir.AxisListType

BATCHES, TOKENS, D = 8, 256, 128
HEADS, DK, FF = 16, 8, 512
P = 128
TILES = TOKENS // P
CHUNKS = FF // P
PAIRS = HEADS // 2
LAYERS = 3
CAUSAL, SELF, CROSS = range(LAYERS)
EPS = 1e-5
BIG = float(2 ** 100)
SCALE = float(1 / np.sqrt(np.float32(DK)))

PRODUCTS = [(0, 0), (0, 1), (1, 0), (1, 1), (0, 2), (2, 0)]
TERMS = len(PRODUCTS)
MAX_ROW = 1 + TERMS * DK
ROWS_S = MAX_ROW
ROWS_T = MAX_ROW + 3
VW = DK + 1
VCOLS = HEADS * VW + 16

LOOP_FROM, LOOP_TO = 3, 7
STEPS = 16
UNITS = [12, 16, 16]

BQ, BK, BO = 0, 3, 6
B2, B1 = 9, 11
NCOL = B1 + 2 * CHUNKS
BV, LNG, LNB = 0, 3, 8
NROW = 13
LN_OUT = {CAUSAL: 0, SELF: 2, CROSS: 3}
LN_TAIL = {CAUSAL: 1, CROSS: 4}
FFN = {CAUSAL: 0, CROSS: 1}


class Batch:

    def __init__(self, reg, off):
        self.reg, self.off = reg, off

    def __add__(self, n):
        return Batch(self.reg, self.off + n)

    def __sub__(self, n):
        return Batch(self.reg, self.off - n)


def exists(b):
    return isinstance(b, Batch) or 0 <= b < BATCHES


def value(b, per=1, plus=0):
    if isinstance(b, Batch):
        return b.reg * per + (b.off * per + plus)
    return b * per + plus


class Signals:

    def __init__(self, sem, names, by=1):
        self.sem, self.names, self.by = sem, list(names), by

    def upto(self, b, name):
        n = len(self.names)
        return self.sem, value(b, n * self.by, (self.names.index(name) + 1) * self.by)


def slot_tasks(i, s):
    return ((s, i - s),
            (s + 1, i - s - 1) if s < 2 else (0, i + 1),
            (s - 1, i - s + 1) if s else (2, i - 3),
            (s - 2, i - s + 2) if s == 2 else (s + 1, i - s - 2))


AT = {
    "split1": [0, 0, 0], "turn1": [2, 2, 2], "pv0": [9, 9, 9],
    "split0": [8, 10, 8], "turn0": [9, 11, 9],
    "pv1": [1, 1, 1], "o0": [3, 3, 3], "o1": [5, 5, 5], "heads": [7, 7, 7], "wo": [8, 8, 8], "back": [9, 9, 9],
    "stats": [10, 10, 10], "centre": [11, 11, 11], "norm": [14, 14, 14],
    "x": [0, None, 5], "up0": [1, None, 6], "up1": [2, None, 8], "down": [4, None, 10], "t_back": [5, None, 11],
    "t_stats": [5, None, 12], "t_centre": [6, None, 13], "t_norm": [8, None, 15],
    "bias": [None, 3, None], "mask": [None, 7, None], "keep": [None, 2, 2],
    "in": [8, 9, 1], "qk": [11, 10, 3], "v": [3, 12, 5],
    "part1": [1, 10, 4], "part2": [4, 12, 8], "v_bias": [4, 13, 6],
}
MAX_STEPS = [(0, 16), (2, 16), (0, 16)]
ATTEND_STEPS = [(0, 16), (0, 16), (0, 16)]


def units(l, step, steps):
    first, last = steps[l]
    return [u for u in range(UNITS[l]) if step == first + u * (last - first) // UNITS[l]]


def unit_of(l, u):
    n = UNITS[l] // 2
    g, v = divmod(u, n)
    if l != CAUSAL:
        return v % 2, 8 * g + 2 * (v // 2), 2
    short = v % 3 == 0
    return (0, 8 * g + 4 * (v // 3), 4) if short else (1, 8 * g + 4 * (v // 3) + 2 * (v % 3 - 1), 2)


def attention_program(nc, x, ctx, key_mask, self_mask, w4, w1, w2, bias_col, bias_row, out, mask_rows):
    es = ExitStack()
    with es:
        def sb(name, shape, dt=f32):
            return es.enter_context(nc.sbuf_tensor(name, shape, dt))

        def sem(name):
            return es.enter_context(nc.semaphore(name))

        def signals(name, names, by=1):
            return Signals(sem(name), names, by)

        def per_layer(name, names, by=1):
            return [signals(f"{name}{l}", names(l) if callable(names) else names, by) for l in range(LAYERS)]

        w4_sb = sb("w4_sb", [P, 4 * LAYERS, D])
        w1_sb = sb("w1_sb", [P, 2, FF])
        w2_sb = sb("w2_sb", [P, 2, CHUNKS, D])
        col = sb("col", [P, NCOL])
        row = sb("row", [P, NROW, D])
        ident_f = sb("ident_f", [P, P])
        ident_b = sb("ident_b", [P, P], bf16)
        causal_q = sb("causal_q", [P, P], bf16)
        causal_k = sb("causal_k", [P, P], bf16)
        keep_row = sb("keep_row", [P, 1])
        half_neg = sb("half_neg", [P, TILES])
        wait_carrier = sb("wait_carrier", [P, 1])
        eps = sb("eps", [P, TILES])
        km_int = sb("km_int", [BATCHES, TOKENS], i32)
        km_bias = sb("km_bias", [BATCHES, TOKENS], bf16)

        stacks = [sb(f"stacks{l}", [ROWS_T, HEADS, 2, TOKENS], bf16) for l in range(LAYERS)]
        q_stack = [st[:, :, 0, :] for st in stacks]
        k_stack = [st[:, :, 1, :] for st in stacks]
        v_sb = [sb(f"v_sb{l}", [P, TILES, VCOLS]) for l in range(LAYERS)]
        neg_max = [sb(f"neg_max{l}", [P, TILES, HEADS]) for l in range(LAYERS)]
        max_rest = [sb(f"max_rest{l}", [P, TILES, HEADS]) for l in range(LAYERS)]
        max_part = [sb(f"max_part{l}", [P, 2, TILES, 3, 8], bf16) for l in range(LAYERS)]
        max_rows = [sb(f"max_rows{l}", [24, 2, TOKENS], bf16) for l in range(LAYERS)]
        ot_sb = [sb(f"ot_sb{l}", [P, 2, 512]) for l in range(LAYERS)]
        rsum = [sb(f"rsum{l}", [P, TILES, PAIRS, 2]) for l in range(LAYERS)]
        heads = [sb(f"heads{l}", [P, TILES, D]) for l in range(LAYERS)]
        heads_t = [sb(f"heads_t{l}", [P, TOKENS]) for l in range(LAYERS)]
        y_t = [sb(f"y_t{l}", [P, TOKENS]) for l in range(LAYERS)]
        y = [sb(f"y{l}", [P, TILES, D]) for l in range(LAYERS)]
        stats = [sb(f"stats{l}", [P, TILES, 6]) for l in range(LAYERS)]
        mean_var = [sb(f"mean_var{l}", [P, TILES, 2]) for l in range(LAYERS)]
        var_eps = [sb(f"var_eps{l}", [P, TILES]) for l in range(LAYERS)]
        rstd = [sb(f"rstd{l}", [P, TILES]) for l in range(LAYERS)]
        centred = [sb(f"centred{l}", [P, TILES, D]) for l in range(LAYERS)]
        x1 = [sb(f"x1_{l}", [P, TILES, D]) for l in range(LAYERS)]
        x2 = [sb(f"x2_{l}", [P, TILES, D]) for l in range(LAYERS)]
        resid = [sb(f"resid{l}", [P, TILES, D]) for l in range(LAYERS)]
        x1_t = [sb(f"x1_t{l}", [P, TOKENS]) for l in range(LAYERS)]
        hid_t = [sb(f"hid_t{l}", [P, CHUNKS, TOKENS]) for l in range(LAYERS)]
        z_t = [sb(f"z_t{l}", [P, TOKENS]) for l in range(LAYERS)]
        z = [sb(f"z{l}", [P, TILES, D]) for l in range(LAYERS)]
        tstats = [sb(f"tstats{l}", [P, TILES, 6]) for l in range(LAYERS)]
        tmean_var = [sb(f"tmean_var{l}", [P, TILES, 2]) for l in range(LAYERS)]
        tvar_eps = [sb(f"tvar_eps{l}", [P, TILES]) for l in range(LAYERS)]
        trstd = [sb(f"trstd{l}", [P, TILES]) for l in range(LAYERS)]
        tcentred = [sb(f"tcentred{l}", [P, TILES, D]) for l in range(LAYERS)]
        x_in = sb("x_in", [P, TILES, D])
        ctx_in = {CAUSAL: sb("ctx_in0", [P, TILES, D]), CROSS: sb("ctx_in2", [P, TILES, D])}
        in_t = [sb(f"in_t{l}", [P, 2, TOKENS]) for l in range(LAYERS)]
        qk = [sb(f"qk{l}", [P, 2 * TOKENS]) for l in range(LAYERS)]
        qk_rest = [sb(f"qk_rest{l}", [P, 2 * TOKENS]) for l in range(LAYERS)]
        qk_part = [sb(f"qk_part{l}", [P, 2, 3, TOKENS], bf16) for l in range(LAYERS)]
        sm_int = sb("sm_int", [P, TILES, TOKENS], i32)
        sm_q = sb("sm_q", [P, TILES, TOKENS], bf16)
        sm_k = sb("sm_k", [P, TILES, TOKENS], bf16)
        p_sb = sb("p_sb", [P, TILES, HEADS, TOKENS])

        bank = [es.enter_context(nc.psum_tensor(f"bank{n}", [P, 512], f32)) for n in range(8)]
        S_BANK, T_BANK = bank[0:2], bank[2:4]
        O_BANK, M_BANK, OUT_BANK, TAIL_BANK = bank[4:8]

        weights0 = sem("weights0")
        loaded = [sem(f"loaded{n}") for n in range(6)]
        consts = signals("consts", ["ident", "selects", "mask"])
        stacks_set = [sem(f"stacks_set{l}") for l in range(LAYERS)]
        made = sem("made")
        mask_saved = sem("mask_saved")
        x_loaded = sem("x_loaded")
        ctx_loaded = {CAUSAL: sem("ctx_loaded0"), CROSS: sem("ctx_loaded2")}
        resid_loaded = sem("resid_loaded")
        sm_loaded = sem("sm_loaded")
        out_stored = sem("out_stored")
        stacked = [sem(f"stacked{l}") for l in range(LAYERS)]
        STACKED = [TERMS * 16, TERMS * 16, (TERMS + 1) * 16]
        s_written = per_layer("s_written", lambda l: range(UNITS[l]))
        s_read = per_layer("s_read", lambda l: range(UNITS[l]))
        t_written = per_layer("t_written", lambda l: range(UNITS[l]))
        p_ready = per_layer("p_ready", lambda l: range(UNITS[l]))
        max_split = per_layer("max_split", [(g, n) for g in range(2) for n in ("part1", "rest", "part2", "part3")])
        max_turned = per_layer("max_turned", range(2))
        max_copied = per_layer("max_copied", range(2))
        max_in = [[signals(f"max_in{l}_{g}", ["dma"], 16) for g in range(2)] for l in range(LAYERS)]
        pv_done = per_layer("pv_done", range(2))
        o_copied = per_layer("o_copied", range(2))
        out_pe = per_layer("out_pe", ["o0", "o1", "heads", "wo", "back"])
        out_act = per_layer("out_act", ["heads", "wo"])
        out_dve = per_layer("out_dve", lambda l: ["recip0"] + ["keep0"] * (l == CAUSAL) + [
            "norm0", "recip1", "norm1", "add", "stats", "aggr", "centre0", "centre1", "norm_a", "norm_b"])
        out_pool = per_layer("out_pool", ["eps", "pow"])
        tail_pe = per_layer("tail_pe", ["x", "up0", "up1", "down", "back"])
        tail_act = per_layer("tail_act", ["x", "up0", "up1", "down"])
        tail_dve = per_layer("tail_dve", ["add", "stats", "aggr", "centre0", "centre1", "norm_a", "norm_b"])
        tail_pool = per_layer("tail_pool", ["eps", "pow"])
        prep_pe = per_layer("prep_pe", lambda l: ["mask"] * (l == SELF) + ["in", "qk", "v"])
        prep_act = per_layer("prep_act", lambda l: ["mask"] * (l == SELF) + ["in", "qk", "part1"])
        prep_dve = per_layer("prep_dve", lambda l: ["rest", "part2", "part3", "v"] if l == SELF else ["v", "part2"])
        prep_pool = per_layer("prep_pool", ["rest", "part3"])
        mask_q = signals("mask_q", ["bias"])
        resid_kept = {SELF: signals("resid_kept1", ["copy"]), CROSS: signals("resid_kept2", ["copy"])}

        def iterations(eng, slot):
            for i in range(-1, LOOP_FROM):
                for s in range(3):
                    slot(i, s)
            with eng.Fori(LOOP_FROM, LOOP_TO) as reg:
                for s in range(3):
                    slot(Batch(reg, 0), s)
            for i in range(LOOP_TO, BATCHES + LAYERS):
                for s in range(3):
                    slot(i, s)

        def constant_rows(eng, l):
            for n, (rows, is_) in enumerate(((v_sb[l][:], 1.0), (k_stack[l][32:ROWS_T], 1.0),
                                             (q_stack[l][0:1], 1.0), (k_stack[l][0:1], 0.0))):
                if n and eng is nc.gpsimd:
                    eng.wait_ge(stacks_set[l], n)
                eng.memset(rows, is_).then_inc(stacks_set[l], 1)

        SET = 4

        def starts(b):
            return not isinstance(b, Batch) and b == 0

        def halves(a):
            return a[:, :].rearrange("p (c t) -> p c t", c=2)

        def earlier_slot(i, s):
            while True:
                i, s = (i, s - 1) if s else (i - 1, 2)
                if isinstance(i, Batch):
                    return i, s
                if i < 0:
                    return None
                if exists(i - s):
                    return i, s

        block = es.enter_context(nc.Block())

        @block.sync
        def _(sp):
            def tokens(a, b):
                at = bass.ds(value(b), 1) if isinstance(b, Batch) else slice(b, b + 1)
                return a[at, :, :].rearrange("a (t p) d -> (a p) t d", p=P)

            def load_prepare0(b):
                if isinstance(b, Batch) or b > 0:
                    sp.wait_ge(*prep_pe[CAUSAL].upto(b - 1, "in"))
                sp.dma_start(x_in[:], tokens(x, b)).then_inc(x_loaded, 16)
                sp.dma_start(ctx_in[CAUSAL][:], tokens(ctx, b)).then_inc(ctx_loaded[CAUSAL], 16)

            def stack(l, b):
                if starts(b):
                    sp.wait_ge(stacks_set[l], SET)
                for part, of in (("part1", prep_act), ("part2", prep_dve), ("part3", prep_dve if l == SELF else prep_pool)):
                    sp.wait_ge(*of[l].upto(b, part))
                    n = int(part[-1]) - 1
                    if n == 0 and l == CROSS:
                        at = bass.ds(value(b), 1) if isinstance(b, Batch) else slice(b, b + 1)
                        sp.dma_start(k_stack[l][0:1, :, :],
                                     mask_rows[at, :].rearrange("(a h) k -> a h k", a=1)
                                     .broadcast_to([1, HEADS, TOKENS])).then_inc(stacked[l], 16)
                    for t, (qn, kn) in enumerate(PRODUCTS):
                        if max(qn, kn) == n:
                            flat = qk_part[l][:, :, :, :].rearrange("p c n t -> p (c n) t")
                            sp.dma_start(stacks[l][1 + DK * t:1 + DK * (t + 1), :, :, :],
                                         flat[:, qn:3 + kn + 1:3 + kn - qn, :]).then_inc(stacked[l], 16)

            def max_dma(l, b, g):
                sp.wait_ge(*max_copied[l].upto(b, g))
                sp.dma_start(q_stack[l][MAX_ROW:MAX_ROW + 3, 8 * g:8 * g + 8, :],
                             max_rows[l][:, g, :]).then_inc(max_in[l][g].sem, 16)

            def slot(i, s):
                (l, b), (ln, bn), (lo, bo), (lt, bt) = slot_tasks(i, s)
                first = not isinstance(i, Batch) and i == -1
                if not isinstance(i, Batch) and (i, s) == (0, 1):
                    sp.wait_ge(*consts.upto(0, "mask"))
                    sp.dma_start(mask_rows[:, :], km_bias[:]).then_inc(mask_saved, 16)
                    sp.wait_ge(mask_saved, 16)
                if s == 0 and exists(i + 1) and not first:
                    load_prepare0(i + 1)
                if s == 0 and exists(i):
                    sp.dma_start(resid[CAUSAL][:], tokens(x, i)).then_inc(resid_loaded, 16)
                if s == 1 and exists(i):
                    at = bass.ds(value(i), 1) if isinstance(i, Batch) else slice(i, i + 1)
                    sp.dma_start(sm_int[:], self_mask[at, :, :].rearrange("a (t p) k -> (a p) t k", p=P))\
                        .then_inc(sm_loaded, 16)
                if s == 2 and exists(i - 1):
                    if isinstance(i, Batch) or i > 1:
                        sp.wait_ge(*prep_pe[CROSS].upto(i - 2, "in"))
                    sp.dma_start(ctx_in[CROSS][:], tokens(ctx, i - 1)).then_inc(ctx_loaded[CROSS], 16)
                if exists(b):
                    max_dma(l, b, 1)
                if s == 1 and exists(i + 1):
                    stack(CAUSAL, i + 1)
                if s == 0 and exists(bt):
                    stack(CROSS, bt)
                if exists(bn):
                    max_dma(ln, bn, 0)
                if s == 1 and exists(bt):
                    sp.wait_ge(*tail_dve[CROSS].upto(bt, "norm_b"))
                    sp.dma_start(tokens(out, bt), x2[CROSS][:]).then_inc(out_stored, 16)
                if s == 2 and exists(bt):
                    stack(SELF, bt)

            load_prepare0(0)
            w4_view = w4.rearrange("n i o -> i n o")
            sp.dma_start(w4_sb[:, 0:4, :], w4_view[:, 0:4, :]).then_inc(weights0, 16)
            sp.dma_start(col[:], bias_col).then_inc(loaded[3], 16)
            sp.dma_start(row[:], bias_row.rearrange("(a n) d -> a n d", a=1).broadcast_to([P, NROW, D]))\
                .then_inc(loaded[4], 16)
            sp.dma_start(km_int[:], key_mask).then_inc(loaded[5], 16)
            sp.dma_start(w4_sb[:, 4:4 * LAYERS, :], w4_view[:, 4:4 * LAYERS, :]).then_inc(loaded[0], 16)
            sp.dma_start(w1_sb[:], w1.rearrange("n i f -> i n f")).then_inc(loaded[1], 16)
            sp.dma_start(w2_sb[:], w2.rearrange("n (c f) o -> f n c o", f=P)).then_inc(loaded[2], 16)
            iterations(sp, slot)
            sp.wait_ge(out_stored, 16 * BATCHES)

        @block.tensor
        def _(pe):
            last_read = {"o": None, "m": None, "out": None, "tail": None, "s": None}

            def bank_free(name):
                if last_read[name] is not None:
                    pe.wait_ge(*last_read[name][0].upto(*last_read[name][1:]))

            def scores(l, b, u):
                if u == 0:
                    if starts(b):
                        pe.wait_ge(stacks_set[l], SET)
                    pe.wait_ge(stacked[l], value(b, STACKED[l], STACKED[l]))
                    if l == SELF:
                        pe.wait_ge(*mask_q.upto(b, "bias"))
                if u >= 2:
                    pe.wait_ge(*s_read[l].upto(b, u - 2))
                elif last_read["s"] is not None:
                    lp, bp = last_read["s"]
                    pe.wait_ge(*s_read[lp].upto(bp, UNITS[lp] - 2 + u))
                qt, h0, n = unit_of(l, u)
                keys = TOKENS if n == 2 else P
                dst = S_BANK[u % 2]
                if l == SELF:
                    nc.tensor.matmul(dst[:, :], ident_b[:], sm_q[:, qt:qt + 1, :].broadcast_to([P, 2, TOKENS]),
                                     start=True, stop=False)
                if l == CAUSAL:
                    nc.tensor.matmul(dst[:, :].rearrange("p (h k) -> p h k", h=n)[:, :, keys - P:keys],
                                     ident_b[:], causal_q[:, :].rearrange("p (a k) -> p a k", a=1)
                                     .broadcast_to([P, n, P]), start=True, stop=False, skip_group_check=True)
                for e in range(n):
                    mm = nc.tensor.matmul(dst[:, e * keys:(e + 1) * keys],
                                          q_stack[l][0:ROWS_S, h0 + e, qt * P:(qt + 1) * P],
                                          k_stack[l][0:ROWS_S, h0 + e, 0:keys],
                                          start=(l == CROSS), stop=(l == CROSS or e == n - 1),
                                          skip_group_check=(l == CAUSAL))
                mm.then_inc(s_written[l].sem, 1)
                if u == UNITS[l] - 1:
                    last_read["s"] = (l, b)

            def scores_t(l, b, u, i, s):
                n = UNITS[l]
                if u % (n // 2) == 0:
                    pe.wait_ge(*max_in[l][u // (n // 2)].upto(b, "dma"))
                if u == 0 and l == SELF:
                    pe.wait_ge(*prep_act[SELF].upto(b, "mask"))
                if u >= 2:
                    pe.wait_ge(*p_ready[l].upto(b, u - 2))
                elif (before := earlier_slot(i, s)) is not None:
                    lp, bp = before[1], before[0] - before[1]
                    pe.wait_ge(*p_ready[lp].upto(bp, UNITS[lp] - 2 + u))
                kt, h0, n = unit_of(l, u)
                if l == CAUSAL:
                    kt = 1 - kt
                q0 = P if n == 4 else 0
                qs = TOKENS - q0
                dst = T_BANK[u % 2]
                if l == SELF:
                    nc.tensor.matmul(dst[:, :], ident_b[:], sm_k[:, kt:kt + 1, :].broadcast_to([P, 2, TOKENS]),
                                     start=True, stop=False)
                if l == CAUSAL:
                    nc.tensor.matmul(dst[:, :].rearrange("p (h q) -> p h q", h=n)[:, :, 0:P],
                                     ident_b[:], causal_k[:, :].rearrange("p (a k) -> p a k", a=1)
                                     .broadcast_to([P, n, P]), start=True, stop=False, skip_group_check=True)
                for e in range(n):
                    mm = nc.tensor.matmul(dst[:, e * qs:(e + 1) * qs],
                                          k_stack[l][0:ROWS_T, h0 + e, kt * P:(kt + 1) * P],
                                          q_stack[l][0:ROWS_T, h0 + e, q0:TOKENS],
                                          start=(l == CROSS), stop=(l == CROSS or e == n - 1),
                                          skip_group_check=(l == CAUSAL))
                mm.then_inc(t_written[l].sem, 1)

            def turn_max(l, b, g):
                bank_free("m")
                pe.wait_ge(*max_split[l].upto(b, (g, "part3")))
                for qt in range(TILES):
                    mm = nc.tensor.transpose(M_BANK[0:24, :].bitcast(bf16)[:, qt * P:(qt + 1) * P],
                                             max_part[l][:, g, qt, :, :].rearrange("p c h -> p (c h)"), ident_b[:])
                mm.then_inc(max_turned[l].sem, 1)
                last_read["m"] = (max_copied[l], b, g)

            def pv(l, b, g, kt):
                if kt == 0:
                    bank_free("o")
                    if g == 0:
                        pe.wait_ge(*prep_dve[l].upto(b, "v"))
                    pe.wait_ge(*p_ready[l].upto(b, (g + 1) * UNITS[l] // 2 - 1))
                for j in range(4):
                    pair = 4 * g + j
                    q0 = P if (kt == 1 and l == CAUSAL) else 0
                    mm = nc.tensor.matmul(
                        O_BANK[32 * j:32 * j + 32, :].rearrange("p (e q) -> p e q", e=2)[:, :, q0:TOKENS],
                        v_sb[l][:, kt, 2 * VW * pair:2 * VW * pair + 32],
                        p_sb[:, kt, 2 * pair:2 * pair + 2, q0:TOKENS],
                        start=(kt == 0), stop=(kt == 1), skip_group_check=True)
                if kt == 1:
                    mm.then_inc(pv_done[l].sem, 1)
                    last_read["o"] = (o_copied[l], b, g)

            def out_turn_o(l, b, qt):
                bank_free("out")
                pe.wait_ge(*o_copied[l].upto(b, 1))
                for g in range(2):
                    for e in range(2):
                        mm = nc.tensor.transpose(OUT_BANK[:, 256 * e + P * g:256 * e + P * (g + 1)],
                                                 ot_sb[l][:, g, e * TOKENS + qt * P:e * TOKENS + (qt + 1) * P],
                                                 ident_f[:])
                mm.then_inc(out_pe[l].sem, 1)
                last_read["out"] = (out_dve[l], b, f"norm{qt}")

            def two_turns(dst, src):
                for t in range(TILES):
                    mm = nc.tensor.transpose(dst[:, t * P:(t + 1) * P], src(t), ident_f[:])
                return mm

            def out_heads(l, b):
                bank_free("out")
                two_turns(OUT_BANK, lambda t: heads[l][:, t, :]).then_inc(out_pe[l].sem, 1)
                last_read["out"] = (out_act[l], b, "heads")

            def out_wo(l, b):
                bank_free("out")
                nc.tensor.matmul(OUT_BANK[:, 0:TOKENS], w4_sb[:, 4 * l + 3, :], heads_t[l][:],
                                 start=True, stop=True).then_inc(out_pe[l].sem, 1)
                last_read["out"] = (out_act[l], b, "wo")

            def out_back(l, b):
                bank_free("out")
                two_turns(OUT_BANK, lambda t: y_t[l][:, t * P:(t + 1) * P]).then_inc(out_pe[l].sem, 1)
                last_read["out"] = (out_dve[l], b, "add")

            def tail_x(l, b):
                bank_free("tail")
                pe.wait_ge(*out_dve[l].upto(b, "norm_b"))
                two_turns(TAIL_BANK, lambda t: x1[l][:, t, :]).then_inc(tail_pe[l].sem, 1)
                last_read["tail"] = (tail_act[l], b, "x")

            def tail_up(l, b, n):
                bank_free("tail")
                for c in range(2):
                    mm = nc.tensor.matmul(TAIL_BANK[:, c * TOKENS:(c + 1) * TOKENS],
                                          w1_sb[:, FFN[l], (2 * n + c) * P:(2 * n + c + 1) * P], x1_t[l][:],
                                          start=True, stop=True)
                mm.then_inc(tail_pe[l].sem, 1)
                last_read["tail"] = (tail_act[l], b, f"up{n}")

            def tail_down(l, b):
                bank_free("tail")
                for c in range(CHUNKS):
                    mm = nc.tensor.matmul(TAIL_BANK[:, 0:TOKENS], w2_sb[:, FFN[l], c, :], hid_t[l][:, c, :],
                                          start=(c == 0), stop=(c == CHUNKS - 1))
                mm.then_inc(tail_pe[l].sem, 1)
                last_read["tail"] = (tail_act[l], b, "down")

            def tail_back(l, b):
                bank_free("tail")
                two_turns(TAIL_BANK, lambda t: z_t[l][:, t * P:(t + 1) * P]).then_inc(tail_pe[l].sem, 1)
                last_read["tail"] = (tail_dve[l], b, "add")

            def prep_in(l, b):
                bank_free("tail")
                if l == CAUSAL:
                    pe.wait_ge(x_loaded, value(b, 16, 16))
                    src = x_in
                elif l == SELF:
                    pe.wait_ge(*tail_dve[CAUSAL].upto(b, "norm_b"))
                    src = x2[CAUSAL]
                else:
                    pe.wait_ge(*out_dve[SELF].upto(b, "norm_b"))
                    src = x1[SELF]
                mm = two_turns(TAIL_BANK, lambda t: src[:, t, :])
                if l != SELF:
                    pe.wait_ge(ctx_loaded[l], value(b, 16, 16))
                    mm = two_turns(TAIL_BANK[:, TOKENS:2 * TOKENS], lambda t: ctx_in[l][:, t, :])
                mm.then_inc(prep_pe[l].sem, 1)
                last_read["tail"] = (prep_act[l], b, "in")

            def prep_qk(l, b):
                bank_free("tail")
                for c in range(2):
                    mm = nc.tensor.matmul(TAIL_BANK[:, c * TOKENS:(c + 1) * TOKENS], w4_sb[:, 4 * l + c, :],
                                          in_t[l][:, 0 if l == SELF else c, :], start=True, stop=True)
                mm.then_inc(prep_pe[l].sem, 1)
                last_read["tail"] = (prep_act[l], b, "qk")

            def prep_v(l, b):
                bank_free("tail")
                kv = 0 if l == SELF else 1
                for kt in range(TILES):
                    mm = nc.tensor.matmul(TAIL_BANK[:, kt * D:(kt + 1) * D], in_t[l][:, kv, kt * P:(kt + 1) * P],
                                          w4_sb[:, 4 * l + 2, :], start=True, stop=True)
                mm.then_inc(prep_pe[l].sem, 1)
                last_read["tail"] = (prep_dve[l], b, "v")

            def prep_mask(b):
                bank_free("tail")
                pe.wait_ge(*mask_q.upto(b, "bias"))
                for kt in range(TILES):
                    for qt in range(TILES):
                        mm = nc.tensor.transpose(
                            TAIL_BANK[:, :].bitcast(bf16)[:, kt * TOKENS + qt * P:kt * TOKENS + (qt + 1) * P],
                            sm_q[:, qt, kt * P:(kt + 1) * P], ident_b[:])
                mm.then_inc(prep_pe[SELF].sem, 1)
                last_read["tail"] = (prep_act[SELF], b, "mask")

            def slot(i, s):
                (l, b), (ln, bn), (lo, bo), (lt, bt) = slot_tasks(i, s)
                if not isinstance(i, Batch) and (i, s) == (-1, 2):
                    pe.wait_ge(*consts.upto(0, "selects"))
                if not isinstance(i, Batch) and (i, s) == (0, 2):
                    for n in range(3):
                        pe.wait_ge(loaded[n], 16)
                for t in range(STEPS):
                    if exists(b):
                        if t == AT["turn1"][l]:
                            turn_max(l, b, 1)
                        if t in (AT["pv0"][l], AT["pv0"][l] + 1):
                            pv(l, b, 0, t - AT["pv0"][l])
                    if exists(bn) and t == AT["turn0"][ln]:
                        turn_max(ln, bn, 0)
                    if exists(bo):
                        if t in (AT["pv1"][lo], AT["pv1"][lo] + 1):
                            pv(lo, bo, 1, t - AT["pv1"][lo])
                        if t == AT["o0"][lo]:
                            out_turn_o(lo, bo, 0)
                        if t == AT["o1"][lo]:
                            out_turn_o(lo, bo, 1)
                        if t == AT["heads"][lo]:
                            out_heads(lo, bo)
                        if t == AT["wo"][lo]:
                            out_wo(lo, bo)
                        if t == AT["back"][lo]:
                            out_back(lo, bo)
                    if exists(bt) and lt in FFN:
                        if t == AT["x"][lt]:
                            tail_x(lt, bt)
                        if t == AT["up0"][lt]:
                            tail_up(lt, bt, 0)
                        if t == AT["up1"][lt]:
                            tail_up(lt, bt, 1)
                        if t == AT["down"][lt]:
                            tail_down(lt, bt)
                        if t == AT["t_back"][lt]:
                            tail_back(lt, bt)
                    if s != 1 and exists(bt):
                        lp = lt + 1
                        if t == AT["mask"][lp]:
                            prep_mask(bt)
                        if t == AT["in"][lp]:
                            prep_in(lp, bt)
                        if t == AT["qk"][lp]:
                            prep_qk(lp, bt)
                        if t == AT["v"][lp]:
                            prep_v(lp, bt)
                    if exists(i + 1):
                        if s == 0 and t == AT["in"][CAUSAL]:
                            prep_in(CAUSAL, i + 1)
                        if s == 0 and t == AT["qk"][CAUSAL]:
                            prep_qk(CAUSAL, i + 1)
                        if s == 1 and t == AT["v"][CAUSAL]:
                            prep_v(CAUSAL, i + 1)
                    if exists(b):
                        for u in units(l, t, ATTEND_STEPS):
                            scores_t(l, b, u, i, s)
                    if exists(bn):
                        for u in units(ln, t, MAX_STEPS):
                            scores(ln, bn, u)

            pe.wait_ge(weights0, 16)
            pe.wait_ge(*consts.upto(0, "ident"))

            def looping(eng, slot):
                for i in range(-1, LOOP_FROM):
                    for s in range(3):
                        slot(i, s)
                with eng.Fori(LOOP_FROM, LOOP_TO) as reg:
                    for k, v in last_read.items():
                        last_read[k] = (v[0], Batch(reg, v[1] - LOOP_FROM), *v[2:])
                    before = dict(last_read)
                    for s in range(3):
                        slot(Batch(reg, 0), s)
                    for k, v in last_read.items():
                        assert (v[0], v[1].off, *v[2:]) == (before[k][0], before[k][1].off + 1, *before[k][2:])
                for k, v in last_read.items():
                    last_read[k] = (v[0], v[1].off + LOOP_TO - 1, *v[2:])
                for i in range(LOOP_TO, BATCHES + LAYERS):
                    for s in range(3):
                        slot(i, s)
            looping(pe, slot)

        @block.scalar
        def _(act):
            def exps(l, b, u, i, s):
                n = UNITS[l] // 2
                if u % n == 0 and (before := earlier_slot(i, s)) is not None:
                    act.wait_ge(*pv_done[before[1]].upto(before[0] - before[1], u // n))
                act.wait_ge(*t_written[l].upto(b, u))
                kt, h0, nh = unit_of(l, u)
                if l == CAUSAL:
                    kt = 1 - kt
                q0 = P if nh == 4 else 0
                nc.scalar.activation(p_sb[:, kt, h0:h0 + nh, q0:TOKENS],
                                     T_BANK[u % 2][:, :].rearrange("p (h q) -> p h q", h=nh),
                                     ACT.Exp, scale=SCALE).then_inc(p_ready[l].sem, 1)

            def copy_max(l, b, g):
                act.wait_ge(*max_turned[l].upto(b, g))
                nc.scalar.activation(max_rows[l][:, g, :], M_BANK[0:24, :].bitcast(bf16)[:, 0:TOKENS], ACT.Copy)\
                    .then_inc(max_copied[l].sem, 1)

            def copy_o(l, b, g):
                act.wait_ge(*pv_done[l].upto(b, g))
                nc.scalar.activation(ot_sb[l][:, g, :], O_BANK[:, :], ACT.Copy).then_inc(o_copied[l].sem, 1)

            def out_heads(l, b):
                act.wait_ge(*out_pe[l].upto(b, "heads"))
                nc.scalar.activation(heads_t[l][:], OUT_BANK[:, 0:TOKENS], ACT.Copy).then_inc(out_act[l].sem, 1)

            def out_wo(l, b):
                act.wait_ge(*out_pe[l].upto(b, "wo"))
                nc.scalar.activation(y_t[l][:], OUT_BANK[:, 0:TOKENS], ACT.Identity,
                                     bias=col[:, BO + l:BO + l + 1]).then_inc(out_act[l].sem, 1)

            def tail_x(l, b):
                act.wait_ge(*tail_pe[l].upto(b, "x"))
                nc.scalar.activation(x1_t[l][:], TAIL_BANK[:, 0:TOKENS], ACT.Copy).then_inc(tail_act[l].sem, 1)

            def tail_up(l, b, n):
                act.wait_ge(*tail_pe[l].upto(b, f"up{n}"))
                for c in range(2):
                    at = B1 + FFN[l] * CHUNKS + 2 * n + c
                    ins = nc.scalar.activation(hid_t[l][:, 2 * n + c, :], TAIL_BANK[:, c * TOKENS:(c + 1) * TOKENS],
                                               ACT.Relu, bias=col[:, at:at + 1])
                ins.then_inc(tail_act[l].sem, 1)

            def tail_down(l, b):
                act.wait_ge(*tail_pe[l].upto(b, "down"))
                nc.scalar.activation(z_t[l][:], TAIL_BANK[:, 0:TOKENS], ACT.Identity,
                                     bias=col[:, B2 + FFN[l]:B2 + FFN[l] + 1]).then_inc(tail_act[l].sem, 1)

            def prep_in(l, b):
                act.wait_ge(*prep_pe[l].upto(b, "in"))
                n = 1 if l == SELF else 2
                nc.scalar.activation(in_t[l][:, 0:n, :].rearrange("p a t -> p (a t)"), TAIL_BANK[:, 0:n * TOKENS],
                                     ACT.Copy).then_inc(prep_act[l].sem, 1)

            def prep_qk(l, b):
                act.wait_ge(*prep_pe[l].upto(b, "qk"))
                for c, at in ((0, BQ + l), (1, BK + l)):
                    ins = nc.scalar.activation(qk[l][:, c * TOKENS:(c + 1) * TOKENS],
                                               TAIL_BANK[:, c * TOKENS:(c + 1) * TOKENS], ACT.Identity,
                                               bias=col[:, at:at + 1])
                ins.then_inc(prep_act[l].sem, 1)

            def prep_part1(l, b):
                if isinstance(b, Batch) or b > 0:
                    act.wait_ge(*t_written[l].upto(b - 1, UNITS[l] - 1))
                    act.wait_ge(stacked[l], value(b, STACKED[l]))
                act.wait_ge(*prep_act[l].upto(b, "qk"))
                nc.scalar.activation(qk_part[l][:, :, 0, :], halves(qk[l]), ACT.Copy).then_inc(prep_act[l].sem, 1)

            def prep_mask(b):
                act.wait_ge(*prep_pe[SELF].upto(b, "mask"))
                nc.scalar.activation(sm_k[:, :, :].rearrange("p t q -> p (t q)"),
                                     TAIL_BANK[:, :].bitcast(bf16)[:, 0:2 * TOKENS], ACT.Copy)\
                    .then_inc(prep_act[SELF].sem, 1)

            def slot(i, s):
                (l, b), (ln, bn), (lo, bo), (lt, bt) = slot_tasks(i, s)
                for t in range(STEPS):
                    if exists(b):
                        if t == AT["turn1"][l]:
                            copy_max(l, b, 1)
                        if t == AT["pv0"][l] + 1:
                            copy_o(l, b, 0)
                    if exists(bn) and t == AT["turn0"][ln]:
                        copy_max(ln, bn, 0)
                    if exists(bo):
                        if t == AT["pv1"][lo] + 1:
                            copy_o(lo, bo, 1)
                        if t == AT["heads"][lo]:
                            out_heads(lo, bo)
                        if t == AT["wo"][lo]:
                            out_wo(lo, bo)
                    if exists(bt) and lt in FFN:
                        if t == AT["x"][lt]:
                            tail_x(lt, bt)
                        if t == AT["up0"][lt]:
                            tail_up(lt, bt, 0)
                        if t == AT["up1"][lt]:
                            tail_up(lt, bt, 1)
                        if t == AT["down"][lt]:
                            tail_down(lt, bt)
                    if s != 1 and exists(bt):
                        lp = lt + 1
                        if t == AT["mask"][lp]:
                            prep_mask(bt)
                        if t == AT["in"][lp]:
                            prep_in(lp, bt)
                        if t == AT["qk"][lp]:
                            prep_qk(lp, bt)
                        if t == AT["part1"][lp]:
                            prep_part1(lp, bt)
                    if exists(i + 1):
                        if s == 0 and t == AT["in"][CAUSAL]:
                            prep_in(CAUSAL, i + 1)
                        if s == 0 and t == AT["qk"][CAUSAL]:
                            prep_qk(CAUSAL, i + 1)
                        if s == 1 and t == AT["part1"][CAUSAL]:
                            prep_part1(CAUSAL, i + 1)
                    if exists(b):
                        for u in units(l, t, ATTEND_STEPS):
                            exps(l, b, u, i, s)

            act.wait_ge(loaded[3], 16)
            iterations(act, slot)

        @block.vector
        def _(dve):
            def reduce_unit(l, b, u):
                dve.wait_ge(*s_written[l].upto(b, u))
                qt, h0, n = unit_of(l, u)
                nc.vector.tensor_reduce(neg_max[l][:, qt, h0:h0 + n],
                                        S_BANK[u % 2][:, :].rearrange("p (h k) -> p h k", h=n),
                                        axis=AX.X, op=ALU.max, negate=True).then_inc(s_read[l].sem, 1)

            def split_max(l, b, g):
                src = neg_max[l][:, :, 8 * g:8 * g + 8]
                rest = max_rest[l][:, :, 8 * g:8 * g + 8]
                part = max_part[l][:, g, :, :, :]
                dve.wait_ge(*s_read[l].upto(b, (g + 1) * UNITS[l] // 2 - 1))
                nc.vector.tensor_copy(part[:, :, 0, :], src).then_inc(max_split[l].sem, 1)
                dve.wait_ge(*max_split[l].upto(b, (g, "part1")))
                nc.vector.tensor_tensor(rest, src, part[:, :, 0, :], ALU.subtract).then_inc(max_split[l].sem, 1)
                dve.wait_ge(*max_split[l].upto(b, (g, "rest")))
                nc.vector.tensor_copy(part[:, :, 1, :], rest).then_inc(max_split[l].sem, 1)
                dve.wait_ge(*max_split[l].upto(b, (g, "part2")))
                nc.vector.tensor_tensor(part[:, :, 2, :], rest, part[:, :, 1, :], ALU.subtract)\
                    .then_inc(max_split[l].sem, 1)

            def out_norm(l, b, qt):
                done = out_dve[l]
                dve.wait_ge(*out_pe[l].upto(b, f"o{qt}"))
                sums = bass.AP(OUT_BANK, DK, [[512, P], [32, PAIRS], [256 + VW, 2]])
                vals = bass.AP(OUT_BANK, 0, [[512, P], [32, PAIRS], [256 + VW, 2], [1, DK]])
                nc.vector.reciprocal(rsum[l][:, qt, :, :], sums).then_inc(done.sem, 1)
                dve.wait_ge(*done.upto(b, f"recip{qt}"))
                if qt == 0:
                    if l == CAUSAL:
                        nc.vector.tensor_scalar(rsum[l][:, 0, :, :], rsum[l][:, 0, :, :], keep_row[:, 0:1], None,
                                                ALU.mult).then_inc(done.sem, 1)
                        dve.wait_ge(*done.upto(b, "keep0"))
                r = rsum[l][:, qt, :, :].rearrange("p (a b) (e c) -> p (a b) e c", a=1, c=1)\
                    .broadcast_to([P, PAIRS, 2, DK])
                nc.vector.tensor_tensor(heads[l][:, qt, :].rearrange("p (a e d) -> p a e d", e=2, d=DK), vals, r,
                                        ALU.mult).then_inc(done.sem, 1)

            def layer_norm(part, l, b, done, psum, res, y, st, mv, cen, ln):
                if part == "add":
                    nc.vector.tensor_tensor(y[l][:].rearrange("p t d -> p (t d)"), psum[:, 0:TOKENS],
                                            res[:].rearrange("p t d -> p (t d)"), ALU.add).then_inc(done.sem, 1)
                if part == "stats":
                    dve.wait_ge(*done.upto(b, "add"))
                    nc.vector.bn_stats(st[l][:, 0, :], y[l][:, 0, :])
                    nc.vector.bn_stats(st[l][:, 1, :], y[l][:, 1, :]).then_inc(done.sem, 1)
                if part == "centre":
                    dve.wait_ge(*done.upto(b, "stats"))
                    nc.vector.memset(wait_carrier[:], 0.0)
                    nc.vector.bn_aggr(mv[l][:, 0, :], st[l][:, 0, :])
                    nc.vector.bn_aggr(mv[l][:, 1, :], st[l][:, 1, :]).then_inc(done.sem, 1)
                    dve.wait_ge(*done.upto(b, "aggr"))
                    for t in range(TILES):
                        nc.vector.scalar_tensor_tensor(out=cen[l][:, t, :], in0=y[l][:, t, :], scalar=mv[l][:, t, 0:1],
                                                       in1=row[:, LNG + ln, :], op0=ALU.subtract, op1=ALU.mult)\
                            .then_inc(done.sem, 1)

            def layer_norm_end(l, b, done, pool, rs, cen, ln, dst):
                dve.wait_ge(*pool[l].upto(b, "pow"))
                dve.wait_ge(*done.upto(b, "centre1"))
                for t in range(TILES):
                    nc.vector.scalar_tensor_tensor(out=dst[l][:, t, :], in0=cen[l][:, t, :], scalar=rs[l][:, t:t + 1],
                                                   in1=row[:, LNB + ln, :], op0=ALU.mult, op1=ALU.add)\
                        .then_inc(done.sem, 1)

            def out_ln(part, l, b):
                if part == "add":
                    dve.wait_ge(*out_pe[l].upto(b, "back"))
                    if l == CAUSAL:
                        dve.wait_ge(resid_loaded, value(b, 16, 16))
                    else:
                        dve.wait_ge(*resid_kept[l].upto(b, "copy"))
                layer_norm(part, l, b, out_dve[l], OUT_BANK, resid[l], y, stats, mean_var, centred, LN_OUT[l])

            def out_ln_end(l, b):
                if l == SELF and (isinstance(b, Batch) or b > 0):
                    dve.wait_ge(*resid_kept[CROSS].upto(b - 1, "copy"))
                layer_norm_end(l, b, out_dve[l], out_pool, rstd, centred, LN_OUT[l], x1)

            def tail_ln(part, l, b):
                if part == "add":
                    dve.wait_ge(*tail_pe[l].upto(b, "back"))
                layer_norm(part, l, b, tail_dve[l], TAIL_BANK, x1[l], z, tstats, tmean_var, tcentred, LN_TAIL[l])

            def tail_ln_end(l, b):
                if l == CROSS and (isinstance(b, Batch) or b > 0):
                    dve.wait_ge(out_stored, value(b, 16))
                if l == CAUSAL and (isinstance(b, Batch) or b > 0):
                    dve.wait_ge(*resid_kept[SELF].upto(b - 1, "copy"))
                layer_norm_end(l, b, tail_dve[l], tail_pool, trstd, tcentred, LN_TAIL[l], x2)

            def prep_v(l, b):
                if starts(b):
                    dve.wait_ge(stacks_set[l], SET)
                dve.wait_ge(*prep_pe[l].upto(b, "v"))
                nc.vector.tensor_tensor(
                    v_sb[l][:, :, 0:HEADS * VW].rearrange("p t (h w) -> p t h w", w=VW)[:, :, :, 0:DK],
                    TAIL_BANK[:, 0:TILES * D].rearrange("p (t h d) -> p t h d", t=TILES, d=DK),
                    row[:, BV + l:BV + l + 1, :].rearrange("p a (h d) -> p a h d", d=DK)
                    .broadcast_to([P, TILES, HEADS, DK]), ALU.add).then_inc(prep_dve[l].sem, 1)

            def prep_part2(l, b):
                of = prep_dve if l == SELF else prep_pool
                dve.wait_ge(*of[l].upto(b, "rest"))
                nc.vector.tensor_copy(qk_part[l][:, :, 1, :], halves(qk_rest[l])).then_inc(prep_dve[l].sem, 1)

            def prep_rest(l, b):
                dve.wait_ge(*prep_act[l].upto(b, "part1"))
                nc.vector.tensor_tensor(halves(qk_rest[l]), halves(qk[l]), qk_part[l][:, :, 0, :], ALU.subtract)\
                    .then_inc(prep_dve[l].sem, 1)

            def prep_part3(l, b):
                dve.wait_ge(*prep_dve[l].upto(b, "part2"))
                nc.vector.tensor_tensor(qk_part[l][:, :, 2, :], halves(qk_rest[l]), qk_part[l][:, :, 1, :], ALU.subtract)\
                    .then_inc(prep_dve[l].sem, 1)

            def keep_residual(l, b, src, src_done):
                if isinstance(b, Batch) or b > 0:
                    dve.wait_ge(*out_dve[l].upto(b - 1, "add"))
                dve.wait_ge(*src_done.upto(b, "norm_b"))
                nc.vector.tensor_copy(resid[l][:], src[:]).then_inc(resid_kept[l].sem, 1)

            def mask_bias(b):
                if isinstance(b, Batch) or b > 0:
                    dve.wait_ge(*s_written[SELF].upto(b - 1, UNITS[SELF] - 1))
                    dve.wait_ge(*prep_pe[SELF].upto(b - 1, "mask"))
                dve.wait_ge(sm_loaded, value(b, 16, 16))
                nc.vector.tensor_scalar(sm_q[:].rearrange("p t k -> p (t k)"),
                                        sm_int[:].rearrange("p t k -> p (t k)"), 0.0, -BIG,
                                        ALU.is_equal, ALU.mult).then_inc(mask_q.sem, 1)

            def slot(i, s):
                (l, b), (ln, bn), (lo, bo), (lt, bt) = slot_tasks(i, s)
                for t in range(STEPS):
                    if t == AT["keep"][SELF] and s == 0 and exists(i - 1):
                        keep_residual(SELF, i - 1, x2[CAUSAL], tail_dve[CAUSAL])
                    if t == AT["keep"][CROSS] and s == 1 and exists(i - 2):
                        keep_residual(CROSS, i - 2, x1[SELF], out_dve[SELF])
                    if t == AT["bias"][SELF] and s == 2 and exists(i):
                        mask_bias(i)
                    if t == AT["split1"][l] and exists(b):
                        split_max(l, b, 1)
                    if t == AT["split0"][ln] and exists(bn):
                        split_max(ln, bn, 0)
                    if exists(bo):
                        if t == AT["o0"][lo]:
                            out_norm(lo, bo, 0)
                        if t == AT["o1"][lo]:
                            out_norm(lo, bo, 1)
                        if t == AT["back"][lo]:
                            out_ln("add", lo, bo)
                        if t == AT["stats"][lo]:
                            out_ln("stats", lo, bo)
                        if t == AT["centre"][lo]:
                            out_ln("centre", lo, bo)
                        if t == AT["norm"][lo]:
                            out_ln_end(lo, bo)
                    if exists(bt) and lt in FFN:
                        if t == AT["t_back"][lt]:
                            tail_ln("add", lt, bt)
                        if t == AT["t_stats"][lt]:
                            tail_ln("stats", lt, bt)
                        if t == AT["t_centre"][lt]:
                            tail_ln("centre", lt, bt)
                        if t == AT["t_norm"][lt]:
                            tail_ln_end(lt, bt)
                    if exists(bt) and lt == CAUSAL:
                        if t == AT["part1"][SELF] + 1:
                            prep_rest(SELF, bt)
                        if t == AT["part2"][SELF]:
                            prep_part2(SELF, bt)
                            prep_part3(SELF, bt)
                        if t == AT["v_bias"][SELF]:
                            prep_v(SELF, bt)
                    if exists(bt) and lt == SELF:
                        if t == AT["v_bias"][CROSS]:
                            prep_v(CROSS, bt)
                        if t == AT["part2"][CROSS]:
                            prep_part2(CROSS, bt)
                    if s == 1 and exists(i + 1):
                        if t == AT["v_bias"][CAUSAL]:
                            prep_v(CAUSAL, i + 1)
                        if t == AT["part2"][CAUSAL]:
                            prep_part2(CAUSAL, i + 1)
                    if exists(bn):
                        for u in units(ln, t, MAX_STEPS):
                            reduce_unit(ln, bn, u)

            constant_rows(nc.vector, CAUSAL)
            dve.wait_ge(loaded[4], 16)
            dve.wait_ge(*consts.upto(0, "selects"))
            iterations(dve, slot)

        @block.gpsimd
        def _(pool):
            nc.gpsimd.memset(ident_f[:], 0.0).then_inc(made, 1)
            pool.wait_ge(made, 1)
            nc.gpsimd.affine_select(out=ident_f[:], in_=ident_f[:], compare_op=ALU.not_equal, fill=1.0, base=0,
                                    pattern=[[-1, P]], channel_multiplier=1).then_inc(consts.sem, 1)
            nc.gpsimd.memset(ident_b[:], 0.0).then_inc(made, 1)
            nc.gpsimd.memset(causal_q[:], 0.0).then_inc(made, 1)
            nc.gpsimd.memset(causal_k[:], 0.0).then_inc(made, 1)
            nc.gpsimd.memset(keep_row[:], 1.0).then_inc(made, 1)
            nc.gpsimd.memset(half_neg[:], -0.5).then_inc(made, 1)
            nc.gpsimd.memset(eps[:], EPS).then_inc(made, 1)
            pool.wait_ge(made, 7)
            nc.gpsimd.affine_select(out=ident_b[:], in_=ident_b[:], compare_op=ALU.not_equal, fill=1.0, base=0,
                                    pattern=[[-1, P]], channel_multiplier=1).then_inc(made, 1)
            nc.gpsimd.affine_select(out=causal_q[:], in_=causal_q[:], compare_op=ALU.is_gt, fill=-BIG, base=0,
                                    pattern=[[-1, P]], channel_multiplier=1).then_inc(made, 1)
            nc.gpsimd.affine_select(out=causal_k[:], in_=causal_k[:], compare_op=ALU.is_gt, fill=-BIG, base=0,
                                    pattern=[[1, P]], channel_multiplier=-1).then_inc(made, 1)
            pool.wait_ge(made, 10)
            pool.wait_ge(*consts.upto(0, "ident"))
            nc.gpsimd.affine_select(out=keep_row[:], in_=keep_row[:], compare_op=ALU.is_gt, fill=0.0, base=0,
                                    pattern=[[0, 1]], channel_multiplier=1).then_inc(consts.sem, 1)

            def other_layers():
                pool.wait_ge(loaded[5], 16)
                nc.gpsimd.tensor_scalar(km_bias[:], km_int[:], 0.0, -BIG, ALU.is_equal, ALU.mult)\
                    .then_inc(consts.sem, 1)
                pool.wait_ge(*consts.upto(0, "mask"))
                constant_rows(nc.gpsimd, SELF)
                pool.wait_ge(stacks_set[SELF], SET)
                constant_rows(nc.gpsimd, CROSS)

            def rstd_of(l, b, dve, done, mv, ve, rs):
                pool.wait_ge(*dve[l].upto(b, "aggr"))
                nc.gpsimd.tensor_tensor(ve[l][:], mv[l][:, :, 1], eps[:], ALU.add).then_inc(done[l].sem, 1)
                pool.wait_ge(*done[l].upto(b, "eps"))
                nc.gpsimd.tensor_tensor(rs[l][:], ve[l][:], half_neg[:], ALU.pow).then_inc(done[l].sem, 1)

            def prep_rest(l, b):
                pool.wait_ge(*prep_act[l].upto(b, "part1"))
                nc.gpsimd.tensor_tensor(halves(qk_rest[l]), halves(qk[l]), qk_part[l][:, :, 0, :], ALU.subtract)\
                    .then_inc(prep_pool[l].sem, 1)

            def prep_part3(l, b):
                pool.wait_ge(*prep_dve[l].upto(b, "part2"))
                nc.gpsimd.tensor_tensor(qk_part[l][:, :, 2, :], halves(qk_rest[l]), qk_part[l][:, :, 1, :], ALU.subtract)\
                    .then_inc(prep_pool[l].sem, 1)

            def slot(i, s):
                (l, b), (ln, bn), (lo, bo), (lt, bt) = slot_tasks(i, s)
                if not isinstance(i, Batch) and (i, s) == (-1, 2):
                    other_layers()
                if s == 1 and exists(i + 1):
                    prep_rest(CAUSAL, i + 1)
                    prep_part3(CAUSAL, i + 1)
                if exists(bt) and lt == SELF:
                    prep_rest(CROSS, bt)
                    prep_part3(CROSS, bt)
                if exists(bt) and lt == CAUSAL:
                    rstd_of(lt, bt, tail_dve, tail_pool, tmean_var, tvar_eps, trstd)
                if exists(bo):
                    rstd_of(lo, bo, out_dve, out_pool, mean_var, var_eps, rstd)
                if exists(bt) and lt == CROSS:
                    rstd_of(lt, bt, tail_dve, tail_pool, tmean_var, tvar_eps, trstd)

            iterations(pool, slot)


def kernel(**inputs):
    import concourse.bacc as bacc
    from concourse.bass_utils import run_bass_kernel_spmd

    a = {k: np.asarray(v) for k, v in inputs.items()}
    L0, L1 = "L0_xattn_", "L1_xattn_"
    by_dim = np.arange(D).reshape(HEADS, DK).T.reshape(-1)
    w4 = [a[L0 + "Wq"][:, by_dim], a[L0 + "Wk"][:, by_dim], a[L0 + "Wv"], a[L0 + "Wo"]]
    for n in ("sa", "ca"):
        w4 += [a[f"{L1}{n}_wq"].T[:, by_dim], a[f"{L1}{n}_wk"].T[:, by_dim], a[f"{L1}{n}_wv"].T, a[f"{L1}{n}_wo"].T]
    cols = [a[L0 + "bq"][by_dim], a[L1 + "sa_bq"][by_dim], a[L1 + "ca_bq"][by_dim],
            a[L0 + "bk"][by_dim], a[L1 + "sa_bk"][by_dim], a[L1 + "ca_bk"][by_dim],
            a[L0 + "bo"], a[L1 + "sa_bo"], a[L1 + "ca_bo"], a[L0 + "b2"], a[L1 + "ffn_b2"],
            *a[L0 + "b1"].reshape(CHUNKS, P), *a[L1 + "ffn_b1"].reshape(CHUNKS, P)]
    rows = [a[L0 + "bv"], a[L1 + "sa_bv"], a[L1 + "ca_bv"],
            a[L0 + "ln1_g"], a[L0 + "ln2_g"], a[L1 + "ln1_g"], a[L1 + "ln2_g"], a[L1 + "ln3_g"],
            a[L0 + "ln1_b"], a[L0 + "ln2_b"], a[L1 + "ln1_b"], a[L1 + "ln2_b"], a[L1 + "ln3_b"]]
    arrays = {
        "x": a["x"], "ctx": a["ctx_1024"],
        "key_mask": a["mask_Bx1x1xS2_if1"].reshape(BATCHES, TOKENS),
        "self_mask": a["mask_Bx1xSxS2_if1"].reshape(BATCHES, TOKENS, TOKENS),
        "w4": np.stack(w4), "w1": np.stack([a[L0 + "W1"], a[L1 + "ffn_w1"].T]),
        "w2": np.stack([a[L0 + "W2"], a[L1 + "ffn_w2"].T]),
        "bias_col": np.stack(cols, axis=1), "bias_row": np.stack(rows),
    }
    arrays = {k: np.ascontiguousarray(v) for k, v in arrays.items()}
    nc = bacc.Bacc("TRN2", target_bir_lowering=False, num_devices=1)
    args = [nc.dram_tensor(k, v.shape, mybir.dt.from_np(v.dtype), kind="ExternalInput").ap()
            for k, v in arrays.items()]
    out = nc.dram_tensor("out", (BATCHES, TOKENS, D), f32, kind="ExternalOutput").ap()
    mask_rows = nc.dram_tensor("mask_rows", (BATCHES, TOKENS), bf16, kind="Internal").ap()
    attention_program(nc, *args, out, mask_rows)
    r = run_bass_kernel_spmd(nc, [arrays], core_ids=[0])
    return r.results[0]["out"]
```

```python
import numpy as np
import concourse.bass as bass
from concourse import mybir
from contextlib import ExitStack

f32 = mybir.dt.float32
bf16 = mybir.dt.bfloat16
i32 = mybir.dt.int32
ALU = mybir.AluOpType
ACT = mybir.ActivationFunctionType
AX = mybir.AxisListType

BATCHES, TOKENS, D = 8, 256, 128
HEADS, DK, FF = 16, 8, 512
P = 128
TILES = TOKENS // P
CHUNKS = FF // P
PAIRS = HEADS // 2
LAYERS = 3
CAUSAL, SELF, CROSS = range(LAYERS)
EPS = 1e-5
BIG = float(2 ** 100)
SCALE = float(1 / np.sqrt(np.float32(DK)))

PRODUCTS = [(0, 0), (0, 1), (1, 0), (1, 1), (0, 2), (2, 0)]
TERMS = len(PRODUCTS)
MAX_ROW = 1 + TERMS * DK
ROWS_S = MAX_ROW
ROWS_T = MAX_ROW + 3
VW = DK + 1
VCOLS = HEADS * VW + 16

LOOP_FROM, LOOP_TO = 3, 7
STEPS = 32
UNITS = [12, 16, 16]

BQ, BK, BO = 0, 3, 6
B2, B1 = 9, 11
NCOL = B1 + 2 * CHUNKS
BV, LNG, LNB = 0, 3, 8
NROW = 13
LN_OUT = {CAUSAL: 0, SELF: 2, CROSS: 3}
LN_TAIL = {CAUSAL: 1, CROSS: 4}
FFN = {CAUSAL: 0, CROSS: 1}


class Batch:

    def __init__(self, reg, off):
        self.reg, self.off = reg, off

    def __add__(self, n):
        return Batch(self.reg, self.off + n)

    def __sub__(self, n):
        return Batch(self.reg, self.off - n)


def exists(b):
    return isinstance(b, Batch) or 0 <= b < BATCHES


def value(b, per=1, plus=0):
    if isinstance(b, Batch):
        return b.reg * per + (b.off * per + plus)
    return b * per + plus


class Signals:

    def __init__(self, sem, names, by=1):
        self.sem, self.names, self.by = sem, list(names), by

    def upto(self, b, name):
        n = len(self.names)
        return self.sem, value(b, n * self.by, (self.names.index(name) + 1) * self.by)


def slot_tasks(i, s):
    return ((s, i - s),
            (s + 1, i - s - 1) if s < 2 else (0, i + 1),
            (s - 1, i - s + 1) if s else (2, i - 3),
            (s - 2, i - s + 2) if s == 2 else (s + 1, i - s - 2))


PACE = {
    "split1": [0, 1, 1], "turn1": [4, 3, 4], "pv0": [20, 22, 20], "split0": [18, 18, 16],
    "turn0": [20, 23, 18], "pv1": [0, 2, 2], "o0": [6, 8, 6], "o1": [8, 10, 8], "heads": [12, 14, 14],
    "wo": [14, 14, 16], "back": [16, 16, 18], "stats": [20, 18, 20], "centre": [22, 18, 25],
    "norm": [24, 24, 28], "x": [0, None, 9], "up0": [2, None, 12], "up1": [4, None, 16],
    "down": [8, None, 20], "t_back": [10, None, 22], "t_stats": [10, None, 24], "t_centre": [12, None, 26],
    "t_norm": [14, None, 30], "bias": [None, 7, None], "mask": [None, 14, None], "keep": [None, 6, 1],
    "in": [14, 18, 2], "qk": [24, 20, 6], "v": [2, 22, 12], "part1": [2, 20, 7], "part2": [6, 22, 16],
    "v_bias": [4, 26, 12], "max": [(1, 32), (4, 32), (1, 28)], "attend": [(0, 29), (0, 30), (0, 32)],
    "rest": [None, 22, None],
}
AROUND = {
    -1: {"turn1": [4, 6, 4], "pv0": [20, 22, 22], "split0": [18, 18, 15], "turn0": [23, 21, 17],
        "pv1": [2, 2, 0], "o0": [6, 9, 5], "o1": [9, 10, 8], "heads": [14, 14, 14], "wo": [16, 14, 17],
        "back": [18, 17, 19], "stats": [22, 18, 21], "centre": [22, 18, 21], "norm": [23, 25, 28],
        "up0": [2, None, 15], "up1": [4, None, 19], "down": [7, None, 19], "t_back": [10, None, 21],
        "t_stats": [12, None, 23], "t_centre": [12, None, 23], "bias": [None, 8, None],
        "keep": [None, 4, 0], "in": [15, 17, 1], "qk": [20, 18, 5], "v": [4, 21, 11], "part1": [2, 20, 9],
        "part2": [6, 25, 17], "v_bias": [4, 25, 11], "max": [(0, 29), (3, 32), (2, 29)],
        "attend": [(0, 32), (2, 30), (0, 32)], "rest": [None, 21, None]},
    0: {"turn1": [4, 6, 5], "pv0": [20, 22, 22], "split0": [18, 18, 15], "turn0": [20, 21, 17],
        "pv1": [2, 1, 4], "o0": [6, 8, 7], "o1": [10, 10, 8], "heads": [14, 14, 14], "wo": [16, 14, 17],
        "back": [18, 16, 19], "stats": [22, 18, 21], "centre": [22, 18, 21], "norm": [23, 25, 28],
        "x": [0, None, 10], "up0": [2, None, 16], "up1": [4, None, 20], "t_centre": [12, None, 24],
        "bias": [None, 8, None], "keep": [None, 4, 0], "in": [15, 17, 2], "qk": [21, 18, 5],
        "v": [4, 21, 11], "part1": [3, 20, 9], "part2": [6, 22, 15], "v_bias": [4, 25, 12],
        "max": [(0, 30), (3, 30), (0, 29)], "attend": [(0, 32), (0, 32), (0, 32)],
        "rest": [None, 21, None]},
    1: {"turn1": [6, 5, 4], "pv0": [20, 22, 21], "split0": [18, 19, 15], "turn0": [20, 22, 17],
        "pv1": [2, 2, 2], "o0": [6, 8, 2], "o1": [10, 10, 8], "heads": [14, 14, 14], "wo": [16, 16, 17],
        "back": [18, 16, 19], "stats": [22, 18, 21], "centre": [22, 18, 21], "norm": [23, 25, 28],
        "x": [0, None, 10], "up0": [2, None, 16], "up1": [4, None, 20], "t_centre": [12, None, 24],
        "bias": [None, 8, None], "keep": [None, 4, 1], "in": [15, 17, 2], "qk": [20, 18, 5],
        "v": [4, 21, 11], "part1": [2, 21, 9], "part2": [6, 22, 15], "v_bias": [4, 25, 11],
        "max": [(0, 30), (3, 32), (0, 29)], "attend": [(1, 32), (0, 32), (0, 32)],
        "rest": [None, 21, None]},
    2: {"turn1": [4, 6, 4], "pv0": [20, 22, 22], "split0": [17, 18, 15], "turn0": [19, 21, 17],
        "pv1": [2, 2, 2], "o0": [6, 8, 5], "o1": [10, 10, 8], "heads": [14, 14, 13], "wo": [16, 14, 17],
        "back": [18, 16, 19], "stats": [22, 18, 21], "centre": [22, 18, 21], "norm": [23, 25, 28],
        "x": [0, None, 10], "up0": [2, None, 16], "up1": [4, None, 20], "t_stats": [11, None, 24],
        "t_centre": [12, None, 24], "bias": [None, 8, None], "keep": [None, 4, 0], "in": [15, 17, 1],
        "qk": [20, 18, 5], "v": [4, 21, 11], "part1": [2, 20, 9], "part2": [6, 22, 15],
        "v_bias": [4, 25, 11], "max": [(0, 30), (3, 32), (0, 29)], "attend": [(0, 32), (0, 32), (0, 32)],
        "rest": [None, 21, None]},
    7: {"turn1": [4, 3, 3], "pv0": [20, 22, 25], "pv1": [0, 1, 2], "heads": [12, 13, 14],
        "norm": [24, 26, 28], "t_norm": [15, None, 30], "v": [2, 22, 9], "part1": [2, 20, 10],
        "v_bias": [4, 27, 12], "max": [(0, 32), (4, 29), (1, 28)]},
    8: {"split1": [1, 1, 1], "turn1": [5, 4, 3], "o1": [8, 11, 8], "norm": [24, 26, 28],
        "t_norm": [15, None, 30], "bias": [None, 4, None], "in": [15, 18, 5], "qk": [25, 20, 6],
        "v": [3, 23, 12], "part1": [3, 20, 10], "part2": [7, 22, 16], "v_bias": [5, 26, 12],
        "max": [(0, 32), (4, 32), (1, 28)]},
    9: {"turn1": [4, 3, 3], "turn0": [20, 22, 18], "pv1": [0, 2, 4], "o0": [6, 8, 8], "wo": [16, 14, 16],
        "norm": [24, 26, 28], "t_norm": [15, None, 30], "in": [14, 17, 1], "qk": [24, 19, 6],
        "v": [2, 22, 9], "part1": [0, 20, 10], "v_bias": [4, 26, 9], "max": [(0, 32), (4, 32), (1, 28)]},
    10: {"turn1": [4, 4, 3], "split0": [18, 18, 15], "turn0": [20, 23, 16], "back": [16, 15, 18],
        "norm": [24, 26, 28], "t_stats": [10, None, 25], "t_norm": [15, None, 28],
        "mask": [None, 10, None], "keep": [None, 5, 1], "qk": [24, 19, 6], "v": [2, 21, 12],
        "part1": [2, 19, 10], "part2": [6, 21, 16], "v_bias": [4, 25, 12],
        "max": [(0, 32), (4, 32), (3, 28)], "rest": [None, 21, None]},
}


def steps_of(i):
    return PACE if isinstance(i, Batch) else {**PACE, **AROUND.get(i, {})}


def units(l, step, steps):
    first, last = steps[l]
    return [u for u in range(UNITS[l]) if step == first + u * (last - first) // UNITS[l]]


def unit_of(l, u):
    n = UNITS[l] // 2
    g, v = divmod(u, n)
    if l != CAUSAL:
        return v % 2, 8 * g + 2 * (v // 2), 2
    short = v % 3 == 0
    return (0, 8 * g + 4 * (v // 3), 4) if short else (1, 8 * g + 4 * (v // 3) + 2 * (v % 3 - 1), 2)


def attention_program(nc, x, ctx, key_mask, self_mask, w4, w1, w2, bias_col, bias_row, out, mask_rows):
    es = ExitStack()
    with es:
        def sb(name, shape, dt=f32):
            return es.enter_context(nc.sbuf_tensor(name, shape, dt))

        def sem(name):
            return es.enter_context(nc.semaphore(name))

        def signals(name, names, by=1):
            return Signals(sem(name), names, by)

        def per_layer(name, names, by=1):
            return [signals(f"{name}{l}", names(l) if callable(names) else names, by) for l in range(LAYERS)]

        w4_sb = sb("w4_sb", [P, 4 * LAYERS, D])
        w1_sb = sb("w1_sb", [P, 2, FF])
        w2_sb = sb("w2_sb", [P, 2, CHUNKS, D])
        col = sb("col", [P, NCOL])
        row = sb("row", [P, NROW, D])
        ident_f = sb("ident_f", [P, P])
        ident_b = sb("ident_b", [P, P], bf16)
        causal_q = sb("causal_q", [P, P], bf16)
        causal_k = sb("causal_k", [P, P], bf16)
        keep_row = sb("keep_row", [P, 1])
        half_neg = sb("half_neg", [P, TILES])
        wait_carrier = sb("wait_carrier", [P, 1])
        eps = sb("eps", [P, TILES])
        km_int = sb("km_int", [BATCHES, TOKENS], i32)
        km_bias = sb("km_bias", [BATCHES, TOKENS], bf16)

        stacks = [sb(f"stacks{l}", [ROWS_T, HEADS, 2, TOKENS], bf16) for l in range(LAYERS)]
        q_stack = [st[:, :, 0, :] for st in stacks]
        k_stack = [st[:, :, 1, :] for st in stacks]
        v_sb = [sb(f"v_sb{l}", [P, TILES, VCOLS]) for l in range(LAYERS)]
        neg_max = [sb(f"neg_max{l}", [P, TILES, HEADS]) for l in range(LAYERS)]
        max_rest = [sb(f"max_rest{l}", [P, TILES, HEADS]) for l in range(LAYERS)]
        max_part = [sb(f"max_part{l}", [P, 2, TILES, 3, 8], bf16) for l in range(LAYERS)]
        max_rows = [sb(f"max_rows{l}", [24, 2, TOKENS], bf16) for l in range(LAYERS)]
        ot_sb = [sb(f"ot_sb{l}", [P, 2, 512]) for l in range(LAYERS)]
        rsum = [sb(f"rsum{l}", [P, TILES, PAIRS, 2]) for l in range(LAYERS)]
        heads = [sb(f"heads{l}", [P, TILES, D]) for l in range(LAYERS)]
        heads_t = [sb(f"heads_t{l}", [P, TOKENS]) for l in range(LAYERS)]
        y_t = [sb(f"y_t{l}", [P, TOKENS]) for l in range(LAYERS)]
        y = [sb(f"y{l}", [P, TILES, D]) for l in range(LAYERS)]
        stats = [sb(f"stats{l}", [P, TILES, 6]) for l in range(LAYERS)]
        mean_var = [sb(f"mean_var{l}", [P, TILES, 2]) for l in range(LAYERS)]
        var_eps = [sb(f"var_eps{l}", [P, TILES]) for l in range(LAYERS)]
        rstd = [sb(f"rstd{l}", [P, TILES]) for l in range(LAYERS)]
        centred = [sb(f"centred{l}", [P, TILES, D]) for l in range(LAYERS)]
        x1 = [sb(f"x1_{l}", [P, TILES, D]) for l in range(LAYERS)]
        x2 = [sb(f"x2_{l}", [P, TILES, D]) for l in range(LAYERS)]
        resid = [sb(f"resid{l}", [P, TILES, D]) for l in range(LAYERS)]
        x1_t = [sb(f"x1_t{l}", [P, TOKENS]) for l in range(LAYERS)]
        hid_t = [sb(f"hid_t{l}", [P, CHUNKS, TOKENS]) for l in range(LAYERS)]
        z_t = [sb(f"z_t{l}", [P, TOKENS]) for l in range(LAYERS)]
        z = [sb(f"z{l}", [P, TILES, D]) for l in range(LAYERS)]
        tstats = [sb(f"tstats{l}", [P, TILES, 6]) for l in range(LAYERS)]
        tmean_var = [sb(f"tmean_var{l}", [P, TILES, 2]) for l in range(LAYERS)]
        tvar_eps = [sb(f"tvar_eps{l}", [P, TILES]) for l in range(LAYERS)]
        trstd = [sb(f"trstd{l}", [P, TILES]) for l in range(LAYERS)]
        tcentred = [sb(f"tcentred{l}", [P, TILES, D]) for l in range(LAYERS)]
        x_in = sb("x_in", [P, TILES, D])
        ctx_in = {CAUSAL: sb("ctx_in0", [P, TILES, D]), CROSS: sb("ctx_in2", [P, TILES, D])}
        in_t = [sb(f"in_t{l}", [P, 2, TOKENS]) for l in range(LAYERS)]
        qk = [sb(f"qk{l}", [P, 2 * TOKENS]) for l in range(LAYERS)]
        qk_rest = [sb(f"qk_rest{l}", [P, 2 * TOKENS]) for l in range(LAYERS)]
        qk_part = [sb(f"qk_part{l}", [P, 2, 3, TOKENS], bf16) for l in range(LAYERS)]
        sm_int = sb("sm_int", [P, TILES, TOKENS], i32)
        sm_q = sb("sm_q", [P, TILES, TOKENS], bf16)
        sm_k = sb("sm_k", [P, TILES, TOKENS], bf16)
        p_sb = sb("p_sb", [P, TILES, HEADS, TOKENS])

        bank = [es.enter_context(nc.psum_tensor(f"bank{n}", [P, 512], f32)) for n in range(8)]
        S_BANK, T_BANK = bank[0:3], bank[3:5]
        O_BANK, OUT_BANK, TAIL_BANK = bank[5:8]

        def s_bank(l, u):
            return S_BANK[(u + (l == CROSS)) % 3]

        weights0 = sem("weights0")
        loaded = [sem(f"loaded{n}") for n in range(6)]
        consts = signals("consts", ["ident", "selects", "mask"])
        stacks_set = [sem(f"stacks_set{l}") for l in range(LAYERS)]
        made = sem("made")
        mask_saved = sem("mask_saved")
        x_loaded = sem("x_loaded")
        ctx_loaded = {CAUSAL: sem("ctx_loaded0"), CROSS: sem("ctx_loaded2")}
        resid_loaded = sem("resid_loaded")
        sm_loaded = sem("sm_loaded")
        out_stored = sem("out_stored")
        stacked = [sem(f"stacked{l}") for l in range(LAYERS)]
        STACKED = [TERMS * 16, TERMS * 16, (TERMS + 1) * 16]
        s_written = per_layer("s_written", lambda l: range(UNITS[l]))
        s_read = per_layer("s_read", lambda l: range(UNITS[l]))
        t_written = per_layer("t_written", lambda l: range(UNITS[l]))
        p_ready = per_layer("p_ready", lambda l: range(UNITS[l]))
        max_split = per_layer("max_split", [(g, n) for g in range(2) for n in ("part1", "rest", "part2", "part3")])
        max_turned = per_layer("max_turned", range(2))
        max_copied = per_layer("max_copied", range(2))
        max_in = [[signals(f"max_in{l}_{g}", ["dma"], 16) for g in range(2)] for l in range(LAYERS)]
        pv_done = per_layer("pv_done", range(2))
        o_copied = per_layer("o_copied", range(2))
        out_pe = per_layer("out_pe", ["o0", "o1", "heads", "wo", "back"])
        out_act = per_layer("out_act", ["heads", "wo"])
        out_dve = per_layer("out_dve", lambda l: ["recip0"] + ["keep0"] * (l == CAUSAL) + [
            "norm0", "recip1", "norm1", "add", "stats", "aggr", "centre0", "centre1", "norm_a", "norm_b"])
        out_pool = per_layer("out_pool", ["eps", "pow"])
        tail_pe = per_layer("tail_pe", ["x", "up0", "up1", "down", "back"])
        tail_act = per_layer("tail_act", ["x", "up0", "up1", "down"])
        tail_dve = per_layer("tail_dve", ["add", "stats", "aggr", "centre0", "centre1", "norm_a", "norm_b"])
        tail_pool = per_layer("tail_pool", ["eps", "pow"])
        prep_pe = per_layer("prep_pe", lambda l: ["mask"] * (l == SELF) + ["in", "qk", "v"])
        prep_act = per_layer("prep_act", lambda l: ["mask"] * (l == SELF) + ["in", "qk", "part1"])
        prep_dve = per_layer("prep_dve", lambda l: ["rest", "part2", "part3", "v"] if l == SELF else ["v", "part2"])
        prep_pool = per_layer("prep_pool", ["rest", "part3"])
        mask_q = signals("mask_q", ["bias"])
        resid_kept = {SELF: signals("resid_kept1", ["copy"]), CROSS: signals("resid_kept2", ["copy"])}

        def iterations(eng, slot):
            for i in range(-1, LOOP_FROM):
                for s in range(3):
                    slot(i, s)
            with eng.Fori(LOOP_FROM, LOOP_TO) as reg:
                for s in range(3):
                    slot(Batch(reg, 0), s)
            for i in range(LOOP_TO, BATCHES + LAYERS):
                for s in range(3):
                    slot(i, s)

        def constant_rows(eng, l):
            for n, (rows, is_) in enumerate(((v_sb[l][:], 1.0), (k_stack[l][32:ROWS_T], 1.0),
                                             (q_stack[l][0:1], 1.0), (k_stack[l][0:1], 0.0))):
                if n and eng is nc.gpsimd:
                    eng.wait_ge(stacks_set[l], n)
                eng.memset(rows, is_).then_inc(stacks_set[l], 1)

        SET = 4

        def starts(b):
            return not isinstance(b, Batch) and b == 0

        def halves(a):
            return a[:, :].rearrange("p (c t) -> p c t", c=2)

        def earlier_slot(i, s):
            while True:
                i, s = (i, s - 1) if s else (i - 1, 2)
                if isinstance(i, Batch):
                    return i, s
                if i < 0:
                    return None
                if exists(i - s):
                    return i, s

        block = es.enter_context(nc.Block())

        @block.sync
        def _(sp):
            def tokens(a, b):
                at = bass.ds(value(b), 1) if isinstance(b, Batch) else slice(b, b + 1)
                return a[at, :, :].rearrange("a (t p) d -> (a p) t d", p=P)

            def load_prepare0(b):
                if isinstance(b, Batch) or b > 0:
                    sp.wait_ge(*prep_pe[CAUSAL].upto(b - 1, "in"))
                sp.dma_start(x_in[:], tokens(x, b)).then_inc(x_loaded, 16)
                sp.dma_start(ctx_in[CAUSAL][:], tokens(ctx, b)).then_inc(ctx_loaded[CAUSAL], 16)

            def stack(l, b):
                if starts(b):
                    sp.wait_ge(stacks_set[l], SET)
                for part, of in (("part1", prep_act), ("part2", prep_dve), ("part3", prep_dve if l == SELF else prep_pool)):
                    sp.wait_ge(*of[l].upto(b, part))
                    n = int(part[-1]) - 1
                    if n == 0 and l == CROSS:
                        at = bass.ds(value(b), 1) if isinstance(b, Batch) else slice(b, b + 1)
                        sp.dma_start(k_stack[l][0:1, :, :],
                                     mask_rows[at, :].rearrange("(a h) k -> a h k", a=1)
                                     .broadcast_to([1, HEADS, TOKENS])).then_inc(stacked[l], 16)
                    for t, (qn, kn) in enumerate(PRODUCTS):
                        if max(qn, kn) == n:
                            flat = qk_part[l][:, :, :, :].rearrange("p c n t -> p (c n) t")
                            sp.dma_start(stacks[l][1 + DK * t:1 + DK * (t + 1), :, :, :],
                                         flat[:, qn:3 + kn + 1:3 + kn - qn, :]).then_inc(stacked[l], 16)

            def max_dma(l, b, g):
                sp.wait_ge(*max_copied[l].upto(b, g))
                sp.dma_start(q_stack[l][MAX_ROW:MAX_ROW + 3, 8 * g:8 * g + 8, :],
                             max_rows[l][:, g, :]).then_inc(max_in[l][g].sem, 16)

            def slot(i, s):
                (l, b), (ln, bn), (lo, bo), (lt, bt) = slot_tasks(i, s)
                first = not isinstance(i, Batch) and i == -1
                if not isinstance(i, Batch) and (i, s) == (0, 1):
                    sp.wait_ge(*consts.upto(0, "mask"))
                    sp.dma_start(mask_rows[:, :], km_bias[:]).then_inc(mask_saved, 16)
                    sp.wait_ge(mask_saved, 16)
                if s == 0 and exists(i + 1) and not first:
                    load_prepare0(i + 1)
                if s == 0 and exists(i):
                    sp.dma_start(resid[CAUSAL][:], tokens(x, i)).then_inc(resid_loaded, 16)
                if s == 1 and exists(i):
                    at = bass.ds(value(i), 1) if isinstance(i, Batch) else slice(i, i + 1)
                    sp.dma_start(sm_int[:], self_mask[at, :, :].rearrange("a (t p) k -> (a p) t k", p=P))\
                        .then_inc(sm_loaded, 16)
                if s == 2 and exists(i - 1):
                    if isinstance(i, Batch) or i > 1:
                        sp.wait_ge(*prep_pe[CROSS].upto(i - 2, "in"))
                    sp.dma_start(ctx_in[CROSS][:], tokens(ctx, i - 1)).then_inc(ctx_loaded[CROSS], 16)
                if exists(b):
                    max_dma(l, b, 1)
                if s == 1 and exists(i + 1):
                    stack(CAUSAL, i + 1)
                if s == 0 and exists(bt):
                    stack(CROSS, bt)
                if exists(bn):
                    max_dma(ln, bn, 0)
                if s == 1 and exists(bt):
                    sp.wait_ge(*tail_dve[CROSS].upto(bt, "norm_b"))
                    sp.dma_start(tokens(out, bt), x2[CROSS][:]).then_inc(out_stored, 16)
                if s == 2 and exists(bt):
                    stack(SELF, bt)

            load_prepare0(0)
            w4_view = w4.rearrange("n i o -> i n o")
            sp.dma_start(w4_sb[:, 0:4, :], w4_view[:, 0:4, :]).then_inc(weights0, 16)
            sp.dma_start(col[:], bias_col).then_inc(loaded[3], 16)
            sp.dma_start(row[:], bias_row.rearrange("(a n) d -> a n d", a=1).broadcast_to([P, NROW, D]))\
                .then_inc(loaded[4], 16)
            sp.dma_start(km_int[:], key_mask).then_inc(loaded[5], 16)
            sp.dma_start(w4_sb[:, 4:4 * LAYERS, :], w4_view[:, 4:4 * LAYERS, :]).then_inc(loaded[0], 16)
            sp.dma_start(w1_sb[:], w1.rearrange("n i f -> i n f")).then_inc(loaded[1], 16)
            sp.dma_start(w2_sb[:], w2.rearrange("n (c f) o -> f n c o", f=P)).then_inc(loaded[2], 16)
            iterations(sp, slot)
            sp.wait_ge(out_stored, 16 * BATCHES)

        @block.tensor
        def _(pe):
            last_read = {"o": None, "out": None, "tail": None, "s": None}

            def bank_free(name):
                if last_read[name] is not None:
                    pe.wait_ge(*last_read[name][0].upto(*last_read[name][1:]))

            def scores(l, b, u):
                if u == 0:
                    if starts(b):
                        pe.wait_ge(stacks_set[l], SET)
                    pe.wait_ge(stacked[l], value(b, STACKED[l], STACKED[l]))
                    if l == SELF:
                        pe.wait_ge(*mask_q.upto(b, "bias"))
                if u >= 3:
                    pe.wait_ge(*s_read[l].upto(b, u - 3))
                elif last_read["s"] is not None:
                    lp, bp = last_read["s"]
                    before = max(v for v in range(UNITS[lp]) if s_bank(lp, v) is s_bank(l, u))
                    pe.wait_ge(*s_read[lp].upto(bp, before))
                qt, h0, n = unit_of(l, u)
                keys = TOKENS if n == 2 else P
                dst = s_bank(l, u)
                if l == SELF:
                    nc.tensor.matmul(dst[:, :], ident_b[:], sm_q[:, qt:qt + 1, :].broadcast_to([P, 2, TOKENS]),
                                     start=True, stop=False)
                if l == CAUSAL:
                    nc.tensor.matmul(dst[:, :].rearrange("p (h k) -> p h k", h=n)[:, :, keys - P:keys],
                                     ident_b[:], causal_q[:, :].rearrange("p (a k) -> p a k", a=1)
                                     .broadcast_to([P, n, P]), start=True, stop=False, skip_group_check=True)
                for e in range(n):
                    mm = nc.tensor.matmul(dst[:, e * keys:(e + 1) * keys],
                                          q_stack[l][0:ROWS_S, h0 + e, qt * P:(qt + 1) * P],
                                          k_stack[l][0:ROWS_S, h0 + e, 0:keys],
                                          start=(l == CROSS), stop=(l == CROSS or e == n - 1),
                                          skip_group_check=(l == CAUSAL))
                mm.then_inc(s_written[l].sem, 1)
                if u == UNITS[l] - 1:
                    last_read["s"] = (l, b)

            def scores_t(l, b, u, i, s):
                n = UNITS[l]
                if u % (n // 2) == 0:
                    pe.wait_ge(*max_in[l][u // (n // 2)].upto(b, "dma"))
                if u == 0 and l == SELF:
                    pe.wait_ge(*prep_act[SELF].upto(b, "mask"))
                if u >= 2:
                    pe.wait_ge(*p_ready[l].upto(b, u - 2))
                elif (before := earlier_slot(i, s)) is not None:
                    lp, bp = before[1], before[0] - before[1]
                    pe.wait_ge(*p_ready[lp].upto(bp, UNITS[lp] - 2 + u))
                kt, h0, n = unit_of(l, u)
                if l == CAUSAL:
                    kt = 1 - kt
                q0 = P if n == 4 else 0
                qs = TOKENS - q0
                dst = T_BANK[u % 2]
                if l == SELF:
                    nc.tensor.matmul(dst[:, :], ident_b[:], sm_k[:, kt:kt + 1, :].broadcast_to([P, 2, TOKENS]),
                                     start=True, stop=False)
                if l == CAUSAL:
                    nc.tensor.matmul(dst[:, :].rearrange("p (h q) -> p h q", h=n)[:, :, 0:P],
                                     ident_b[:], causal_k[:, :].rearrange("p (a k) -> p a k", a=1)
                                     .broadcast_to([P, n, P]), start=True, stop=False, skip_group_check=True)
                for e in range(n):
                    mm = nc.tensor.matmul(dst[:, e * qs:(e + 1) * qs],
                                          k_stack[l][0:ROWS_T, h0 + e, kt * P:(kt + 1) * P],
                                          q_stack[l][0:ROWS_T, h0 + e, q0:TOKENS],
                                          start=(l == CROSS), stop=(l == CROSS or e == n - 1),
                                          skip_group_check=(l == CAUSAL))
                mm.then_inc(t_written[l].sem, 1)

            def turn_max(l, b, g):
                bank_free("out")
                pe.wait_ge(*max_split[l].upto(b, (g, "part3")))
                for qt in range(TILES):
                    mm = nc.tensor.transpose(OUT_BANK[0:24, :].bitcast(bf16)[:, qt * P:(qt + 1) * P],
                                             max_part[l][:, g, qt, :, :].rearrange("p c h -> p (c h)"), ident_b[:])
                mm.then_inc(max_turned[l].sem, 1)
                last_read["out"] = (max_copied[l], b, g)

            def pv(l, b, g, kt):
                if kt == 0:
                    bank_free("o")
                    if g == 0:
                        pe.wait_ge(*prep_dve[l].upto(b, "v"))
                    pe.wait_ge(*p_ready[l].upto(b, (g + 1) * UNITS[l] // 2 - 1))
                for j in range(4):
                    pair = 4 * g + j
                    q0 = P if (kt == 1 and l == CAUSAL) else 0
                    mm = nc.tensor.matmul(
                        O_BANK[32 * j:32 * j + 32, :].rearrange("p (e q) -> p e q", e=2)[:, :, q0:TOKENS],
                        v_sb[l][:, kt, 2 * VW * pair:2 * VW * pair + 32],
                        p_sb[:, kt, 2 * pair:2 * pair + 2, q0:TOKENS],
                        start=(kt == 0), stop=(kt == 1), skip_group_check=True)
                if kt == 1:
                    mm.then_inc(pv_done[l].sem, 1)
                    last_read["o"] = (o_copied[l], b, g)

            def out_turn_o(l, b, qt):
                bank_free("out")
                pe.wait_ge(*o_copied[l].upto(b, 1))
                for g in range(2):
                    for e in range(2):
                        mm = nc.tensor.transpose(OUT_BANK[:, 256 * e + P * g:256 * e + P * (g + 1)],
                                                 ot_sb[l][:, g, e * TOKENS + qt * P:e * TOKENS + (qt + 1) * P],
                                                 ident_f[:])
                mm.then_inc(out_pe[l].sem, 1)
                last_read["out"] = (out_dve[l], b, f"norm{qt}")

            def two_turns(dst, src):
                for t in range(TILES):
                    mm = nc.tensor.transpose(dst[:, t * P:(t + 1) * P], src(t), ident_f[:])
                return mm

            def out_heads(l, b):
                bank_free("out")
                two_turns(OUT_BANK, lambda t: heads[l][:, t, :]).then_inc(out_pe[l].sem, 1)
                last_read["out"] = (out_act[l], b, "heads")

            def out_wo(l, b):
                bank_free("out")
                nc.tensor.matmul(OUT_BANK[:, 0:TOKENS], w4_sb[:, 4 * l + 3, :], heads_t[l][:],
                                 start=True, stop=True).then_inc(out_pe[l].sem, 1)
                last_read["out"] = (out_act[l], b, "wo")

            def out_back(l, b):
                bank_free("out")
                two_turns(OUT_BANK, lambda t: y_t[l][:, t * P:(t + 1) * P]).then_inc(out_pe[l].sem, 1)
                last_read["out"] = (out_dve[l], b, "add")

            def tail_x(l, b):
                bank_free("tail")
                pe.wait_ge(*out_dve[l].upto(b, "norm_b"))
                two_turns(TAIL_BANK, lambda t: x1[l][:, t, :]).then_inc(tail_pe[l].sem, 1)
                last_read["tail"] = (tail_act[l], b, "x")

            def tail_up(l, b, n):
                bank_free("tail")
                for c in range(2):
                    mm = nc.tensor.matmul(TAIL_BANK[:, c * TOKENS:(c + 1) * TOKENS],
                                          w1_sb[:, FFN[l], (2 * n + c) * P:(2 * n + c + 1) * P], x1_t[l][:],
                                          start=True, stop=True)
                mm.then_inc(tail_pe[l].sem, 1)
                last_read["tail"] = (tail_act[l], b, f"up{n}")

            def tail_down(l, b):
                bank_free("tail")
                for c in range(CHUNKS):
                    mm = nc.tensor.matmul(TAIL_BANK[:, 0:TOKENS], w2_sb[:, FFN[l], c, :], hid_t[l][:, c, :],
                                          start=(c == 0), stop=(c == CHUNKS - 1))
                mm.then_inc(tail_pe[l].sem, 1)
                last_read["tail"] = (tail_act[l], b, "down")

            def tail_back(l, b):
                bank_free("tail")
                two_turns(TAIL_BANK, lambda t: z_t[l][:, t * P:(t + 1) * P]).then_inc(tail_pe[l].sem, 1)
                last_read["tail"] = (tail_dve[l], b, "add")

            def prep_in(l, b):
                bank_free("tail")
                if l == CAUSAL:
                    pe.wait_ge(x_loaded, value(b, 16, 16))
                    src = x_in
                elif l == SELF:
                    pe.wait_ge(*tail_dve[CAUSAL].upto(b, "norm_b"))
                    src = x2[CAUSAL]
                else:
                    pe.wait_ge(*out_dve[SELF].upto(b, "norm_b"))
                    src = x1[SELF]
                mm = two_turns(TAIL_BANK, lambda t: src[:, t, :])
                if l != SELF:
                    pe.wait_ge(ctx_loaded[l], value(b, 16, 16))
                    mm = two_turns(TAIL_BANK[:, TOKENS:2 * TOKENS], lambda t: ctx_in[l][:, t, :])
                mm.then_inc(prep_pe[l].sem, 1)
                last_read["tail"] = (prep_act[l], b, "in")

            def prep_qk(l, b):
                bank_free("tail")
                for c in range(2):
                    mm = nc.tensor.matmul(TAIL_BANK[:, c * TOKENS:(c + 1) * TOKENS], w4_sb[:, 4 * l + c, :],
                                          in_t[l][:, 0 if l == SELF else c, :], start=True, stop=True)
                mm.then_inc(prep_pe[l].sem, 1)
                last_read["tail"] = (prep_act[l], b, "qk")

            def prep_v(l, b):
                bank_free("tail")
                kv = 0 if l == SELF else 1
                for kt in range(TILES):
                    mm = nc.tensor.matmul(TAIL_BANK[:, kt * D:(kt + 1) * D], in_t[l][:, kv, kt * P:(kt + 1) * P],
                                          w4_sb[:, 4 * l + 2, :], start=True, stop=True)
                mm.then_inc(prep_pe[l].sem, 1)
                last_read["tail"] = (prep_dve[l], b, "v")

            def prep_mask(b):
                bank_free("tail")
                pe.wait_ge(*mask_q.upto(b, "bias"))
                for kt in range(TILES):
                    for qt in range(TILES):
                        mm = nc.tensor.transpose(
                            TAIL_BANK[:, :].bitcast(bf16)[:, kt * TOKENS + qt * P:kt * TOKENS + (qt + 1) * P],
                            sm_q[:, qt, kt * P:(kt + 1) * P], ident_b[:])
                mm.then_inc(prep_pe[SELF].sem, 1)
                last_read["tail"] = (prep_act[SELF], b, "mask")

            def slot(i, s):
                (l, b), (ln, bn), (lo, bo), (lt, bt) = slot_tasks(i, s)
                at = steps_of(i)
                if not isinstance(i, Batch) and (i, s) == (-1, 2):
                    pe.wait_ge(*consts.upto(0, "selects"))
                if not isinstance(i, Batch) and (i, s) == (0, 2):
                    for n in range(3):
                        pe.wait_ge(loaded[n], 16)
                for t in range(STEPS):
                    if exists(b):
                        if t == at["turn1"][l]:
                            turn_max(l, b, 1)
                        if t in (at["pv0"][l], at["pv0"][l] + 2):
                            pv(l, b, 0, (t - at["pv0"][l]) // 2)
                    if exists(bn) and t == at["turn0"][ln]:
                        turn_max(ln, bn, 0)
                    if exists(bo):
                        if t in (at["pv1"][lo], at["pv1"][lo] + 2):
                            pv(lo, bo, 1, (t - at["pv1"][lo]) // 2)
                        if t == at["o0"][lo]:
                            out_turn_o(lo, bo, 0)
                        if t == at["o1"][lo]:
                            out_turn_o(lo, bo, 1)
                        if t == at["heads"][lo]:
                            out_heads(lo, bo)
                        if t == at["wo"][lo]:
                            out_wo(lo, bo)
                        if t == at["back"][lo]:
                            out_back(lo, bo)
                    if exists(bt) and lt in FFN:
                        if t == at["x"][lt]:
                            tail_x(lt, bt)
                        if t == at["up0"][lt]:
                            tail_up(lt, bt, 0)
                        if t == at["up1"][lt]:
                            tail_up(lt, bt, 1)
                        if t == at["down"][lt]:
                            tail_down(lt, bt)
                        if t == at["t_back"][lt]:
                            tail_back(lt, bt)
                    if s != 1 and exists(bt):
                        lp = lt + 1
                        if t == at["mask"][lp]:
                            prep_mask(bt)
                        if t == at["in"][lp]:
                            prep_in(lp, bt)
                        if t == at["qk"][lp]:
                            prep_qk(lp, bt)
                        if t == at["v"][lp]:
                            prep_v(lp, bt)
                    if exists(i + 1):
                        if s == 0 and t == at["in"][CAUSAL]:
                            prep_in(CAUSAL, i + 1)
                        if s == 0 and t == at["qk"][CAUSAL]:
                            prep_qk(CAUSAL, i + 1)
                        if s == 1 and t == at["v"][CAUSAL]:
                            prep_v(CAUSAL, i + 1)
                    if exists(b):
                        for u in units(l, t, at["attend"]):
                            scores_t(l, b, u, i, s)
                    if exists(bn):
                        for u in units(ln, t, at["max"]):
                            scores(ln, bn, u)

            pe.wait_ge(weights0, 16)
            pe.wait_ge(*consts.upto(0, "ident"))

            def looping(eng, slot):
                for i in range(-1, LOOP_FROM):
                    for s in range(3):
                        slot(i, s)
                with eng.Fori(LOOP_FROM, LOOP_TO) as reg:
                    for k, v in last_read.items():
                        last_read[k] = (v[0], Batch(reg, v[1] - LOOP_FROM), *v[2:])
                    before = dict(last_read)
                    for s in range(3):
                        slot(Batch(reg, 0), s)
                    for k, v in last_read.items():
                        assert (v[0], v[1].off, *v[2:]) == (before[k][0], before[k][1].off + 1, *before[k][2:])
                for k, v in last_read.items():
                    last_read[k] = (v[0], v[1].off + LOOP_TO - 1, *v[2:])
                for i in range(LOOP_TO, BATCHES + LAYERS):
                    for s in range(3):
                        slot(i, s)
            looping(pe, slot)

        @block.scalar
        def _(act):
            def exps(l, b, u, i, s):
                n = UNITS[l] // 2
                if u % n == 0 and (before := earlier_slot(i, s)) is not None:
                    act.wait_ge(*pv_done[before[1]].upto(before[0] - before[1], u // n))
                act.wait_ge(*t_written[l].upto(b, u))
                kt, h0, nh = unit_of(l, u)
                if l == CAUSAL:
                    kt = 1 - kt
                q0 = P if nh == 4 else 0
                nc.scalar.activation(p_sb[:, kt, h0:h0 + nh, q0:TOKENS],
                                     T_BANK[u % 2][:, :].rearrange("p (h q) -> p h q", h=nh),
                                     ACT.Exp, scale=SCALE).then_inc(p_ready[l].sem, 1)

            def copy_max(l, b, g):
                act.wait_ge(*max_turned[l].upto(b, g))
                nc.scalar.activation(max_rows[l][:, g, :], OUT_BANK[0:24, :].bitcast(bf16)[:, 0:TOKENS], ACT.Copy)\
                    .then_inc(max_copied[l].sem, 1)

            def copy_o(l, b, g):
                act.wait_ge(*pv_done[l].upto(b, g))
                nc.scalar.activation(ot_sb[l][:, g, :], O_BANK[:, :], ACT.Copy).then_inc(o_copied[l].sem, 1)

            def out_heads(l, b):
                act.wait_ge(*out_pe[l].upto(b, "heads"))
                nc.scalar.activation(heads_t[l][:], OUT_BANK[:, 0:TOKENS], ACT.Copy).then_inc(out_act[l].sem, 1)

            def out_wo(l, b):
                act.wait_ge(*out_pe[l].upto(b, "wo"))
                nc.scalar.activation(y_t[l][:], OUT_BANK[:, 0:TOKENS], ACT.Identity,
                                     bias=col[:, BO + l:BO + l + 1]).then_inc(out_act[l].sem, 1)

            def tail_x(l, b):
                act.wait_ge(*tail_pe[l].upto(b, "x"))
                nc.scalar.activation(x1_t[l][:], TAIL_BANK[:, 0:TOKENS], ACT.Copy).then_inc(tail_act[l].sem, 1)

            def tail_up(l, b, n):
                act.wait_ge(*tail_pe[l].upto(b, f"up{n}"))
                for c in range(2):
                    at = B1 + FFN[l] * CHUNKS + 2 * n + c
                    ins = nc.scalar.activation(hid_t[l][:, 2 * n + c, :], TAIL_BANK[:, c * TOKENS:(c + 1) * TOKENS],
                                               ACT.Relu, bias=col[:, at:at + 1])
                ins.then_inc(tail_act[l].sem, 1)

            def tail_down(l, b):
                act.wait_ge(*tail_pe[l].upto(b, "down"))
                nc.scalar.activation(z_t[l][:], TAIL_BANK[:, 0:TOKENS], ACT.Identity,
                                     bias=col[:, B2 + FFN[l]:B2 + FFN[l] + 1]).then_inc(tail_act[l].sem, 1)

            def prep_in(l, b):
                act.wait_ge(*prep_pe[l].upto(b, "in"))
                n = 1 if l == SELF else 2
                nc.scalar.activation(in_t[l][:, 0:n, :].rearrange("p a t -> p (a t)"), TAIL_BANK[:, 0:n * TOKENS],
                                     ACT.Copy).then_inc(prep_act[l].sem, 1)

            def prep_qk(l, b):
                act.wait_ge(*prep_pe[l].upto(b, "qk"))
                for c, at in ((0, BQ + l), (1, BK + l)):
                    ins = nc.scalar.activation(qk[l][:, c * TOKENS:(c + 1) * TOKENS],
                                               TAIL_BANK[:, c * TOKENS:(c + 1) * TOKENS], ACT.Identity,
                                               bias=col[:, at:at + 1])
                ins.then_inc(prep_act[l].sem, 1)

            def prep_part1(l, b):
                if isinstance(b, Batch) or b > 0:
                    act.wait_ge(*t_written[l].upto(b - 1, UNITS[l] - 1))
                    act.wait_ge(stacked[l], value(b, STACKED[l]))
                act.wait_ge(*prep_act[l].upto(b, "qk"))
                nc.scalar.activation(qk_part[l][:, :, 0, :], halves(qk[l]), ACT.Copy).then_inc(prep_act[l].sem, 1)

            def prep_mask(b):
                act.wait_ge(*prep_pe[SELF].upto(b, "mask"))
                nc.scalar.activation(sm_k[:, :, :].rearrange("p t q -> p (t q)"),
                                     TAIL_BANK[:, :].bitcast(bf16)[:, 0:2 * TOKENS], ACT.Copy)\
                    .then_inc(prep_act[SELF].sem, 1)

            def slot(i, s):
                (l, b), (ln, bn), (lo, bo), (lt, bt) = slot_tasks(i, s)
                at = steps_of(i)
                for t in range(STEPS):
                    if exists(b):
                        if t == at["turn1"][l]:
                            copy_max(l, b, 1)
                        if t == at["pv0"][l] + 2:
                            copy_o(l, b, 0)
                    if exists(bn) and t == at["turn0"][ln]:
                        copy_max(ln, bn, 0)
                    if exists(bo):
                        if t == at["pv1"][lo] + 2:
                            copy_o(lo, bo, 1)
                        if t == at["heads"][lo]:
                            out_heads(lo, bo)
                        if t == at["wo"][lo]:
                            out_wo(lo, bo)
                    if exists(bt) and lt in FFN:
                        if t == at["x"][lt]:
                            tail_x(lt, bt)
                        if t == at["up0"][lt]:
                            tail_up(lt, bt, 0)
                        if t == at["up1"][lt]:
                            tail_up(lt, bt, 1)
                        if t == at["down"][lt]:
                            tail_down(lt, bt)
                    if s != 1 and exists(bt):
                        lp = lt + 1
                        if t == at["mask"][lp]:
                            prep_mask(bt)
                        if t == at["in"][lp]:
                            prep_in(lp, bt)
                        if t == at["qk"][lp]:
                            prep_qk(lp, bt)
                        if t == at["part1"][lp]:
                            prep_part1(lp, bt)
                    if exists(i + 1):
                        if s == 0 and t == at["in"][CAUSAL]:
                            prep_in(CAUSAL, i + 1)
                        if s == 0 and t == at["qk"][CAUSAL]:
                            prep_qk(CAUSAL, i + 1)
                        if s == 1 and t == at["part1"][CAUSAL]:
                            prep_part1(CAUSAL, i + 1)
                    if exists(b):
                        for u in units(l, t, at["attend"]):
                            exps(l, b, u, i, s)

            act.wait_ge(loaded[3], 16)
            iterations(act, slot)

        @block.vector
        def _(dve):
            def reduce_unit(l, b, u):
                dve.wait_ge(*s_written[l].upto(b, u))
                qt, h0, n = unit_of(l, u)
                nc.vector.tensor_reduce(neg_max[l][:, qt, h0:h0 + n],
                                        s_bank(l, u)[:, :].rearrange("p (h k) -> p h k", h=n),
                                        axis=AX.X, op=ALU.max, negate=True).then_inc(s_read[l].sem, 1)

            def split_max(l, b, g):
                src = neg_max[l][:, :, 8 * g:8 * g + 8]
                rest = max_rest[l][:, :, 8 * g:8 * g + 8]
                part = max_part[l][:, g, :, :, :]
                dve.wait_ge(*s_read[l].upto(b, (g + 1) * UNITS[l] // 2 - 1))
                nc.vector.tensor_copy(part[:, :, 0, :], src).then_inc(max_split[l].sem, 1)
                dve.wait_ge(*max_split[l].upto(b, (g, "part1")))
                nc.vector.tensor_tensor(rest, src, part[:, :, 0, :], ALU.subtract).then_inc(max_split[l].sem, 1)
                dve.wait_ge(*max_split[l].upto(b, (g, "rest")))
                nc.vector.tensor_copy(part[:, :, 1, :], rest).then_inc(max_split[l].sem, 1)
                dve.wait_ge(*max_split[l].upto(b, (g, "part2")))
                nc.vector.tensor_tensor(part[:, :, 2, :], rest, part[:, :, 1, :], ALU.subtract)\
                    .then_inc(max_split[l].sem, 1)

            def out_norm(l, b, qt):
                done = out_dve[l]
                dve.wait_ge(*out_pe[l].upto(b, f"o{qt}"))
                sums = bass.AP(OUT_BANK, DK, [[512, P], [32, PAIRS], [256 + VW, 2]])
                vals = bass.AP(OUT_BANK, 0, [[512, P], [32, PAIRS], [256 + VW, 2], [1, DK]])
                nc.vector.reciprocal(rsum[l][:, qt, :, :], sums).then_inc(done.sem, 1)
                dve.wait_ge(*done.upto(b, f"recip{qt}"))
                if qt == 0:
                    if l == CAUSAL:
                        nc.vector.tensor_scalar(rsum[l][:, 0, :, :], rsum[l][:, 0, :, :], keep_row[:, 0:1], None,
                                                ALU.mult).then_inc(done.sem, 1)
                        dve.wait_ge(*done.upto(b, "keep0"))
                r = rsum[l][:, qt, :, :].rearrange("p (a b) (e c) -> p (a b) e c", a=1, c=1)\
                    .broadcast_to([P, PAIRS, 2, DK])
                nc.vector.tensor_tensor(heads[l][:, qt, :].rearrange("p (a e d) -> p a e d", e=2, d=DK), vals, r,
                                        ALU.mult).then_inc(done.sem, 1)

            def layer_norm(part, l, b, done, psum, res, y, st, mv, cen, ln):
                if part == "add":
                    nc.vector.tensor_tensor(y[l][:].rearrange("p t d -> p (t d)"), psum[:, 0:TOKENS],
                                            res[:].rearrange("p t d -> p (t d)"), ALU.add).then_inc(done.sem, 1)
                if part == "stats":
                    dve.wait_ge(*done.upto(b, "add"))
                    nc.vector.bn_stats(st[l][:, 0, :], y[l][:, 0, :])
                    nc.vector.bn_stats(st[l][:, 1, :], y[l][:, 1, :]).then_inc(done.sem, 1)
                if part == "centre":
                    dve.wait_ge(*done.upto(b, "stats"))
                    nc.vector.memset(wait_carrier[:], 0.0)
                    nc.vector.bn_aggr(mv[l][:, 0, :], st[l][:, 0, :])
                    nc.vector.bn_aggr(mv[l][:, 1, :], st[l][:, 1, :]).then_inc(done.sem, 1)
                    dve.wait_ge(*done.upto(b, "aggr"))
                    for t in range(TILES):
                        nc.vector.scalar_tensor_tensor(out=cen[l][:, t, :], in0=y[l][:, t, :], scalar=mv[l][:, t, 0:1],
                                                       in1=row[:, LNG + ln, :], op0=ALU.subtract, op1=ALU.mult)\
                            .then_inc(done.sem, 1)

            def layer_norm_end(l, b, done, pool, rs, cen, ln, dst):
                dve.wait_ge(*pool[l].upto(b, "pow"))
                dve.wait_ge(*done.upto(b, "centre1"))
                for t in range(TILES):
                    nc.vector.scalar_tensor_tensor(out=dst[l][:, t, :], in0=cen[l][:, t, :], scalar=rs[l][:, t:t + 1],
                                                   in1=row[:, LNB + ln, :], op0=ALU.mult, op1=ALU.add)\
                        .then_inc(done.sem, 1)

            def out_ln(part, l, b):
                if part == "add":
                    dve.wait_ge(*out_pe[l].upto(b, "back"))
                    if l == CAUSAL:
                        dve.wait_ge(resid_loaded, value(b, 16, 16))
                    else:
                        dve.wait_ge(*resid_kept[l].upto(b, "copy"))
                layer_norm(part, l, b, out_dve[l], OUT_BANK, resid[l], y, stats, mean_var, centred, LN_OUT[l])

            def out_ln_end(l, b):
                if l == SELF and (isinstance(b, Batch) or b > 0):
                    dve.wait_ge(*resid_kept[CROSS].upto(b - 1, "copy"))
                layer_norm_end(l, b, out_dve[l], out_pool, rstd, centred, LN_OUT[l], x1)

            def tail_ln(part, l, b):
                if part == "add":
                    dve.wait_ge(*tail_pe[l].upto(b, "back"))
                layer_norm(part, l, b, tail_dve[l], TAIL_BANK, x1[l], z, tstats, tmean_var, tcentred, LN_TAIL[l])

            def tail_ln_end(l, b):
                if l == CROSS and (isinstance(b, Batch) or b > 0):
                    dve.wait_ge(out_stored, value(b, 16))
                if l == CAUSAL and (isinstance(b, Batch) or b > 0):
                    dve.wait_ge(*resid_kept[SELF].upto(b - 1, "copy"))
                layer_norm_end(l, b, tail_dve[l], tail_pool, trstd, tcentred, LN_TAIL[l], x2)

            def prep_v(l, b):
                if starts(b):
                    dve.wait_ge(stacks_set[l], SET)
                dve.wait_ge(*prep_pe[l].upto(b, "v"))
                nc.vector.tensor_tensor(
                    v_sb[l][:, :, 0:HEADS * VW].rearrange("p t (h w) -> p t h w", w=VW)[:, :, :, 0:DK],
                    TAIL_BANK[:, 0:TILES * D].rearrange("p (t h d) -> p t h d", t=TILES, d=DK),
                    row[:, BV + l:BV + l + 1, :].rearrange("p a (h d) -> p a h d", d=DK)
                    .broadcast_to([P, TILES, HEADS, DK]), ALU.add).then_inc(prep_dve[l].sem, 1)

            def prep_part2(l, b):
                of = prep_dve if l == SELF else prep_pool
                dve.wait_ge(*of[l].upto(b, "rest"))
                nc.vector.tensor_copy(qk_part[l][:, :, 1, :], halves(qk_rest[l])).then_inc(prep_dve[l].sem, 1)

            def prep_rest(l, b):
                dve.wait_ge(*prep_act[l].upto(b, "part1"))
                nc.vector.tensor_tensor(halves(qk_rest[l]), halves(qk[l]), qk_part[l][:, :, 0, :], ALU.subtract)\
                    .then_inc(prep_dve[l].sem, 1)

            def prep_part3(l, b):
                dve.wait_ge(*prep_dve[l].upto(b, "part2"))
                nc.vector.tensor_tensor(qk_part[l][:, :, 2, :], halves(qk_rest[l]), qk_part[l][:, :, 1, :], ALU.subtract)\
                    .then_inc(prep_dve[l].sem, 1)

            def keep_residual(l, b, src, src_done):
                if isinstance(b, Batch) or b > 0:
                    dve.wait_ge(*out_dve[l].upto(b - 1, "add"))
                dve.wait_ge(*src_done.upto(b, "norm_b"))
                nc.vector.tensor_copy(resid[l][:], src[:]).then_inc(resid_kept[l].sem, 1)

            def mask_bias(b):
                if isinstance(b, Batch) or b > 0:
                    dve.wait_ge(*s_written[SELF].upto(b - 1, UNITS[SELF] - 1))
                    dve.wait_ge(*prep_pe[SELF].upto(b - 1, "mask"))
                dve.wait_ge(sm_loaded, value(b, 16, 16))
                nc.vector.tensor_scalar(sm_q[:].rearrange("p t k -> p (t k)"),
                                        sm_int[:].rearrange("p t k -> p (t k)"), 0.0, -BIG,
                                        ALU.is_equal, ALU.mult).then_inc(mask_q.sem, 1)

            def slot(i, s):
                (l, b), (ln, bn), (lo, bo), (lt, bt) = slot_tasks(i, s)
                at = steps_of(i)
                for t in range(STEPS):
                    if t == at["keep"][SELF] and s == 0 and exists(i - 1):
                        keep_residual(SELF, i - 1, x2[CAUSAL], tail_dve[CAUSAL])
                    if t == at["keep"][CROSS] and s == 1 and exists(i - 2):
                        keep_residual(CROSS, i - 2, x1[SELF], out_dve[SELF])
                    if t == at["bias"][SELF] and s == 2 and exists(i):
                        mask_bias(i)
                    if t == at["split1"][l] and exists(b):
                        split_max(l, b, 1)
                    if t == at["split0"][ln] and exists(bn):
                        split_max(ln, bn, 0)
                    if exists(bo):
                        if t == at["o0"][lo]:
                            out_norm(lo, bo, 0)
                        if t == at["o1"][lo]:
                            out_norm(lo, bo, 1)
                        if t == at["back"][lo]:
                            out_ln("add", lo, bo)
                        if t == at["stats"][lo]:
                            out_ln("stats", lo, bo)
                        if t == at["centre"][lo]:
                            out_ln("centre", lo, bo)
                        if t == at["norm"][lo]:
                            out_ln_end(lo, bo)
                    if exists(bt) and lt in FFN:
                        if t == at["t_back"][lt]:
                            tail_ln("add", lt, bt)
                        if t == at["t_stats"][lt]:
                            tail_ln("stats", lt, bt)
                        if t == at["t_centre"][lt]:
                            tail_ln("centre", lt, bt)
                        if t == at["t_norm"][lt]:
                            tail_ln_end(lt, bt)
                    if exists(bt) and lt == CAUSAL:
                        if t == at["rest"][SELF]:
                            prep_rest(SELF, bt)
                        if t == at["part2"][SELF]:
                            prep_part2(SELF, bt)
                            prep_part3(SELF, bt)
                        if t == at["v_bias"][SELF]:
                            prep_v(SELF, bt)
                    if exists(bt) and lt == SELF:
                        if t == at["v_bias"][CROSS]:
                            prep_v(CROSS, bt)
                        if t == at["part2"][CROSS]:
                            prep_part2(CROSS, bt)
                    if s == 1 and exists(i + 1):
                        if t == at["v_bias"][CAUSAL]:
                            prep_v(CAUSAL, i + 1)
                        if t == at["part2"][CAUSAL]:
                            prep_part2(CAUSAL, i + 1)
                    if exists(bn):
                        for u in units(ln, t, at["max"]):
                            reduce_unit(ln, bn, u)

            constant_rows(nc.vector, CAUSAL)
            dve.wait_ge(loaded[4], 16)
            dve.wait_ge(*consts.upto(0, "selects"))
            iterations(dve, slot)

        @block.gpsimd
        def _(pool):
            nc.gpsimd.memset(ident_f[:], 0.0).then_inc(made, 1)
            pool.wait_ge(made, 1)
            nc.gpsimd.affine_select(out=ident_f[:], in_=ident_f[:], compare_op=ALU.not_equal, fill=1.0, base=0,
                                    pattern=[[-1, P]], channel_multiplier=1).then_inc(consts.sem, 1)
            nc.gpsimd.memset(ident_b[:], 0.0).then_inc(made, 1)
            nc.gpsimd.memset(causal_q[:], 0.0).then_inc(made, 1)
            nc.gpsimd.memset(causal_k[:], 0.0).then_inc(made, 1)
            nc.gpsimd.memset(keep_row[:], 1.0).then_inc(made, 1)
            nc.gpsimd.memset(half_neg[:], -0.5).then_inc(made, 1)
            nc.gpsimd.memset(eps[:], EPS).then_inc(made, 1)
            pool.wait_ge(made, 7)
            nc.gpsimd.affine_select(out=ident_b[:], in_=ident_b[:], compare_op=ALU.not_equal, fill=1.0, base=0,
                                    pattern=[[-1, P]], channel_multiplier=1).then_inc(made, 1)
            nc.gpsimd.affine_select(out=causal_q[:], in_=causal_q[:], compare_op=ALU.is_gt, fill=-BIG, base=0,
                                    pattern=[[-1, P]], channel_multiplier=1).then_inc(made, 1)
            nc.gpsimd.affine_select(out=causal_k[:], in_=causal_k[:], compare_op=ALU.is_gt, fill=-BIG, base=0,
                                    pattern=[[1, P]], channel_multiplier=-1).then_inc(made, 1)
            pool.wait_ge(made, 10)
            pool.wait_ge(*consts.upto(0, "ident"))
            nc.gpsimd.affine_select(out=keep_row[:], in_=keep_row[:], compare_op=ALU.is_gt, fill=0.0, base=0,
                                    pattern=[[0, 1]], channel_multiplier=1).then_inc(consts.sem, 1)

            def other_layers():
                pool.wait_ge(loaded[5], 16)
                nc.gpsimd.tensor_scalar(km_bias[:], km_int[:], 0.0, -BIG, ALU.is_equal, ALU.mult)\
                    .then_inc(consts.sem, 1)
                pool.wait_ge(*consts.upto(0, "mask"))
                constant_rows(nc.gpsimd, SELF)
                pool.wait_ge(stacks_set[SELF], SET)
                constant_rows(nc.gpsimd, CROSS)

            def rstd_of(l, b, dve, done, mv, ve, rs):
                pool.wait_ge(*dve[l].upto(b, "aggr"))
                nc.gpsimd.tensor_tensor(ve[l][:], mv[l][:, :, 1], eps[:], ALU.add).then_inc(done[l].sem, 1)
                pool.wait_ge(*done[l].upto(b, "eps"))
                nc.gpsimd.tensor_tensor(rs[l][:], ve[l][:], half_neg[:], ALU.pow).then_inc(done[l].sem, 1)

            def prep_rest(l, b):
                pool.wait_ge(*prep_act[l].upto(b, "part1"))
                nc.gpsimd.tensor_tensor(halves(qk_rest[l]), halves(qk[l]), qk_part[l][:, :, 0, :], ALU.subtract)\
                    .then_inc(prep_pool[l].sem, 1)

            def prep_part3(l, b):
                pool.wait_ge(*prep_dve[l].upto(b, "part2"))
                nc.gpsimd.tensor_tensor(qk_part[l][:, :, 2, :], halves(qk_rest[l]), qk_part[l][:, :, 1, :], ALU.subtract)\
                    .then_inc(prep_pool[l].sem, 1)

            def slot(i, s):
                (l, b), (ln, bn), (lo, bo), (lt, bt) = slot_tasks(i, s)
                if not isinstance(i, Batch) and (i, s) == (-1, 2):
                    other_layers()
                if s == 1 and exists(i + 1):
                    prep_rest(CAUSAL, i + 1)
                    prep_part3(CAUSAL, i + 1)
                if exists(bt) and lt == SELF:
                    prep_rest(CROSS, bt)
                    prep_part3(CROSS, bt)
                if exists(bt) and lt == CAUSAL:
                    rstd_of(lt, bt, tail_dve, tail_pool, tmean_var, tvar_eps, trstd)
                if exists(bo):
                    rstd_of(lo, bo, out_dve, out_pool, mean_var, var_eps, rstd)
                if exists(bt) and lt == CROSS:
                    rstd_of(lt, bt, tail_dve, tail_pool, tmean_var, tvar_eps, trstd)

            iterations(pool, slot)


def kernel(**inputs):
    import concourse.bacc as bacc
    from concourse.bass_utils import run_bass_kernel_spmd

    a = {k: np.asarray(v) for k, v in inputs.items()}
    L0, L1 = "L0_xattn_", "L1_xattn_"
    by_dim = np.arange(D).reshape(HEADS, DK).T.reshape(-1)
    w4 = [a[L0 + "Wq"][:, by_dim], a[L0 + "Wk"][:, by_dim], a[L0 + "Wv"], a[L0 + "Wo"]]
    for n in ("sa", "ca"):
        w4 += [a[f"{L1}{n}_wq"].T[:, by_dim], a[f"{L1}{n}_wk"].T[:, by_dim], a[f"{L1}{n}_wv"].T, a[f"{L1}{n}_wo"].T]
    cols = [a[L0 + "bq"][by_dim], a[L1 + "sa_bq"][by_dim], a[L1 + "ca_bq"][by_dim],
            a[L0 + "bk"][by_dim], a[L1 + "sa_bk"][by_dim], a[L1 + "ca_bk"][by_dim],
            a[L0 + "bo"], a[L1 + "sa_bo"], a[L1 + "ca_bo"], a[L0 + "b2"], a[L1 + "ffn_b2"],
            *a[L0 + "b1"].reshape(CHUNKS, P), *a[L1 + "ffn_b1"].reshape(CHUNKS, P)]
    rows = [a[L0 + "bv"], a[L1 + "sa_bv"], a[L1 + "ca_bv"],
            a[L0 + "ln1_g"], a[L0 + "ln2_g"], a[L1 + "ln1_g"], a[L1 + "ln2_g"], a[L1 + "ln3_g"],
            a[L0 + "ln1_b"], a[L0 + "ln2_b"], a[L1 + "ln1_b"], a[L1 + "ln2_b"], a[L1 + "ln3_b"]]
    arrays = {
        "x": a["x"], "ctx": a["ctx_1024"],
        "key_mask": a["mask_Bx1x1xS2_if1"].reshape(BATCHES, TOKENS),
        "self_mask": a["mask_Bx1xSxS2_if1"].reshape(BATCHES, TOKENS, TOKENS),
        "w4": np.stack(w4), "w1": np.stack([a[L0 + "W1"], a[L1 + "ffn_w1"].T]),
        "w2": np.stack([a[L0 + "W2"], a[L1 + "ffn_w2"].T]),
        "bias_col": np.stack(cols, axis=1), "bias_row": np.stack(rows),
    }
    arrays = {k: np.ascontiguousarray(v) for k, v in arrays.items()}
    nc = bacc.Bacc("TRN2", target_bir_lowering=False, num_devices=1)
    args = [nc.dram_tensor(k, v.shape, mybir.dt.from_np(v.dtype), kind="ExternalInput").ap()
            for k, v in arrays.items()]
    out = nc.dram_tensor("out", (BATCHES, TOKENS, D), f32, kind="ExternalOutput").ap()
    mask_rows = nc.dram_tensor("mask_rows", (BATCHES, TOKENS), bf16, kind="Internal").ap()
    attention_program(nc, *args, out, mask_rows)
    r = run_bass_kernel_spmd(nc, [arrays], core_ids=[0])
    return r.results[0]["out"]
```
